# Optimizing a Trainium2 kernel written in Bass

```python
import numpy as np
import jax
import jax.numpy as jnp

def _softmax(x, axis=-1):
    return jax.nn.softmax(x, axis=axis)

def _gelu(x):
    return jax.nn.gelu(x, approximate=True)

def _silu(x):
    return jax.nn.silu(x)

def _sigmoid(x):
    return jax.nn.sigmoid(x)

def _layernorm(x, axis=-1, eps=1e-05):
    m = jnp.mean(x, axis=axis, keepdims=True)
    v = jnp.var(x, axis=axis, keepdims=True)
    return (x - m) / jnp.sqrt(v + eps)

def _scatter_add(tgt, idx, src, axis=0):
    return tgt.at[idx].add(src)

def _segment_sum(src, seg, n):
    return jax.ops.segment_sum(src, seg, n)
kernel_name = 'mk_gnn_resnorm_d4_gnn_r32_234944'

def setup_inputs(seed: int=0):
    np.random.seed(seed)
    _w = jnp.asarray

    def _rec_inputs():
        import jax
        import jax.numpy as jnp
        _gk = jax.random.key(seed)
        x = -0.0002117 + 1 * jax.random.normal(jax.random.fold_in(_gk, 1), (50000, 256), jnp.float32)
        src = jax.random.randint(jax.random.fold_in(_gk, 2), (50000,), 0, 50000, jnp.int32)
        dst = jax.random.randint(jax.random.fold_in(_gk, 3), (50000,), 0, 50000, jnp.int32)
        _o = jnp.argsort(dst, stable=True)
        src = src[_o]
        dst = dst[_o]
        edge_attr_20 = jax.random.uniform(jax.random.fold_in(_gk, 12), (50000, 20), jnp.float32, 0.0, 1)
        edge_attr_3 = -1.09012e-05 + 0.99985 * jax.random.normal(jax.random.fold_in(_gk, 13), (50000, 3), jnp.float32)
        edge_attr_64 = -9.77346e-05 + 0.999888 * jax.random.normal(jax.random.fold_in(_gk, 14), (50000, 64), jnp.float32)
        edge_weight = jax.random.uniform(jax.random.fold_in(_gk, 16), (50000,), jnp.float32, 0.0, 1)
        return (x, src, dst, edge_attr_20, edge_attr_3, edge_attr_64, edge_weight)
    x, src, dst, edge_attr_20, edge_attr_3, edge_attr_64, edge_weight = _rec_inputs()

    def _L0_gnn_setup():
        import jax, jax.numpy as jnp
        import numpy as np
        N_NODES = 3125
        K_HOPS = 2
        ALPHA = 0.5

        def _gcn_norm(edge_index, edge_weight, num_nodes):
            loops = jnp.arange(num_nodes, dtype=edge_index.dtype)
            src = jnp.concatenate([edge_index[0], loops])
            dst = jnp.concatenate([edge_index[1], loops])
            w = jnp.concatenate([edge_weight, jnp.ones((num_nodes,), edge_weight.dtype)])
            deg = jax.ops.segment_sum(w, dst, num_segments=num_nodes)
            dinv = jnp.where(deg > 0, jax.lax.rsqrt(jnp.maximum(deg, 1e-12)), 0.0)
            norm = dinv[src] * w * dinv[dst]
            return (src, dst, norm)
        key = jax.random.key(seed)
        k1, k2, k3, k4, k5 = jax.random.split(key, 5)
        N, E, D_IN, D_OUT = (N_NODES, 100000, 256, 256)
        x = jax.random.normal(k1, (N, D_IN), dtype=jnp.float32)
        edge_index = jax.random.randint(k2, (2, E), 0, N, dtype=jnp.int64)
        edge_weight = jax.random.uniform(k3, (E,), dtype=jnp.float32)
        W = jax.random.normal(k4, (D_OUT, D_IN), dtype=jnp.float32) / np.sqrt(D_IN)
        b = jax.random.normal(k5, (D_OUT,), dtype=jnp.float32) * 0.01
        return {'x': x, 'edge_index': edge_index, 'edge_weight': edge_weight, 'W': W, 'b': b}
    _L0_gnn_all = _L0_gnn_setup()
    _L0_gnn_in = {k: v for k, v in _L0_gnn_all.items() if k in ('W', 'b')}
    del _L0_gnn_all

    def _L1_gnn_setup():
        import jax, jax.numpy as jnp
        import numpy as np
        N = 50000
        E = 12500
        IN = 256
        H = 8
        D = 32
        EF = 3
        key = jax.random.key(seed)
        ks = jax.random.split(key, 8)
        x = jax.random.normal(ks[0], (N, IN), dtype=jnp.float32)
        edge_index = jax.random.randint(ks[1], (2, E), 0, N, dtype=jnp.int64)
        edge_attr = jax.random.normal(ks[2], (E, EF), dtype=jnp.float32)
        W = jax.random.normal(ks[3], (H * D, IN), dtype=jnp.float32) * np.float32(np.sqrt(2.0 / (IN + H * D)))
        a_src = jax.random.normal(ks[4], (H, D), dtype=jnp.float32) * np.float32(np.sqrt(2.0 / (H + D)))
        a_dst = jax.random.normal(ks[5], (H, D), dtype=jnp.float32) * np.float32(np.sqrt(2.0 / (H + D)))
        edge_W = jax.random.normal(ks[6], (H * D, EF), dtype=jnp.float32) * np.float32(np.sqrt(2.0 / (EF + H * D)))
        edge_b = jnp.zeros((H * D,), dtype=jnp.float32)
        bias = jnp.zeros((H * D,), dtype=jnp.float32)
        return {'x': x, 'W': W, 'a_src': a_src, 'a_dst': a_dst, 'edge_W': edge_W, 'edge_b': edge_b, 'bias': bias, 'edge_attr': edge_attr, 'edge_index': edge_index}
    _L1_gnn_all = _L1_gnn_setup()
    _L1_gnn_in = {k: v for k, v in _L1_gnn_all.items() if k in ('W', 'a_src', 'a_dst', 'edge_W', 'edge_b', 'bias')}
    del _L1_gnn_all

    def _L2_gnn_setup():
        import jax, jax.numpy as jnp
        import numpy as np
        N_NODES = 50000
        N_EDGES = 25000
        IN_DIM = 256
        E_DIM = 64
        N_HEADS = 8
        OUT_DIM = 32
        NEG_SLOPE = 0.2
        key = jax.random.key(seed)
        ks = jax.random.split(key, 10)
        return {'feat': jax.random.normal(ks[0], (N_NODES, IN_DIM), dtype=jnp.float32), 'edge_attr': jax.random.normal(ks[1], (N_EDGES, E_DIM), dtype=jnp.float32), 'src': jax.random.randint(ks[2], (N_EDGES,), 0, N_NODES, dtype=jnp.int32), 'dst': jax.random.randint(ks[3], (N_EDGES,), 0, N_NODES, dtype=jnp.int32), 'W_fc': jax.random.normal(ks[4], (IN_DIM, N_HEADS * OUT_DIM), dtype=jnp.float32) * (1.0 / np.sqrt(IN_DIM)), 'W_e': jax.random.normal(ks[5], (E_DIM, N_HEADS * OUT_DIM), dtype=jnp.float32) * (1.0 / np.sqrt(E_DIM)), 'attn_h': jax.random.normal(ks[6], (N_HEADS, OUT_DIM), dtype=jnp.float32) * 0.1, 'attn_e': jax.random.normal(ks[7], (N_HEADS, OUT_DIM), dtype=jnp.float32) * 0.1, 'attn_t': jax.random.normal(ks[8], (N_HEADS, OUT_DIM), dtype=jnp.float32) * 0.1, 'bias': jnp.zeros((N_HEADS, OUT_DIM), dtype=jnp.float32)}
    _L2_gnn_all = _L2_gnn_setup()
    _L2_gnn_in = {k: v for k, v in _L2_gnn_all.items() if k in ('W_fc', 'W_e', 'attn_h', 'attn_e', 'attn_t', 'bias')}
    del _L2_gnn_all

    def _L3_gnn_setup():
        import jax, jax.numpy as jnp
        import numpy as np
        N, E, HDIM, NG = (10000, 10000, 256, 20)
        BN_EPS = 1e-05
        key = jax.random.key(seed)
        ks = jax.random.split(key, 12)
        inp = {'x': jax.random.normal(ks[0], (N, HDIM), dtype=jnp.float32), 'rbf': jax.random.uniform(ks[1], (E, NG), dtype=jnp.float32), 'ei': jax.random.randint(ks[2], (2, E), 0, N, dtype=jnp.int64), 'Wf1': jax.random.normal(ks[3], (NG, HDIM), dtype=jnp.float32) / np.sqrt(NG), 'bf1': jnp.zeros((HDIM,), dtype=jnp.float32), 'Wf2': jax.random.normal(ks[4], (HDIM, HDIM), dtype=jnp.float32) / np.sqrt(HDIM), 'bf2': jnp.zeros((HDIM,), dtype=jnp.float32), 'Wu1': jax.random.normal(ks[5], (HDIM, HDIM), dtype=jnp.float32) / np.sqrt(HDIM), 'bu1': jnp.zeros((HDIM,), dtype=jnp.float32), 'Wu2': jax.random.normal(ks[6], (HDIM, HDIM), dtype=jnp.float32) / np.sqrt(HDIM), 'bu2': jnp.zeros((HDIM,), dtype=jnp.float32), 'gamma': jnp.ones((HDIM,), dtype=jnp.float32), 'beta': jnp.zeros((HDIM,), dtype=jnp.float32)}
        return inp
    _L3_gnn_all = _L3_gnn_setup()
    _L3_gnn_in = {k: v for k, v in _L3_gnn_all.items() if k in ('Wf1', 'bf1', 'Wf2', 'bf2', 'Wu1', 'bu1', 'Wu2', 'bu2', 'gamma', 'beta')}
    del _L3_gnn_all
    return {'x': x, 'src': src, 'dst': dst, 'edge_attr_20': edge_attr_20, 'edge_attr_3': edge_attr_3, 'edge_attr_64': edge_attr_64, 'edge_weight': edge_weight, 'L0_gnn_W': _L0_gnn_in['W'], 'L0_gnn_b': _L0_gnn_in['b'], 'L1_gnn_W': _L1_gnn_in['W'], 'L1_gnn_a_src': _L1_gnn_in['a_src'], 'L1_gnn_a_dst': _L1_gnn_in['a_dst'], 'L1_gnn_edge_W': _L1_gnn_in['edge_W'], 'L1_gnn_edge_b': _L1_gnn_in['edge_b'], 'L1_gnn_bias': _L1_gnn_in['bias'], 'L2_gnn_W_fc': _L2_gnn_in['W_fc'], 'L2_gnn_W_e': _L2_gnn_in['W_e'], 'L2_gnn_attn_h': _L2_gnn_in['attn_h'], 'L2_gnn_attn_e': _L2_gnn_in['attn_e'], 'L2_gnn_attn_t': _L2_gnn_in['attn_t'], 'L2_gnn_bias': _L2_gnn_in['bias'], 'L3_gnn_Wf1': _L3_gnn_in['Wf1'], 'L3_gnn_bf1': _L3_gnn_in['bf1'], 'L3_gnn_Wf2': _L3_gnn_in['Wf2'], 'L3_gnn_bf2': _L3_gnn_in['bf2'], 'L3_gnn_Wu1': _L3_gnn_in['Wu1'], 'L3_gnn_bu1': _L3_gnn_in['bu1'], 'L3_gnn_Wu2': _L3_gnn_in['Wu2'], 'L3_gnn_bu2': _L3_gnn_in['bu2'], 'L3_gnn_gamma': _L3_gnn_in['gamma'], 'L3_gnn_beta': _L3_gnn_in['beta']}

def reference(x, src, dst, edge_attr_20, edge_attr_3, edge_attr_64, edge_weight, L0_gnn_W, L0_gnn_b, L1_gnn_W, L1_gnn_a_src, L1_gnn_a_dst, L1_gnn_edge_W, L1_gnn_edge_b, L1_gnn_bias, L2_gnn_W_fc, L2_gnn_W_e, L2_gnn_attn_h, L2_gnn_attn_e, L2_gnn_attn_t, L2_gnn_bias, L3_gnn_Wf1, L3_gnn_bf1, L3_gnn_Wf2, L3_gnn_bf2, L3_gnn_Wu1, L3_gnn_bu1, L3_gnn_Wu2, L3_gnn_bu2, L3_gnn_gamma, L3_gnn_beta):
    import jax
    import jax.numpy as jnp

    def _L0_gnn_ref(x, edge_index, edge_weight, W, b):
        import jax, jax.numpy as jnp
        import numpy as np
        N_NODES = 3125
        K_HOPS = 2
        ALPHA = 0.5

        def _gcn_norm(edge_index, edge_weight, num_nodes):
            loops = jnp.arange(num_nodes, dtype=edge_index.dtype)
            src = jnp.concatenate([edge_index[0], loops])
            dst = jnp.concatenate([edge_index[1], loops])
            w = jnp.concatenate([edge_weight, jnp.ones((num_nodes,), edge_weight.dtype)])
            deg = jax.ops.segment_sum(w, dst, num_segments=num_nodes)
            dinv = jnp.where(deg > 0, jax.lax.rsqrt(jnp.maximum(deg, 1e-12)), 0.0)
            norm = dinv[src] * w * dinv[dst]
            return (src, dst, norm)
        N = x.shape[0]
        src, dst, norm = _gcn_norm(edge_index, edge_weight, N)
        h = x
        for _ in range(K_HOPS):
            msg = jax.ops.segment_sum(norm[:, None] * h[src], dst, num_segments=N)
            h = (1.0 - ALPHA) * msg + ALPHA * x
        h = jax.nn.relu(h)
        return h @ W.T + b

    def _L1_gnn_ref(x, W, a_src, a_dst, edge_W, edge_b, bias, edge_attr, edge_index):
        import jax, jax.numpy as jnp
        import numpy as np
        N = 50000
        E = 12500
        IN = 256
        H = 8
        D = 32
        EF = 3
        n = x.shape[0]
        h = (x @ W.T).reshape(n, H, D)
        src, dst = (edge_index[0], edge_index[1])
        h_src = h[src]
        h_dst = h[dst]
        alpha = jnp.einsum('ehd,hd->eh', h_src, a_src) + jnp.einsum('ehd,hd->eh', h_dst, a_dst)
        enc = jax.nn.relu(edge_attr @ edge_W.T + edge_b).reshape(-1, H, D)
        alpha = alpha + jnp.sum(enc * h_dst, axis=-1)
        alpha = jnp.where(alpha >= 0, alpha, 0.2 * alpha)
        amax = jax.ops.segment_max(alpha, dst, num_segments=n)
        ex = jnp.exp(alpha - amax[dst])
        denom = jax.ops.segment_sum(ex, dst, num_segments=n)
        attn = ex / jnp.maximum(denom[dst], 1e-10)
        out = jax.ops.segment_sum(h_src * attn[..., None], dst, num_segments=n)
        return out.reshape(n, H * D) + bias

    def _L2_gnn_ref(feat, edge_attr, src, dst, W_fc, W_e, attn_h, attn_e, attn_t, bias):
        import jax, jax.numpy as jnp
        import numpy as np
        N_NODES = 50000
        N_EDGES = 25000
        IN_DIM = 256
        E_DIM = 64
        N_HEADS = 8
        OUT_DIM = 32
        NEG_SLOPE = 0.2
        N = feat.shape[0]
        H, D = attn_h.shape
        ft = (feat @ W_fc).reshape(N, H, D)
        eh = jnp.einsum('nhd,hd->nh', ft, attn_h)
        et = jnp.einsum('nhd,hd->nh', ft, attn_t)
        fe = (edge_attr @ W_e).reshape(-1, H, D)
        ee = jnp.einsum('ehd,hd->eh', fe, attn_e)
        e = jax.nn.leaky_relu(eh[src] + ee + et[dst], negative_slope=NEG_SLOPE)
        e_max = jax.ops.segment_max(e, dst, num_segments=N)
        e_max = jax.lax.stop_gradient(jnp.where(jnp.isfinite(e_max), e_max, 0.0))
        ex = jnp.exp(e - e_max[dst])
        denom = jax.ops.segment_sum(ex, dst, num_segments=N)
        a = ex / denom[dst]
        msg = ft[src] * a[:, :, None]
        rst = jax.ops.segment_sum(msg, dst, num_segments=N)
        rst = rst + bias[None, :, :]
        return rst.reshape(N, H * D)

    def _L3_gnn_ref(x, rbf, Wf1, bf1, Wf2, bf2, Wu1, bu1, Wu2, bu2, gamma, beta, ei):
        import jax, jax.numpy as jnp
        import numpy as np
        N, E, HDIM, NG = (10000, 10000, 256, 20)
        BN_EPS = 1e-05
        row, col = (ei[0], ei[1])
        filt = jax.nn.silu(rbf @ Wf1 + bf1) @ Wf2 + bf2
        msg = x[col] * filt
        agg = jax.ops.segment_sum(msg, row, num_segments=x.shape[0])
        h = jax.nn.silu(agg @ Wu1 + bu1) @ Wu2 + bu2
        mean = jnp.mean(h, axis=0)
        var = jnp.mean(jnp.square(h - mean), axis=0)
        bn = gamma * (h - mean) * jax.lax.rsqrt(var + BN_EPS) + beta
        return x + bn
    edge_index = jnp.stack([src, dst])
    x = _layernorm(x + _L0_gnn_ref(x, edge_index, edge_weight, L0_gnn_W, L0_gnn_b), axis=-1)
    x = _layernorm(x + _L1_gnn_ref(x, L1_gnn_W, L1_gnn_a_src, L1_gnn_a_dst, L1_gnn_edge_W, L1_gnn_edge_b, L1_gnn_bias, edge_attr_3, edge_index), axis=-1)
    x = _layernorm(x + _L2_gnn_ref(x, edge_attr_64, src, dst, L2_gnn_W_fc, L2_gnn_W_e, L2_gnn_attn_h, L2_gnn_attn_e, L2_gnn_attn_t, L2_gnn_bias), axis=-1)
    x = _layernorm(x + _L3_gnn_ref(x, edge_attr_20, L3_gnn_Wf1, L3_gnn_bf1, L3_gnn_Wf2, L3_gnn_bf2, L3_gnn_Wu1, L3_gnn_bu1, L3_gnn_Wu2, L3_gnn_bu2, L3_gnn_gamma, L3_gnn_beta, edge_index), axis=-1)
    return x

_drawn_inputs = setup_inputs


def setup_inputs(seed=0):
    import zlib

    import numpy as np

    out = dict(_drawn_inputs(seed))
    spreads = {'L1_gnn_edge_b': (0.0, 0.303),
     'L1_gnn_bias': (0.0, 0.1),
     'L2_gnn_bias': (0.0, 0.1),
     'L3_gnn_bf1': (0.0, 0.1),
     'L3_gnn_bf2': (0.0, 0.1),
     'L3_gnn_bu1': (0.0, 0.1),
     'L3_gnn_bu2': (0.0, 0.8),
     'L3_gnn_gamma': (1.0, 0.2),
     'L3_gnn_beta': (0.0, 0.1)}
    factors = {'L0_gnn_b': 6.335}
    for name, (base, spread) in spreads.items():
        noise = np.random.default_rng([zlib.crc32(name.encode()), seed]).standard_normal(out[name].shape)
        drawn = base * np.exp(spread * noise) if base else spread * noise
        out[name] = jnp.asarray(drawn.astype(out[name].dtype))
    for name, factor in factors.items():
        out[name] = (out[name] * factor).astype(out[name].dtype)
    return out
```

```python
from contextlib import ExitStack

import concourse.bass as bass
from concourse import mybir

P = 128
D = 256
H = 8
HD = D // H
HW = HD + 1
VW = H * HW
SW = VW + H
TW = SW + H
K = D // P
NONE = -1.0e30
OUT = 1.0e6
EPS = 1e-5

ALU = mybir.AluOpType
ACT = mybir.ActivationFunctionType
AX = mybir.AxisListType.X
F32 = mybir.dt.float32
I32 = mybir.dt.int32



def signal(stage, s):
    sems, _, dmas = stage
    return sems[s if dmas else 0]


def done(stage, i, s, back=0):
    sems, slots, dmas = stage
    if dmas:
        return sems[(s - back) % slots], (i + ((s - back) // slots + 1)) * (16 * dmas)
    return sems[0], i * slots + (s - back + 1)


def total(stage, rounds):
    sems, slots, dmas = stage
    return [(sem, rounds * (16 * dmas if dmas else slots)) for sem in sems]


def pipelined(e, rounds, slots, stages, cut=0):
    most = max(lag for _, lag in stages)

    def step(i, s, which):
        for stage, lag in stages:
            if which(lag):
                stage(i - (1 if s < lag else 0), (s - lag) % slots)

    for s in range(slots):
        step(0, s, lambda lag: s >= lag)
    for s in range(slots):
        step(1, s, lambda lag: True)
    first = 2
    if cut > 1:
        if cut > first:
            with e.Fori(first, cut) as i:
                for s in range(slots):
                    step(i, s, lambda lag: True)
        for s in range(slots):
            step(cut, s, lambda lag: True)
        first = cut + 1
    with e.Fori(first, rounds) as i:
        for s in range(slots):
            step(i, s, lambda lag: True)
    for s in range(most):
        step(rounds, s, lambda lag: lag > s)


def build(nc, N, x, src, dst, dst_next, ew, rbfT, attr3T, attr64T, w0T, b0, w1aug, w1, a1, encW, bias1,
          wfc, wfcT, ah, ae, weT, bias2, wf1, bf1, wf2, bf2, wu1, bu1, wu2, bu2, gamma, beta, out):
    C = x.shape[1]
    NP = P * C
    VC = N - (P - 1) * C
    assert C % 8 == 0 and VC % 8 == 0 and 0 < VC < C

    alone = (nc.sync.engine, nc.gpsimd.engine, nc.scalar.engine)
    used = {}

    def fresh(name):
        used[name] = used.get(name, 0) + 1
        return f"{name}_{used[name]}"

    def semaphore(name):
        return nc.alloc_semaphore(fresh(name))

    def stage_of(name, slots, dmas=0):
        return [semaphore(f"{name}{s}") for s in range(slots if dmas else 1)], slots, dmas

    def sbuf(name, shape, dt):
        return nc.sbuf_tensor(fresh(name), shape, dt)

    def psum(name, shape, dt):
        return nc.psum_tensor(fresh(name), shape, dt)

    marks = nc.alloc_semaphore("marks")

    def hold(e, sem, value):
        if isinstance(value, int) and value <= 0:
            return
        e.wait_ge(sem, value)
        if e.engine in alone:
            e.sem_inc(marks, 1)

    def dram(name, rows, width):
        return nc.dram_tensor(name, (rows, width), F32).ap()

    def nodes(t):
        return t[0:NP, :].rearrange("(p c) d -> p c d", p=P)

    Y, S = dram("Y", NP, D), dram("S", NP, SW)
    X1, X2, X3 = dram("X1", NP, D), dram("X2", NP, D), dram("X3", NP, D)
    T1, T2, ET = dram("T1", NP, TW), dram("T2", NP, SW), dram("ET", NP, H)
    A = [dram("A0", NP + P, D), dram("A1", NP + P, D)]
    HT = nc.dram_tensor("HT", (P, C // 4, K, 4 * P), F32).ap()

    with ExitStack() as keep:
        def sb(name, shape, dt=F32):
            return keep.enter_context(sbuf(name, shape, dt))

        src_i, dst_i, scat_i = sb("src_i", [P, C], I32), sb("dst_i", [P, C], I32), sb("scat_i", [P, C], I32)
        src_f, same, pen, w_sb = sb("src_f", [P, C]), sb("same", [P, C]), sb("pen", [P, C]), sb("w_sb", [P, C])
        dinv, ca, cb, srcmt = sb("dinv", [P, C]), sb("ca", [P, C]), sb("cb", [P, C]), sb("srcmt", [P, C])
        first_i = sb("first_i", [P, 1], I32)
        trash = sb("trash", [P, 1])
        ident, before, earlier, chain, chainT, penT = [sb(n, [P, P]) for n in ("ident", "before", "earlier", "chain", "chainT", "penT")]
        epsc = sb("epsc", [P, 1])
        mask = sb("mask", [P, TW])
        w0s, wf2s, wu1s, wu2s = [sb(n, [P, K, D]) for n in ("w0s", "wf2s", "wu1s", "wu2s")]
        w1s, w2s = sb("w1s", [P, K, TW]), sb("w2s", [P, K, TW])
        encs, wf1s, fes = sb("encs", [4, D]), sb("wf1s", [wf1.shape[0], D]), sb("fes", [attr64T.shape[0], H])
        b0s, b1s, b2s, bf2s = [sb(n, [P, D]) for n in ("b0s", "b1s", "b2s", "bf2s")]
        bf1s, bu1s, bu2s, gms, bts = [sb(n, [P, K]) for n in ("bf1s", "bu1s", "bu2s", "gms", "bts")]
        tail = sb("tail", [P, SW])
        stats = sb("stats", [P, K, C // 4, 6])

        def setup():
            with ExitStack() as ctx:
                def tmp(name, shape, dt=F32):
                    return ctx.enter_context(sbuf(name, shape, dt))

                def sem(name):
                    return semaphore(name)

                zero = tmp("zero", [P, SW])
                dst_f, next_i, islast, notl = tmp("dst_f", [P, C]), tmp("next_i", [P, C], I32), tmp("islast", [P, C]), tmp("notl", [P, C])
                any_last, firstf, lastf = tmp("any_last", [P, 1]), tmp("firstf", [P, 1]), tmp("lastf", [P, 1])
                cols, rows0 = tmp("cols", [P, C]), tmp("rows0", [P, P])
                pcol, w1n, a1s, wfT, ahs, aes, weTs = (tmp("pcol", [P, 1]), tmp("w1n", [P, K, D]), tmp("a1s", [P, K, 2 * H]),
                                                  tmp("wfT", [P, K, D]), tmp("ahs", [P, K, 2 * H]), tmp("aes", [P, K, H]),
                                                  tmp("weTs", [P, K, attr64T.shape[0]]))
                dst_c, lo_f = tmp("dst_c", [P, C]), tmp("lo_f", [P, C])
                ge, hot, hotc = tmp("ge", [P, 2, P + 1]), tmp("hot", [P, 2, P]), tmp("hotc", [P, 2, C])
                lows = tmp("lows", [P, P + 1])
                psT = ctx.enter_context(psum("psT", [P, P], F32))
                psDeg = ctx.enter_context(psum("psDeg", [P, 512], F32))
                psF = ctx.enter_context(psum("psF", [P, K, 16], F32))
                psG = ctx.enter_context(psum("psG", [P, K, 16], F32))
                psE = ctx.enter_context(psum("psE", [P, 16], F32))
                loaded, zeroed, iotas, prep, tr, folds, onehot, summed, filled, rooted = [sem(n) for n in (
                    "loaded", "zeroed", "iotas", "prep", "tr", "folds", "onehot", "summed", "filled", "rooted")]
                loads = [(src_i[:], src), (dst_i[:], dst), (next_i[:], dst_next), (w_sb[:], ew),
                         (encs[:], encW), (wf1s[:], wf1)]
                loads += [(t[:], w.rearrange("(k p) d -> p k d", p=P)) for t, w in (
                    (w0s, w0T), (w1s, w1aug), (w2s, wfc), (wf2s, wf2), (wu1s, wu1), (wu2s, wu2), (w1n, w1), (a1s, a1),
                    (wfT, wfcT), (ahs, ah), (aes, ae), (weTs, weT))]
                loads += [(t[:], b.to_broadcast([P, D])) for t, b in ((b0s, b0), (b1s, bias1), (b2s, bias2), (bf2s, bf2))]
                loads += [(t[:], b) for t, b in ((bf1s, bf1), (bu1s, bu1), (bu2s, bu2), (gms, gamma), (bts, beta))]
                NL = 16 * len(loads)
                fills = []
                for t, rows, width in ((S, NP, SW), (A[0], NP, D), (A[1], NP, D)):
                    for c0 in range(0, C, 56):
                        n = min(56, C - c0)
                        fills.append((nodes(t)[:, c0:c0 + n, :], zero[:, 0:width].rearrange("p (c d) -> p c d", c=1).to_broadcast([P, n, width])))
                for t in A:
                    fills.append((t[NP:NP + P, :], zero[:, 0:D]))

                with nc.Block() as block:
                    @block.sync
                    def _(e):
                        for to, frm in loads:
                            e.dma_start(to, frm).then_inc(loaded, 16)
                        e.wait_ge(zeroed, 1)
                        for to, frm in fills:
                            e.dma_start(to, frm).then_inc(filled, 16)
                        e.wait_ge(filled, 16 * len(fills))

                    @block.gpsimd
                    def _(e):
                        e.memset(zero[:], 0.0).then_inc(zeroed, 1)
                        e.memset(ident[:], 0.0).then_inc(iotas, 1)
                        e.memset(before[:], 1.0).then_inc(iotas, 1)
                        e.memset(epsc[:], EPS).then_inc(iotas, 1)
                        e.memset(mask[:], 0.0).then_inc(iotas, 1)
                        e.iota(cols[:], pattern=[[1, C]], base=0, channel_multiplier=0, allow_small_or_imprecise_dtypes=True).then_inc(iotas, 1)
                        e.iota(lows[:], pattern=[[C, P + 1]], base=0, channel_multiplier=0, allow_small_or_imprecise_dtypes=True).then_inc(iotas, 1)
                        e.iota(pcol[:], pattern=[[0, 1]], base=0, channel_multiplier=1, allow_small_or_imprecise_dtypes=True).then_inc(iotas, 1)
                        e.iota(trash[:], pattern=[[0, 1]], base=NP, channel_multiplier=1, allow_small_or_imprecise_dtypes=True).then_inc(iotas, 1)
                        e.memset(earlier[:], 1.0).then_inc(iotas, 1)
                        e.wait_ge(iotas, 9)
                        e.affine_select(out=ident[:], in_=ident[:], compare_op=ALU.not_equal, fill=1.0, base=0,
                                        pattern=[[-1, P]], channel_multiplier=1).then_inc(iotas, 1)
                        e.affine_select(out=before[:], in_=before[:], compare_op=ALU.is_gt, fill=0.0, base=0,
                                        pattern=[[1, P]], channel_multiplier=-1).then_inc(iotas, 1)
                        e.affine_select(out=earlier[:], in_=earlier[:], compare_op=ALU.is_gt, fill=0.0, base=0,
                                        pattern=[[-1, P]], channel_multiplier=1).then_inc(iotas, 1)
                        e.memset(mask[:, 0:VW].rearrange("p (h w) -> p h w", h=H)[:, :, HD:HW], 1.0).then_inc(iotas, 1)

                    @block.vector
                    def _(e):
                        n = [0]

                        def link(ins):
                            n[0] += 1
                            ins.then_inc(prep, 1)
                            e.wait_ge(prep, n[0])

                        e.wait_ge(loaded, NL)
                        e.wait_ge(iotas, 13)
                        link(e.tensor_copy(src_f[:], src_i[:]))
                        link(e.tensor_copy(dst_f[:], dst_i[:]))
                        link(e.tensor_copy(notl[:], next_i[:]))
                        link(e.memset(same[:, 0:1], 0.0))
                        link(e.tensor_tensor(same[:, 1:C], dst_f[:, 1:C], dst_f[:, 0:C - 1], ALU.is_equal))
                        link(e.tensor_tensor(islast[:], dst_f[:], notl[:], ALU.is_lt))
                        link(e.tensor_scalar(pen[:], same[:], -1.0, -NONE, ALU.add, ALU.mult))
                        link(e.tensor_scalar(notl[:], dst_f[:], -OUT, None, ALU.add))
                        link(e.tensor_tensor(notl[:], notl[:], islast[:], ALU.mult))
                        link(e.tensor_scalar(scat_i[:], notl[:], OUT, None, ALU.add))
                        link(e.tensor_reduce(any_last[:], islast[:], AX, ALU.max))
                        link(e.tensor_copy(firstf[:], dst_f[:, 0:1]))
                        link(e.tensor_copy(lastf[:], dst_f[:, C - 1:C]))
                        link(e.tensor_scalar(pcol[:], firstf[:], -OUT, any_last[:], ALU.add, ALU.mult))
                        link(e.tensor_scalar(first_i[:], pcol[:], OUT, None, ALU.add))
                        link(e.tensor_scalar(srcmt[:], src_f[:], trash[:], None, ALU.subtract))
                        e.wait_ge(tr, 1)
                        link(e.tensor_scalar(chain[:], psT[:], lastf[:], None, ALU.is_equal))
                        link(e.tensor_tensor(chain[:], chain[:], before[:], ALU.mult))
                        e.wait_ge(tr, 2)
                        link(e.tensor_copy(chainT[:], psT[:]))
                        link(e.tensor_scalar(penT[:], chainT[:], -1.0, -NONE, ALU.add, ALU.mult))
                        e.wait_ge(folds, 1)
                        link(e.tensor_copy(w1s[:, :, VW:TW], psF[:]))
                        link(e.tensor_copy(w2s[:, :, VW:TW], psG[:]))
                        link(e.tensor_copy(fes[:], psE[0:fes.shape[0], 0:H]))
                        assert n[0] == 23

                    @block.tensor
                    def _(e):
                        e.wait_ge(prep, 13)
                        e.wait_ge(iotas, 13)
                        e.transpose(psT[:], firstf[:].to_broadcast([P, P]), ident[:]).then_inc(tr, 1)
                        e.wait_ge(prep, 18)
                        e.transpose(psT[:], chain[:], ident[:]).then_inc(tr, 1)
                        for m in range(K):
                            for k in range(K):
                                e.matmul(psF[:, m, :], w1n[:, k, m * P:(m + 1) * P], a1s[:, k, :], start=k == 0, stop=k == K - 1)
                            for k in range(K):
                                e.matmul(psG[:, m, :], wfT[:, k, m * P:(m + 1) * P], ahs[:, k, :], start=k == 0, stop=k == K - 1)
                        for k in range(K):
                            mm = e.matmul(psE[0:weTs.shape[2], 0:H], weTs[:, k, :], aes[:, k, :], start=k == 0, stop=k == K - 1)
                        mm.then_inc(folds, 1)

                with nc.Block() as block:
                    onehot2 = stage_of("hots", 2)
                    taken = stage_of("taken", 2)
                    steps = sem("dsteps")

                    @block.vector
                    def _(e):
                        def one_hot(i, s):
                            c = i * 2 + s
                            d1 = dst_f[:, bass.ds(c, 1)]
                            hold(e, *done(taken, i, s, 2))
                            e.tensor_scalar(ge[:, s, :], lows[:], d1, None, ALU.is_le).then_inc(steps, 1)
                            e.wait_ge(steps, i * 4 + (2 * s + 1))
                            e.tensor_tensor(hot[:, s, :], ge[:, s, 0:P], ge[:, s, 1:P + 1], ALU.subtract)
                            e.tensor_reduce(lo_f[:, bass.ds(c, 1)], ge[:, s, :], AX, ALU.add).then_inc(steps, 1)
                            e.wait_ge(steps, i * 4 + (2 * s + 2))
                            e.scalar_tensor_tensor(dst_c[:, bass.ds(c, 1)], lo_f[:, bass.ds(c, 1)], -float(C), d1, ALU.mult, ALU.add).then_inc(rooted, 1)
                            e.wait_ge(rooted, i * 2 + (s + 1))
                            e.tensor_scalar(hotc[:, s, :], cols[:], dst_c[:, bass.ds(c, 1)], float(C), ALU.subtract, ALU.is_equal)\
                                .then_inc(signal(onehot2, s), 1)

                        pipelined(e, C // 2, 2, [(one_hot, 0)])


                    @block.scalar
                    def _(e):
                        def weigh(i, s):
                            hold(e, *done(onehot2, i, s))
                            e.activation(hot[:, s, :], hot[:, s, :], ACT.Copy, scale=w_sb[:, bass.ds(i * 2 + s, 1)]).then_inc(onehot, 1)

                        pipelined(e, C // 2, 2, [(weigh, 0)])

                    @block.tensor
                    def _(e):
                        def both(i, first, last):
                            for s in range(2):
                                e.wait_ge(onehot, i * 2 + (s + 1))
                                e.matmul(psDeg[:, 0:C], hot[:, s, :], hotc[:, s, :], start=first and s == 0, stop=last and s == 1)\
                                    .then_inc(signal(taken, s), 1)

                        both(0, True, False)
                        with e.Fori(1, C // 2 - 1) as i:
                            both(i, False, False)
                        both(C // 2 - 1, False, True)

                with nc.Block() as block:
                    deg, ok, dsq = tmp("deg", [P, C]), tmp("ok", [P, C]), tmp("dsq", [P, C])
                    clamped, sq = sem("clamped"), sem("sq")

                    @block.vector
                    def _(e):
                        n = [0]

                        def link(ins):
                            n[0] += 1
                            ins.then_inc(clamped, 1)
                            e.wait_ge(clamped, n[0])

                        link(e.tensor_scalar(deg[:], psDeg[:, 0:C], 1.0, None, ALU.add))
                        link(e.tensor_scalar(ok[:], deg[:], 0.0, None, ALU.is_gt))
                        link(e.tensor_scalar(deg[:], deg[:], 1e-12, None, ALU.max))
                        e.wait_ge(sq, 1)
                        link(e.reciprocal(dsq[:], dsq[:]))
                        link(e.tensor_tensor(dinv[:], dsq[:], ok[:], ALU.mult))
                        link(e.scalar_tensor_tensor(ca[:], dinv[:], 0.5, dinv[:], ALU.mult, ALU.mult))
                        link(e.scalar_tensor_tensor(cb[:], ca[:], 0.5, dinv[:], ALU.add, ALU.mult))

                    @block.scalar
                    def _(e):
                        e.wait_ge(clamped, 3)
                        e.activation(dsq[:], deg[:], ACT.Sqrt).then_inc(sq, 1)

        def hop_table(first):
            with ExitStack() as ctx:
                G, NS = 4, 2
                R = C // (G * NS)
                tiles = lambda n, w: [ctx.enter_context(sbuf(f"{n}{s}", [P, G, w], F32)) for s in range(NS)]
                xt, st = tiles("xt", D), tiles("st", SW)
                loaded = stage_of("loaded", NS, 1 if first else 2)
                stored = stage_of("stored", NS, 1)
                scaled, ready = stage_of("scaled", NS), stage_of("ready", NS)
                
                with nc.Block() as block:
                    @block.sync
                    def _(e):

                        def load(i, s):
                            c = bass.ds(i * (G * NS) + s * G, G)
                            hold(e, *done(stored, i, s, NS))
                            e.dma_start(xt[s][:], x[:, c, :]).then_inc(signal(loaded, s), 16)
                            if not first:
                                e.dma_start(st[s][:], nodes(S)[:, c, :]).then_inc(signal(loaded, s), 16)

                        def store(i, s):
                            hold(e, *done(ready, i, s))
                            e.dma_start(nodes(Y)[:, bass.ds(i * (G * NS) + s * G, G), :], xt[s][:]).then_inc(signal(stored, s), 16)

                        pipelined(e, R, NS, [(load, 0), (store, 1)])
                        for sem, value in total(stored, R):
                            e.wait_ge(sem, value)

                    @block.scalar
                    def _(e):
                        def scale(i, s):
                            hold(e, *done(loaded, i, s))
                            for k in range(G):
                                c = bass.ds(i * (G * NS) + (s * G + k), 1)
                                if first and k % 2 == 0:
                                    ins = e.activation(xt[s][:, k, :], xt[s][:, k, :], ACT.Copy, scale=dinv[:, c])
                                elif not first:
                                    ins = e.activation(st[s][:, k, 0:D], st[s][:, k, 0:D], ACT.Copy, scale=ca[:, c])
                            ins.then_inc(signal(scaled, s), 1)

                        pipelined(e, R, NS, [(scale, 0)])

                    @block.vector
                    def _(e):
                        def add(i, s):
                            hold(e, *done(loaded, i, s))
                            hold(e, *done(scaled, i, s))
                            for k in range(G):
                                c = bass.ds(i * (G * NS) + (s * G + k), 1)
                                if first and k % 2 == 1:
                                    ins = e.tensor_scalar(xt[s][:, k, :], xt[s][:, k, :], dinv[:, c], None, ALU.mult)
                                elif not first:
                                    ins = e.scalar_tensor_tensor(xt[s][:, k, :], xt[s][:, k, :], cb[:, c], st[s][:, k, 0:D], ALU.mult, ALU.add)
                            ins.then_inc(signal(ready, s), 1)

                        pipelined(e, R, NS, [(add, 0)])

        def hop_edges():
            with ExitStack() as ctx:
                G, NS, LAG = 2, 4, 2
                R = C // (G * NS)
                tiles = lambda n, w, dt=F32: [ctx.enter_context(sbuf(f"{n}{s}", [P, G, w], dt)) for s in range(NS)]
                rows, sums = tiles("rows", D), tiles("sums", SW)
                gi, si = tiles("gi", 1, I32), tiles("si", 1, I32)
                indexed, gathered, scattered = (stage_of("indexed", NS, 2), stage_of("gathered", NS, G),
                                                stage_of("scattered", NS, G))
                weighted, summed = stage_of("weighted", NS), stage_of("summed", NS)
                steps = semaphore("steps")
                started = semaphore("started")
                with nc.Block() as block:
                    @block.sync
                    def _(e):

                        def stage(i, s):
                            c = bass.ds(i * (G * NS) + s * G, G)
                            hold(e, *done(gathered, i, s, NS))
                            hold(e, *done(scattered, i, s, NS))
                            e.dma_start(gi[s][:, :, 0], src_i[:, c]).then_inc(signal(indexed, s), 16)
                            e.dma_start(si[s][:, :, 0], scat_i[:, c]).then_inc(signal(indexed, s), 16)

                        pipelined(e, R, NS, [(stage, 0)])

                    @block.gpsimd
                    def _(e):
                        def gather(i, s):
                            hold(e, *done(indexed, i, s))
                            hold(e, *done(summed, i, s, NS))
                            for k in range(G):
                                e.indirect_dma_start(rows[s][:, k, :], None, Y, bass.IndirectOffsetOnAxis(ap=gi[s][:, k, :], axis=0))\
                                    .then_inc(signal(gathered, s), 16)

                        def scatter(i, s):
                            hold(e, *done(summed, i, s))
                            for k in range(G):
                                e.indirect_dma_start(S, bass.IndirectOffsetOnAxis(ap=si[s][:, k, :], axis=0), sums[s][:, k, :], None,
                                                     bounds_check=NP - 1, oob_is_err=False).then_inc(signal(scattered, s), 16)

                        pipelined(e, R, NS, [(gather, 0), (scatter, LAG)])
                        for sem, value in total(scattered, R):
                            e.wait_ge(sem, value)

                    @block.scalar
                    def _(e):
                        def weigh(i, s):
                            hold(e, *done(gathered, i, s))
                            for k in range(G):
                                ins = e.activation(rows[s][:, k, :], rows[s][:, k, :], ACT.Copy, scale=w_sb[:, bass.ds(i * (G * NS) + (s * G + k), 1)])
                            ins.then_inc(signal(weighted, s), 1)

                        pipelined(e, R, NS, [(weigh, 0)])

                    @block.vector
                    def _(e):
                        for s in range(NS):
                            ins = e.memset(sums[s][:], 0.0)
                        ins.then_inc(started, 1)
                        e.wait_ge(started, 1)

                        def add(i, s):
                            hold(e, *done(weighted, i, s))
                            hold(e, *done(scattered, i, s, NS))
                            for k in range(G):
                                last = sums[s][:, k - 1, 0:D] if k else sums[(s - 1) % NS][:, G - 1, 0:D]
                                ins = e.scalar_tensor_tensor(sums[s][:, k, 0:D], last, same[:, bass.ds(i * (G * NS) + (s * G + k), 1)],
                                                             rows[s][:, k, :], ALU.mult, ALU.add)
                                if k < G - 1:
                                    ins.then_inc(steps, 1)
                                    e.wait_ge(steps, i * NS * (G - 1) + (s * (G - 1) + k + 1))
                            ins.then_inc(signal(summed, s), 1)
                            hold(e, *done(summed, i, s))

                        pipelined(e, R, NS, [(add, 0)])
                with nc.Block() as block:
                    own, ps = ctx.enter_context(sbuf("own", [P, SW], F32)), ctx.enter_context(psum("psC", [P, D], F32))
                    fetched, cleared, carried, fixed, put = [semaphore(n) for n in (
                        "fetched", "cleared", "carried", "fixed", "put")]

                    @block.vector
                    def _(e):
                        e.memset(own[:], 0.0).then_inc(cleared, 1)
                        e.wait_ge(carried, 1)
                        e.wait_ge(fetched, 16)
                        e.tensor_tensor(own[:, 0:D], own[:, 0:D], ps[:], ALU.add).then_inc(fixed, 1)

                    @block.tensor
                    def _(e):
                        e.matmul(ps[:], chain[:], sums[NS - 1][:, G - 1, 0:D], start=True, stop=True).then_inc(carried, 1)

                    @block.gpsimd
                    def _(e):
                        at = bass.IndirectOffsetOnAxis(ap=first_i[:], axis=0)
                        e.wait_ge(cleared, 1)
                        e.indirect_dma_start(own[:], None, S, at, bounds_check=NP - 1, oob_is_err=False).then_inc(fetched, 16)
                        e.wait_ge(fixed, 1)
                        e.indirect_dma_start(S, at, own[:], None, bounds_check=NP - 1, oob_is_err=False).then_inc(put, 16)
                        e.wait_ge(put, 16)

        def norm_of(ctx, NS, G, z, y):
            t = lambda n, w: [ctx.enter_context(sbuf(f"{n}{s}", [P, G, w], F32)) for s in range(NS)]
            row_stats, mean_var, sd, rsd, shift = t("row_stats", 6), t("mean_var", 2), t("sd", 1), t("rsd", 1), t("shift", 1)
            measured, rooted, inverted, folded, recip = (
                stage_of(n, NS) for n in ("measured", "rooted", "inverted", "folded", "recip"))

            def ln_measure(e, i, s):
                for k in range(G):
                    ins = e.bn_stats(row_stats[s][:, k, :], z[s][:, k, :])
                ins.then_inc(signal(folded, s), 1)
                hold(e, *done(folded, i, s))
                e.sem_inc(marks, 1)
                for k in range(G):
                    ins = e.bn_aggr(mean_var[s][:, k, :], row_stats[s][:, k, :])
                ins.then_inc(signal(measured, s), 1)

            def ln_root(e, i, s):
                hold(e, *done(measured, i, s))
                e.activation(sd[s][:, :, 0], mean_var[s][:, :, 1], ACT.Sqrt, bias=epsc[:]).then_inc(signal(rooted, s), 1)

            def ln_invert(e, i, s):
                hold(e, *done(rooted, i, s))
                e.reciprocal(rsd[s][:, :, 0], sd[s][:, :, 0]).then_inc(signal(recip, s), 1)
                hold(e, *done(recip, i, s))
                e.scalar_tensor_tensor(shift[s][:, :, 0], mean_var[s][:, :, 0], -1.0, rsd[s][:, :, 0], ALU.mult, ALU.mult)\
                    .then_inc(signal(inverted, s), 1)

            def ln_apply(e, i, s, finished):
                hold(e, *done(inverted, i, s))
                for k in range(G):
                    ins = e.activation(y[s][:, k, :], z[s][:, k, :], ACT.Identity, bias=shift[s][:, k, :], scale=rsd[s][:, k, :])
                ins.then_inc(signal(finished, s), 1)

            return ln_measure, ln_root, ln_invert, ln_apply

        def layer_nodes(layer):
            xin = x if layer == 0 else nodes((X1, X2)[layer - 1])
            xout = nodes((X1, X2, X3)[layer])
            table = layer < 2
            with ExitStack() as ctx:
                G, NS = 2, 4
                R = C // (G * NS)
                tiles = lambda n, w: [ctx.enter_context(sbuf(f"{n}{s}", [P, G, w], F32)) for s in range(NS)]
                xt, st, xb, z, xo = tiles("xt", D), tiles("st", SW), tiles("xb", D), tiles("z", D), tiles("xo", D)
                yt, rT = (tiles("yt", D), tiles("rT", D)) if layer == 0 else (None, None)
                den = tiles("den", H) if layer else None
                xT, tt = (tiles("xT", D), tiles("tt", TW)) if table else (None, None)
                bank = lambda n, w: ctx.enter_context(psum(n, [P, w], F32))
                psR = [bank(f"psR{j}", G * D) for j in range(2)] if layer == 0 else None
                psZ = [bank(f"psZ{j}", G * D) for j in range(2)] if layer == 0 else None
                psX = [bank(f"psX{j}", G * D) for j in range(2)] if table else None
                psV = [bank(f"psV{j}", 512) for j in range(2)] if table else None
                weights = (w1s, w2s, None)[layer]
                NL = 3 if layer == 0 else 2
                NO = (2, 3, 1)[layer]
                names = "biased mixed rectified turned copied product summed normed turnedx copiedx tabled evened".split()
                st_ = {n: stage_of(n, NS) for n in names}
                loaded, stored = stage_of("loaded", NS, NL), stage_of("stored", NS, NO)
                steps = semaphore("steps")
                ln_measure, ln_root, ln_invert, ln_apply = norm_of(ctx, NS, G, z, xo)
                with nc.Block() as block:
                    @block.sync
                    def _(e):

                        def load(i, s):
                            c = bass.ds(i * (G * NS) + s * G, G)
                            hold(e, *done(stored, i, s, NS))
                            e.dma_start(xt[s][:], xin[:, c, :]).then_inc(signal(loaded, s), 16)
                            e.dma_start(st[s][:], nodes(S)[:, c, :]).then_inc(signal(loaded, s), 16)
                            if layer == 0:
                                e.dma_start(yt[s][:], nodes(Y)[:, c, :]).then_inc(signal(loaded, s), 16)

                        def store(i, s):
                            c = bass.ds(i * (G * NS) + s * G, G)
                            hold(e, *done(st_["normed"], i, s))
                            e.dma_start(xout[:, c, :], xo[s][:]).then_inc(signal(stored, s), 16)
                            if table:
                                hold(e, *done(st_["evened"], i, s))
                            if layer == 0:
                                e.dma_start(nodes(T1)[:, c, :], tt[s][:]).then_inc(signal(stored, s), 16)
                            if layer == 1:
                                e.dma_start(nodes(T2)[:, c, :], tt[s][:, :, 0:SW]).then_inc(signal(stored, s), 16)
                                e.dma_start(nodes(ET)[:, c, :], tt[s][:, :, SW:TW]).then_inc(signal(stored, s), 16)

                        pipelined(e, R, NS, [(load, 0), (store, 3)])
                        for sem, value in total(stored, R):
                            e.wait_ge(sem, value)

                    @block.gpsimd
                    def _(e):
                        bias = (b0s, b1s, b2s)[layer]

                        def add_bias(i, s):
                            hold(e, *done(loaded, i, s))
                            e.tensor_tensor(xb[s][:], xt[s][:], bias[:].rearrange("p (g d) -> p g d", g=1).to_broadcast([P, G, D]), ALU.add)\
                                .then_inc(signal(st_["biased"], s), 1)

                        pipelined(e, R, NS, [(add_bias, 0)])

                    @block.vector
                    def _(e):
                        def mix(i, s):
                            hold(e, *done(loaded, i, s))
                            if layer == 0:
                                e.tensor_tensor(yt[s][:], yt[s][:], st[s][:, :, 0:D], ALU.add).then_inc(steps, 1)
                                e.wait_ge(steps, i * NS + (s + 1))
                                for k in range(G):
                                    ins = e.scalar_tensor_tensor(yt[s][:, k, :], yt[s][:, k, :], dinv[:, bass.ds(i * (G * NS) + (s * G + k), 1)],
                                                                 xt[s][:, k, :], ALU.mult, ALU.add)
                                ins.then_inc(signal(st_["mixed"], s), 1)
                                return
                            v = st[s][:, :, 0:VW].rearrange("p g (h w) -> p g h w", h=H)
                            e.tensor_scalar(den[s][:], v[:, :, :, HD], 1e-10, None, ALU.max).then_inc(steps, 1)
                            e.wait_ge(steps, i * (2 * NS) + (2 * s + 1))
                            e.reciprocal(den[s][:], den[s][:]).then_inc(steps, 1)
                            e.wait_ge(steps, i * (2 * NS) + (2 * s + 2))
                            e.tensor_tensor(z[s][:].rearrange("p g (h d) -> p g h d", h=H), v[:, :, :, 0:HD],
                                            den[s][:].rearrange("p g (h w) -> p g h w", w=1).to_broadcast([P, G, H, HD]), ALU.mult)\
                                .then_inc(signal(st_["mixed"], s), 1)

                        def add(i, s):
                            if layer == 0:
                                hold(e, *done(st_["product"], i, s))
                                more = psZ[s % 2][:].rearrange("p (g d) -> p g d", g=G)
                            else:
                                hold(e, *done(st_["mixed"], i, s))
                                more = z[s][:]
                            hold(e, *done(st_["biased"], i, s))
                            e.tensor_tensor(z[s][:], more, xb[s][:], ALU.add).then_inc(signal(st_["summed"], s), 1)
                            hold(e, *done(st_["summed"], i, s))
                            ln_measure(e, i, s)

                        def even(i, s):
                            for k in range(G):
                                e.wait_ge(signal(st_["tabled"], s), i * (NS * G) + (s * G + k + 1))
                                ins = e.tensor_tensor(tt[s][:, k, :], psV[k][:, 0:TW], mask[:], ALU.add)
                            ins.then_inc(signal(st_["evened"], s), 1)

                        stages = [(mix, 0), (add, 1 if layer == 0 else 0), (lambda i, s: ln_invert(e, i, s), 1 if layer else 2)]
                        if table:
                            stages.append((even, 3))
                        pipelined(e, R, NS, stages)

                    @block.scalar
                    def _(e):
                        def rectify(i, s):
                            hold(e, *done(st_["mixed"], i, s))
                            e.activation(yt[s][:], yt[s][:], ACT.Relu, scale=0.5).then_inc(signal(st_["rectified"], s), 1)

                        def copy_turned(i, s):
                            hold(e, *done(st_["turned"], i, s))
                            e.copy(rT[s][:].rearrange("p g d -> p (g d)"), psR[s % 2][:]).then_inc(signal(st_["copied"], s), 1)

                        def copy_turned_x(i, s):
                            hold(e, *done(st_["turnedx"], i, s))
                            e.copy(xT[s][:].rearrange("p g d -> p (g d)"), psX[s % 2][:]).then_inc(signal(st_["copiedx"], s), 1)

                        stages = [(rectify, 0), (copy_turned, 0)] if layer == 0 else []
                        stages.append((lambda i, s: ln_root(e, i, s), 0 if layer else 1))
                        stages.append((lambda i, s: ln_apply(e, i, s, st_["normed"]), 1 if layer else 2))
                        if table:
                            stages.append((copy_turned_x, 2))
                        pipelined(e, R, NS, stages)

                    @block.tensor
                    def _(e):
                        def turn(i, s, a, ps, finished):
                            for k in range(G):
                                for m in range(K):
                                    mm = e.transpose(ps[:, (k * K + m) * P:(k * K + m + 1) * P], a[:, k, m * P:(m + 1) * P], ident[:])
                            mm.then_inc(signal(finished, s), 1)

                        def turn_r(i, s):
                            hold(e, *done(st_["rectified"], i, s))
                            hold(e, *done(st_["copied"], i, s, 2))
                            turn(i, s, yt[s], psR[s % 2], st_["turned"])

                        def product(i, s):
                            hold(e, *done(st_["copied"], i, s))
                            hold(e, *done(st_["summed"], i, s, 2))
                            for k in range(G):
                                for m in range(K):
                                    mm = e.matmul(psZ[s % 2][:, k * D:(k + 1) * D], rT[s][:, k, m * P:(m + 1) * P], w0s[:, m, :],
                                                  start=m == 0, stop=m == K - 1)
                            mm.then_inc(signal(st_["product"], s), 1)

                        def turn_x(i, s):
                            hold(e, *done(st_["normed"], i, s))
                            hold(e, *done(st_["copiedx"], i, s, 2))
                            turn(i, s, xo[s], psX[s % 2], st_["turnedx"])

                        def tabulate(i, s):
                            hold(e, *done(st_["copiedx"], i, s))
                            hold(e, *done(st_["evened"], i, s, 1))
                            for k in range(G):
                                for m in range(K):
                                    mm = e.matmul(psV[k][:, 0:TW], xT[s][:, k, m * P:(m + 1) * P], weights[:, m, :],
                                                  start=m == 0, stop=m == K - 1)
                                mm.then_inc(signal(st_["tabled"], s), 1)

                        stages = [(turn_r, 0), (product, 1)] if layer == 0 else []
                        if table:
                            stages += [(turn_x, 2), (tabulate, 3)]
                        if stages:
                            pipelined(e, R, NS, stages)

        def attention_edges(layer):
            with ExitStack() as ctx:
                G, NS, LAG = 2, 4, 2
                R = C // (G * NS)
                tiles = lambda n, w, dt=F32, p=P: [ctx.enter_context(sbuf(f"{n}{s}", [p, G, w], dt)) for s in range(NS)]
                table, dtable = (T1, T1) if layer == 1 else (T2, ET)
                W, DW = table.shape[1], dtable.shape[1]
                rows, rowsd, sums = tiles("rows", W), tiles("rowsd", DW), tiles("sums", SW)
                gi, gd, si = tiles("gi", 1, I32), tiles("gd", 1, I32), tiles("si", 1, I32)
                KA = 4 if layer == 1 else attr64T.shape[0]
                attr = tiles("attr", P, F32, KA)
                enc = tiles("enc", D) if layer == 1 else None
                lg, dot, mp, diff, ex = tiles("lg", H), tiles("dot", H), tiles("mp", H), tiles("diff", 2 * H), tiles("ex", 2 * H)
                EW = D if layer == 1 else H
                psE = [ctx.enter_context(psum(f"psE{j}", [P, 512], F32)) for j in range(2)]
                indexed, gathered, scattered, attred = (stage_of("indexed", NS, 3), stage_of("gathered", NS, 2 * G),
                                                        stage_of("scattered", NS, G), stage_of("attred", NS, 1))
                encoded, rectified, scored, exped, summed = (stage_of(n, NS) for n in ("encoded", "rectified", "scored", "exped", "summed"))
                steps, bsteps, started = [semaphore(n) for n in ("steps", "bsteps", "started")]
                heads = lambda a: a.rearrange("p (h w) -> p h w", h=H)
                with nc.Block() as block:
                    @block.sync
                    def _(e):
                        e.wait_ge(started, 1)
                        edge_attr = attr3T if layer == 1 else attr64T

                        def stage(i, s):
                            c = bass.ds(i * (G * NS) + s * G, G)
                            hold(e, *done(encoded, i, s, NS))
                            e.dma_start(attr[s][0:edge_attr.shape[0]], edge_attr[:, c, :]).then_inc(signal(attred, s), 16)
                            hold(e, *done(gathered, i, s, NS))
                            hold(e, *done(scattered, i, s, NS))
                            e.dma_start(gi[s][:, :, 0], src_i[:, c]).then_inc(signal(indexed, s), 16)
                            e.dma_start(gd[s][:, :, 0], dst_i[:, c]).then_inc(signal(indexed, s), 16)
                            e.dma_start(si[s][:, :, 0], scat_i[:, c]).then_inc(signal(indexed, s), 16)

                        pipelined(e, R, NS, [(stage, 0)])

                    @block.gpsimd
                    def _(e):
                        def gather(i, s):
                            hold(e, *done(indexed, i, s))
                            hold(e, *done(summed, i, s, NS))
                            for k in range(G):
                                e.indirect_dma_start(rowsd[s][:, k, :], None, dtable, bass.IndirectOffsetOnAxis(ap=gd[s][:, k, :], axis=0))\
                                    .then_inc(signal(gathered, s), 16)
                                e.indirect_dma_start(rows[s][:, k, :], None, table, bass.IndirectOffsetOnAxis(ap=gi[s][:, k, :], axis=0))\
                                    .then_inc(signal(gathered, s), 16)

                        def scatter(i, s):
                            hold(e, *done(summed, i, s))
                            for k in range(G):
                                e.indirect_dma_start(S, bass.IndirectOffsetOnAxis(ap=si[s][:, k, :], axis=0), sums[s][:, k, :], None,
                                                     bounds_check=NP - 1, oob_is_err=False).then_inc(signal(scattered, s), 16)

                        pipelined(e, R, NS, [(gather, 0), (scatter, LAG)])
                        for sem, value in total(scattered, R):
                            e.wait_ge(sem, value)

                    @block.tensor
                    def _(e):
                        weights = encs if layer == 1 else fes

                        def encode(i, s):
                            hold(e, *done(attred, i, s))
                            if layer == 1:
                                hold(e, *done(rectified, i, s, 2))
                            else:
                                hold(e, *done(scored, i, s, 2))
                            for k in range(G):
                                mm = e.matmul(psE[s % 2][:, k * EW:(k + 1) * EW], attr[s][:, k, :], weights[:], start=True, stop=True)
                            mm.then_inc(signal(encoded, s), 1)

                        pipelined(e, R, NS, [(encode, 0)])

                    @block.scalar
                    def _(e):
                        def rectify(i, s):
                            hold(e, *done(encoded, i, s))
                            hold(e, *done(scored, i, s, NS))
                            e.activation(enc[s][:].rearrange("p g d -> p (g d)"), psE[s % 2][:], ACT.Relu).then_inc(signal(rectified, s), 1)

                        def exponentials(i, s):
                            hold(e, *done(scored, i, s))
                            hold(e, *done(summed, i, s, NS))
                            e.activation(ex[s][:], diff[s][:], ACT.Exp).then_inc(signal(exped, s), 1)

                        pipelined(e, R, NS, ([(rectify, 0)] if layer == 1 else []) + [(exponentials, 0)])

                    @block.vector
                    def _(e):
                        for s in range(NS):
                            ins = e.memset(sums[s][:], 0.0)
                            if layer == 1:
                                ins = e.memset(attr[s][:], 1.0)
                        ins.then_inc(started, 1)
                        e.wait_ge(started, 1)
                        SC = 8 if layer == 1 else 6

                        def score(i, s):
                            n = [0]

                            def link(ins):
                                n[0] += 1
                                ins.then_inc(steps, 1)
                                e.wait_ge(steps, i * (NS * SC) + (s * SC + n[0]))

                            hold(e, *done(gathered, i, s))
                            hold(e, *done(scattered, i, s, NS))
                            hold(e, *done(summed, i, s, NS))
                            hold(e, *done(exped, i, s, NS))
                            if layer == 1:
                                hd = rowsd[s][:, :, 0:VW].rearrange("p g (h w) -> p g h w", h=H)[:, :, :, 0:HD]
                                e4 = enc[s][:].rearrange("p g (h d) -> p g h d", h=H)
                                hold(e, *done(rectified, i, s))
                                link(e.tensor_tensor(e4, e4, hd, ALU.mult))
                                link(e.tensor_reduce(dot[s][:], e4, AX, ALU.add))
                                link(e.tensor_tensor(dot[s][:], dot[s][:], rows[s][:, :, VW:SW], ALU.add))
                                link(e.tensor_tensor(dot[s][:], dot[s][:], rowsd[s][:, :, SW:TW], ALU.add))
                            else:
                                hold(e, *done(encoded, i, s))
                                link(e.tensor_tensor(dot[s][:], rows[s][:, :, VW:SW], rowsd[s][:], ALU.add))
                                link(e.tensor_tensor(dot[s][:], dot[s][:], psE[s % 2][:, 0:G * H].rearrange("p (g h) -> p g h", g=G), ALU.add))
                            link(e.scalar_tensor_tensor(lg[s][:], dot[s][:], 0.2, dot[s][:], ALU.mult, ALU.max))
                            for k in range(G):
                                pc = pen[:, bass.ds(i * (G * NS) + (s * G + k), 1)]
                                last = sums[s][:, k - 1, VW:SW] if k else sums[(s - 1) % NS][:, G - 1, VW:SW]
                                e.tensor_scalar(mp[s][:, k, :], last, pc, None, ALU.add)
                                link(e.scalar_tensor_tensor(sums[s][:, k, VW:SW], last, pc, lg[s][:, k, :], ALU.add, ALU.max))
                            link(e.tensor_tensor(diff[s][:, :, 0:H], mp[s][:], sums[s][:, :, VW:SW], ALU.subtract))
                            e.tensor_tensor(diff[s][:, :, H:2 * H], lg[s][:], sums[s][:, :, VW:SW], ALU.subtract).then_inc(signal(scored, s), 1)
                            assert n[0] == SC

                        def add(i, s):
                            hold(e, *done(exped, i, s))
                            wide = lambda a: a.rearrange("p g (h w) -> p g h w", w=1).to_broadcast([P, G, H, HW])
                            v = rows[s][:, :, 0:VW].rearrange("p g (h w) -> p g h w", h=H)
                            e.tensor_tensor(v, v, wide(ex[s][:, :, H:2 * H]), ALU.mult)
                            B = 2 * G - 1
                            n = 0
                            for k in range(G):
                                last = sums[s][:, k - 1, 0:VW] if k else sums[(s - 1) % NS][:, G - 1, 0:VW]
                                r = ex[s][:, k, 0:H].rearrange("p (h w) -> p h w", w=1).to_broadcast([P, H, HW])
                                n += 1
                                e.tensor_tensor(heads(sums[s][:, k, 0:VW]), heads(last), r, ALU.mult).then_inc(bsteps, 1)
                                e.wait_ge(bsteps, i * (NS * B) + (s * B + n))
                                ins = e.tensor_tensor(sums[s][:, k, 0:VW], sums[s][:, k, 0:VW], rows[s][:, k, 0:VW], ALU.add)
                                if k < G - 1:
                                    n += 1
                                    ins.then_inc(bsteps, 1)
                                    e.wait_ge(bsteps, i * (NS * B) + (s * B + n))
                            ins.then_inc(signal(summed, s), 1)
                            hold(e, *done(summed, i, s))

                        pipelined(e, R, NS, [(score, 0), (add, 1)])
                with nc.Block() as block:
                    end = sums[NS - 1][:, G - 1, :]
                    t = lambda n, sh: ctx.enter_context(sbuf(n, sh, F32))
                    own, mall, eT, mc, mn, r, dm = (t("own", [P, SW]), t("mall", [P, H, P]), t("eT", [P, H, P]), t("mc", [P, H]),
                                                    t("mn", [P, H]), t("r", [P, H]), t("dm", [P, H]))
                    psM = ctx.enter_context(psum("psM", [P, H, P], F32))
                    psC = ctx.enter_context(psum("psC", [P, 512], F32))
                    fetched, cleared, turned, fx, exd, put = [semaphore(n) for n in (
                        "fetched", "cleared", "fturned", "fx", "exd", "put")]

                    @block.gpsimd
                    def _(e):
                        at = bass.IndirectOffsetOnAxis(ap=first_i[:], axis=0)
                        e.wait_ge(cleared, 1)
                        e.indirect_dma_start(own[:], None, S, at, bounds_check=NP - 1, oob_is_err=False).then_inc(fetched, 16)
                        e.wait_ge(fx, 9)
                        e.indirect_dma_start(S, at, own[:], None, bounds_check=NP - 1, oob_is_err=False).then_inc(put, 16)
                        e.wait_ge(put, 16)

                    @block.tensor
                    def _(e):
                        for h in range(H):
                            mm = e.transpose(psM[:, h, :], end[:, VW + h:VW + h + 1].to_broadcast([P, P]), ident[:])
                        mm.then_inc(turned, 1)
                        e.wait_ge(exd, 1)
                        for h in range(H):
                            mm = e.transpose(psM[:, h, :], mall[:, h, :], ident[:])
                        mm.then_inc(turned, 1)
                        e.wait_ge(fx, 6)
                        for h in range(H):
                            mm = e.matmul(psC[:, h * HW:(h + 1) * HW], eT[:, h, :], end[:, h * HW:(h + 1) * HW], start=True, stop=True)
                        mm.then_inc(turned, 1)

                    @block.scalar
                    def _(e):
                        e.wait_ge(fx, 5)
                        e.activation(mall[:], mall[:], ACT.Exp).then_inc(exd, 1)
                        e.activation(r[:], dm[:], ACT.Exp).then_inc(exd, 1)

                    @block.vector
                    def _(e):
                        n = [0]

                        def link(ins):
                            n[0] += 1
                            ins.then_inc(fx, 1)
                            e.wait_ge(fx, n[0])

                        e.memset(own[:], 0.0).then_inc(cleared, 1)
                        e.wait_ge(turned, 1)
                        link(e.tensor_tensor(mall[:], psM[:], penT[:].rearrange("p (h q) -> p h q", h=1).to_broadcast([P, H, P]), ALU.add))
                        link(e.tensor_reduce(mc[:], mall[:], AX, ALU.max))
                        e.wait_ge(fetched, 16)
                        link(e.tensor_tensor(mn[:], mc[:], own[:, VW:SW], ALU.max))
                        link(e.tensor_tensor(dm[:], own[:, VW:SW], mn[:], ALU.subtract))
                        link(e.tensor_tensor(mall[:], mall[:], mn[:].rearrange("p (h q) -> p h q", q=1).to_broadcast([P, H, P]), ALU.subtract))
                        e.wait_ge(turned, 2)
                        link(e.tensor_copy(eT[:], psM[:]))
                        e.wait_ge(exd, 2)
                        link(e.tensor_tensor(heads(own[:, 0:VW]), heads(own[:, 0:VW]), r[:].rearrange("p (h w) -> p h w", w=1).to_broadcast([P, H, HW]), ALU.mult))
                        e.wait_ge(turned, 3)
                        link(e.tensor_tensor(own[:, 0:VW], own[:, 0:VW], psC[:, 0:VW], ALU.add))
                        link(e.tensor_copy(own[:, VW:SW], mn[:]))

        def filter_edges():
            with ExitStack() as ctx:
                G, NS, LAG = 2, 4, 2
                R = C // (G * NS)
                tiles = lambda n, w, dt=F32, p=P: [ctx.enter_context(sbuf(f"{n}{s}", [p, G, w], dt)) for s in range(NS)]
                NG = rbfT.shape[0]
                rbf = tiles("rbf", P, F32, NG)
                rows, comb, eq, low = tiles("rows", D), tiles("comb", D), tiles("eq", P), tiles("low", P)
                hid = [ctx.enter_context(sbuf(f"hid{s}", [P, K, G * P], F32)) for s in range(NS)]
                fl = tiles("fl", D)
                sc, cnt, gi, ai = tiles("sc", 1), tiles("cnt", 1), tiles("gi", 1, I32), tiles("ai", 1, I32)
                bank = lambda n: ctx.enter_context(psum(n, [P, 512], F32))
                psH, psI, psF, psM = [[bank(f"{n}{j}") for j in range(2)] for n in ("psH", "psI", "psF", "psM")]
                indexed, gathered, added, attred = (stage_of("indexed", NS, 1), stage_of("gathered", NS, G),
                                                    stage_of("added", NS, G), stage_of("attred", NS, 1))
                stages = [stage_of(n, NS) for n in (
                    "columned", "hidden", "sourced", "active", "filtered", "compared", "message", "joined", "copied")]
                columned, hidden, sourced, active, filtered, compared, message, joined, copied = stages
                steps, msteps = [semaphore(n) for n in ("steps", "msteps")]
                with nc.Block() as block:
                    @block.sync
                    def _(e):

                        def stage(i, s):
                            c = bass.ds(i * (G * NS) + s * G, G)
                            hold(e, *done(hidden, i, s, NS))
                            e.dma_start(rbf[s][:], rbfT[:, c, :]).then_inc(signal(attred, s), 16)
                            hold(e, *done(gathered, i, s, NS))
                            e.dma_start(gi[s][:, :, 0], dst_i[:, c]).then_inc(signal(indexed, s), 16)

                        pipelined(e, R, NS, [(stage, 0)])

                    @block.gpsimd
                    def _(e):
                        def gather(i, s):
                            hold(e, *done(indexed, i, s))
                            hold(e, *done(message, i, s, NS))
                            for k in range(G):
                                e.indirect_dma_start(rows[s][:, k, :], None, X3, bass.IndirectOffsetOnAxis(ap=gi[s][:, k, :], axis=0))\
                                    .then_inc(signal(gathered, s), 16)

                        def add(i, s):
                            hold(e, *done(copied, i, s))
                            hold(e, *done(added, i, s, 1))
                            for k in range(G):
                                e.indirect_dma_start(A[k], bass.IndirectOffsetOnAxis(ap=ai[s][:, k, :], axis=0), comb[s][:, k, :], None,
                                                     compute_op=ALU.add).then_inc(signal(added, s), 16)

                        pipelined(e, R, NS, [(gather, 0), (add, LAG)])
                        for sem, value in total(added, R):
                            e.wait_ge(sem, value)

                    @block.tensor
                    def _(e):
                        def hide(i, s):
                            hold(e, *done(attred, i, s))
                            hold(e, *done(active, i, s, 2))
                            for m in range(K):
                                mm = e.matmul(psH[s % 2][:, m * G * P:(m + 1) * G * P], wf1s[:, m * P:(m + 1) * P],
                                              rbf[s][:].rearrange("p g q -> p (g q)"), start=True, stop=True)
                            mm.then_inc(signal(hidden, s), 1)
                            hold(e, *done(compared, i, s, 2))
                            hold(e, *done(columned, i, s))
                            for k in range(G):
                                mm = e.transpose(psI[s % 2][:, k * P:(k + 1) * P], sc[s][:, k, :].to_broadcast([P, P]), ident[:])
                            mm.then_inc(signal(sourced, s), 1)

                        def filt(i, s):
                            hold(e, *done(active, i, s))
                            hold(e, *done(message, i, s, 2))
                            for k in range(G):
                                for m in range(K):
                                    mm = e.matmul(psF[s % 2][:, k * D:(k + 1) * D], hid[s][:, m, k * P:(k + 1) * P], wf2s[:, m, :],
                                                  start=m == 0, stop=m == K - 1)
                            mm.then_inc(signal(filtered, s), 1)

                        def join(i, s):
                            hold(e, *done(message, i, s))
                            hold(e, *done(compared, i, s))
                            hold(e, *done(copied, i, s, 2))
                            for k in range(G):
                                mm = e.matmul(psM[s % 2][:, k * D:(k + 1) * D], eq[s][:, k, :], fl[s][:, k, :], start=True, stop=True)
                            mm.then_inc(signal(joined, s), 1)

                        pipelined(e, R, NS, [(hide, 0), (filt, 1), (join, 2)])

                    @block.scalar
                    def _(e):
                        def column(i, s):
                            hold(e, *done(sourced, i, s, NS))
                            e.copy(sc[s][:, :, 0], src_f[:, bass.ds(i * (G * NS) + s * G, G)]).then_inc(signal(columned, s), 1)

                        def activate(i, s):
                            hold(e, *done(hidden, i, s))
                            hold(e, *done(message, i, s, NS))
                            for m in range(K):
                                ins = e.activation(hid[s][:, m, :], psH[s % 2][:, m * G * P:(m + 1) * G * P], ACT.Silu, bias=bf1s[:, m:m + 1])
                            ins.then_inc(signal(active, s), 1)

                        def copy(i, s):
                            hold(e, *done(joined, i, s))
                            hold(e, *done(added, i, s, NS))
                            e.copy(comb[s][:].rearrange("p g d -> p (g d)"), psM[s % 2][:]).then_inc(signal(copied, s), 1)

                        pipelined(e, R, NS, [(column, 0), (activate, 0), (copy, 2)])

                    @block.vector
                    def _(e):
                        def compare(i, s):
                            hold(e, *done(sourced, i, s))
                            hold(e, *done(joined, i, s, NS))
                            hold(e, *done(added, i, s, NS))
                            for k in range(G):
                                c = bass.ds(i * (G * NS) + (s * G + k), 1)
                                turned_k = psI[s % 2][:, k * P:(k + 1) * P]
                                e.tensor_scalar(eq[s][:, k, :], turned_k, src_f[:, c], None, ALU.is_equal)
                                e.scalar_tensor_tensor(low[s][:, k, :], turned_k, src_f[:, c], earlier[:], ALU.is_equal, ALU.mult,
                                                       accum_out=cnt[s][:, k, :]).then_inc(steps, 1)
                            base = G + 2
                            e.wait_ge(steps, i * (NS * base) + (s * base + G))
                            e.tensor_scalar(cnt[s][:], cnt[s][:], 0.0, None, ALU.is_equal).then_inc(steps, 1)
                            e.wait_ge(steps, i * (NS * base) + (s * base + G + 1))
                            c = bass.ds(i * (G * NS) + s * G, G)
                            e.tensor_tensor(cnt[s][:, :, 0], cnt[s][:, :, 0], srcmt[:, c], ALU.mult).then_inc(steps, 1)
                            e.wait_ge(steps, i * (NS * base) + (s * base + G + 2))
                            e.tensor_scalar(ai[s][:], cnt[s][:], trash[:], None, ALU.add).then_inc(signal(compared, s), 1)

                        def multiply(i, s):
                            hold(e, *done(filtered, i, s))
                            hold(e, *done(joined, i, s, NS))
                            hold(e, *done(gathered, i, s))
                            e.tensor_tensor(fl[s][:], psF[s % 2][:].rearrange("p (g d) -> p g d", g=G),
                                            bf2s[:].rearrange("p (g d) -> p g d", g=1).to_broadcast([P, G, D]), ALU.add).then_inc(msteps, 1)
                            e.wait_ge(msteps, i * NS + (s + 1))
                            e.tensor_tensor(fl[s][:], fl[s][:], rows[s][:], ALU.mult).then_inc(signal(message, s), 1)

                        pipelined(e, R, NS, [(compare, 0), (multiply, 1)])

        def update_nodes():
            with ExitStack() as ctx:
                G, NS = 4, 2
                R = C // (G * NS)
                t = lambda n: [ctx.enter_context(sbuf(f"{n}{s}", [P, K, G * P], F32)) for s in range(NS)]
                agg, more = [[ctx.enter_context(sbuf(f"{n}{s}", [P, G, D], F32)) for s in range(NS)] for n in ("agg", "more")]
                aT, hid, ht = t("aT"), t("hid"), t("ht")
                psA, psH, psO = [ctx.enter_context(psum(n, [P, K, G * P], F32)) for n in ("psA", "psH", "psO")]
                loaded, stored = stage_of("loaded", NS, 2), stage_of("stored", NS, 1)
                stages = [stage_of(n, NS) for n in ("summed", "turned", "copied", "hidden", "active", "updated", "biased", "measured")]
                summed, turned, copied, hidden, active, updated, biased, measured = stages
                with nc.Block() as block:
                    @block.sync
                    def _(e):

                        def load(i, s):
                            c = bass.ds(i * (G * NS) + s * G, G)
                            hold(e, *done(stored, i, s, NS))
                            hold(e, *done(measured, i, s, NS))
                            e.dma_start(agg[s][:], nodes(A[0])[:, c, :]).then_inc(signal(loaded, s), 16)
                            e.dma_start(more[s][:], nodes(A[1])[:, c, :]).then_inc(signal(loaded, s), 16)

                        def store(i, s):
                            hold(e, *done(biased, i, s))
                            e.dma_start(HT[:, bass.ds(i * NS + s, 1), :, :].rearrange("p g k q -> p (g k) q"), ht[s][:]).then_inc(signal(stored, s), 16)

                        pipelined(e, R, NS, [(load, 0), (store, 1)])
                        for sem, value in total(stored, R):
                            e.wait_ge(sem, value)

                    @block.tensor
                    def _(e):
                        def turn(i, s):
                            hold(e, *done(summed, i, s))
                            hold(e, *done(copied, i, s, 1))
                            for m in range(K):
                                for k in range(G):
                                    mm = e.transpose(psA[:, m, k * P:(k + 1) * P], agg[s][:, k, m * P:(m + 1) * P], ident[:])
                            mm.then_inc(signal(turned, s), 1)

                        def product(a, w, ps, finished, s):
                            for n in range(K):
                                for m in range(K):
                                    mm = e.matmul(ps[:, n, :], w[:, m, n * P:(n + 1) * P], a[s][:, m, :], start=m == 0, stop=m == K - 1)
                            mm.then_inc(signal(finished, s), 1)

                        def hide(i, s):
                            hold(e, *done(copied, i, s))
                            hold(e, *done(active, i, s, 1))
                            product(aT, wu1s, psH, hidden, s)

                        def update(i, s):
                            hold(e, *done(active, i, s))
                            hold(e, *done(biased, i, s, 1))
                            product(hid, wu2s, psO, updated, s)

                        pipelined(e, R, NS, [(turn, 0), (update, 1), (hide, 0)])

                    @block.scalar
                    def _(e):
                        def activate(i, s):
                            hold(e, *done(hidden, i, s))
                            for m in range(K):
                                ins = e.activation(hid[s][:, m, :], psH[:, m, :], ACT.Silu, bias=bu1s[:, m:m + 1])
                            ins.then_inc(signal(active, s), 1)

                        def bias(i, s):
                            hold(e, *done(updated, i, s))
                            for m in range(K):
                                ins = e.activation(ht[s][:, m, :], psO[:, m, :], ACT.Identity, bias=bu2s[:, m:m + 1])
                            ins.then_inc(signal(biased, s), 1)

                        pipelined(e, R, NS, [(bias, 1), (activate, 0)])

                    @block.vector
                    def _(e):
                        def add(i, s):
                            hold(e, *done(loaded, i, s))
                            e.tensor_tensor(agg[s][:], agg[s][:], more[s][:], ALU.add).then_inc(signal(summed, s), 1)

                        def copy(i, s):
                            hold(e, *done(turned, i, s))
                            e.tensor_copy(aT[s][:], psA[:]).then_inc(signal(copied, s), 1)

                        full = VC // (G * NS)
                        there = [P]

                        def measure(i, s):
                            if isinstance(i, int):
                                there[0] = P if i < full else P - 1
                            hold(e, *done(biased, i, s))
                            for m in range(K):
                                h4 = ht[s][:, m, :].rearrange("p (g q) -> p g q", g=G)[:, :, 0:there[0]]
                                ins = e.bn_stats(stats[:, m, bass.ds(i * NS + s, 1), :].rearrange("p a b -> p (a b)"), h4)
                            ins.then_inc(signal(measured, s), 1)

                        pipelined(e, R, NS, [(add, 0), (copy, 0), (measure, 1)], cut=full)

        def finish_nodes():
            with ExitStack() as ctx:
                G, NS = 4, 2
                R = C // (G * NS)
                mv, sd, scale, shift = [ctx.enter_context(sbuf(n, [P, K, w], F32)) for n, w in (("bmv", 2), ("bsd", 1), ("scale", 1), ("shift", 1))]
                ht = [ctx.enter_context(sbuf(f"ht{s}", [P, K, G * P], F32)) for s in range(NS)]
                xt, z, xo = [[ctx.enter_context(sbuf(f"{n}{s}", [P, G, D], F32)) for s in range(NS)] for n in ("xt", "z", "xo")]
                ps = [ctx.enter_context(psum(f"psN{j}", [P, G, D], F32)) for j in range(NS)]
                loaded, stored = stage_of("loaded", NS, 2), stage_of("stored", NS, 1)
                stages = [stage_of(n, NS) for n in ("normed", "turned", "summed", "finished")]
                normed, turned, summed, finished = stages
                ln_measure, ln_root, ln_invert, ln_apply = norm_of(ctx, NS, G, z, xo)
                agged, rooted, scaled = [semaphore(n) for n in ("agged", "brooted", "scaled")]
                with nc.Block() as block:
                    @block.sync
                    def _(e):

                        def load(i, s):
                            hold(e, *done(stored, i, s, NS))
                            e.dma_start(ht[s][:], HT[:, bass.ds(i * NS + s, 1), :, :].rearrange("p g k q -> p (g k) q")).then_inc(signal(loaded, s), 16)
                            e.dma_start(xt[s][:], nodes(X3)[:, bass.ds(i * (G * NS) + s * G, G), :]).then_inc(signal(loaded, s), 16)

                        def store(i, s):
                            hold(e, *done(finished, i, s))
                            e.dma_start(out[:, bass.ds(i * (G * NS) + s * G, G), :], xo[s][:]).then_inc(signal(stored, s), 16)

                        pipelined(e, R, NS, [(load, 0), (store, 1)])
                        for sem, value in total(stored, R):
                            e.wait_ge(sem, value)

                    @block.tensor
                    def _(e):
                        def turn(i, s):
                            hold(e, *done(normed, i, s))
                            hold(e, *done(summed, i, s, NS))
                            for k in range(G):
                                for m in range(K):
                                    mm = e.transpose(ps[s][:, k, m * P:(m + 1) * P], ht[s][:, m, k * P:(k + 1) * P], ident[:])
                            mm.then_inc(signal(turned, s), 1)

                        pipelined(e, R, NS, [(turn, 0)])

                    @block.scalar
                    def _(e):
                        e.wait_ge(agged, 1)
                        e.activation(sd[:, :, 0], mv[:, :, 1], ACT.Sqrt, bias=epsc[:]).then_inc(rooted, 1)
                        e.wait_ge(scaled, 4)

                        def batch_norm(i, s):
                            hold(e, *done(loaded, i, s))
                            for m in range(K):
                                ins = e.activation(ht[s][:, m, :], ht[s][:, m, :], ACT.Identity, bias=shift[:, m, :], scale=scale[:, m, :])
                            ins.then_inc(signal(normed, s), 1)

                        pipelined(e, R, NS, [(batch_norm, 0), (lambda i, s: ln_root(e, i, s), 0), (lambda i, s: ln_apply(e, i, s, finished), 1)])

                    @block.vector
                    def _(e):
                        for m in range(K):
                            ins = e.bn_aggr(mv[:, m, :], stats[:, m, :, :].rearrange("p a b -> p (a b)"))
                        ins.then_inc(agged, 1)
                        e.wait_ge(rooted, 1)
                        e.reciprocal(sd[:], sd[:]).then_inc(scaled, 1)
                        e.wait_ge(scaled, 1)
                        e.tensor_tensor(scale[:, :, 0], sd[:, :, 0], gms[:], ALU.mult).then_inc(scaled, 1)
                        e.wait_ge(scaled, 2)
                        e.tensor_tensor(shift[:, :, 0], scale[:, :, 0], mv[:, :, 0], ALU.mult).then_inc(scaled, 1)
                        e.wait_ge(scaled, 3)
                        e.tensor_tensor(shift[:, :, 0], bts[:], shift[:, :, 0], ALU.subtract).then_inc(scaled, 1)

                        def add(i, s):
                            hold(e, *done(turned, i, s))
                            e.scalar_tensor_tensor(z[s][:], xt[s][:], 2.0, ps[s][:], ALU.mult, ALU.add).then_inc(signal(summed, s), 1)
                            hold(e, *done(summed, i, s))
                            ln_measure(e, i, s)

                        pipelined(e, R, NS, [(add, 0), (lambda i, s: ln_invert(e, i, s), 1)])

        for phase in (setup, lambda: hop_table(True), hop_edges, lambda: hop_table(False), hop_edges,
                      lambda: layer_nodes(0), lambda: attention_edges(1), lambda: layer_nodes(1),
                      lambda: attention_edges(2), lambda: layer_nodes(2), filter_edges, update_nodes, finish_nodes):
            with nc.cleanup_on_exit():
                phase()


def kernel(**inputs):
    import numpy as np
    import concourse.bacc as bacc
    from concourse.bass_utils import run_bass_kernel_spmd

    a = {k: np.asarray(v) for k, v in inputs.items()}
    N, E = a["x"].shape[0], a["src"].shape[0]
    C = -(-max(N, E) // (P * 8)) * 8
    NP = P * C

    def pad(v, fill=0):
        return np.concatenate([v, np.full((NP - v.shape[0], *v.shape[1:]), fill, v.dtype)])

    def by_column(v):
        return np.ascontiguousarray(pad(v).reshape(P, C, -1).transpose(2, 1, 0))

    def spread(v):
        m = np.zeros((D, H), v.dtype)
        for h in range(H):
            m[h * HD:(h + 1) * HD, h] = v[h]
        return m

    def with_gaps(w):
        m = np.zeros((D, TW), w.dtype)
        m[:, 0:VW].reshape(D, H, HW)[:, :, 0:HD] = w.reshape(D, H, HD)
        return m

    halves = lambda v: np.ascontiguousarray(v.reshape(K, P).T)
    row = lambda v: v.reshape(1, D)
    dst = np.concatenate([pad(a["dst"], N), np.full(1, N + 1, a["dst"].dtype)])
    T = lambda v: np.ascontiguousarray(v.T)
    arrays = dict(
        x=pad(a["x"]).reshape(P, C, D), src=pad(a["src"], N).reshape(P, C), dst=np.ascontiguousarray(dst[:NP].reshape(P, C)),
        dst_next=np.ascontiguousarray(dst[1:].reshape(P, C)), ew=pad(a["edge_weight"]).reshape(P, C),
        rbfT=by_column(a["edge_attr_20"]), attr3T=by_column(a["edge_attr_3"]), attr64T=by_column(a["edge_attr_64"]),
        w0T=T(a["L0_gnn_W"]), b0=row(a["L0_gnn_b"]),
        w1aug=with_gaps(T(a["L1_gnn_W"])), w1=a["L1_gnn_W"],
        a1=np.concatenate([spread(a["L1_gnn_a_src"]), spread(a["L1_gnn_a_dst"])], axis=1),
        encW=np.concatenate([T(a["L1_gnn_edge_W"]), row(a["L1_gnn_edge_b"])]), bias1=row(a["L1_gnn_bias"]),
        wfc=with_gaps(a["L2_gnn_W_fc"]), wfcT=T(a["L2_gnn_W_fc"]),
        ah=np.concatenate([spread(a["L2_gnn_attn_h"]), spread(a["L2_gnn_attn_t"])], axis=1),
        ae=spread(a["L2_gnn_attn_e"]), weT=T(a["L2_gnn_W_e"]), bias2=row(a["L2_gnn_bias"]),
        wf1=a["L3_gnn_Wf1"], bf1=halves(a["L3_gnn_bf1"]), wf2=a["L3_gnn_Wf2"], bf2=row(a["L3_gnn_bf2"]),
        wu1=a["L3_gnn_Wu1"], bu1=halves(a["L3_gnn_bu1"]), wu2=a["L3_gnn_Wu2"], bu2=halves(a["L3_gnn_bu2"]),
        gamma=halves(a["L3_gnn_gamma"]), beta=halves(a["L3_gnn_beta"]))
    nc = bacc.Bacc("TRN2", target_bir_lowering=False, num_devices=1)
    args = {n: nc.dram_tensor(f"in_{n}", v.shape, mybir.dt.from_np(v.dtype), kind="ExternalInput").ap() for n, v in arrays.items()}
    out = nc.dram_tensor("out", (P, C, D), F32, kind="ExternalOutput").ap()
    build(nc, N, out=out, **args)
    r = run_bass_kernel_spmd(nc, [{f"in_{n}": v for n, v in arrays.items()}], core_ids=[0])
    return r.results[0]["out"].reshape(NP, D)[:N]
```

```python
from contextlib import ExitStack

import concourse.bass as bass
from concourse import mybir

P = 128
D = 256
H = 8
HD = D // H
HW = HD + 1
VW = H * HW
SW = VW + H
TW = SW + H
DW = D + 2 * H
K = D // P
NONE = -1.0e30
OUT = 1.0e6
EPS = 1e-5

ALU = mybir.AluOpType
ACT = mybir.ActivationFunctionType
AX = mybir.AxisListType.X
F32 = mybir.dt.float32
I32 = mybir.dt.int32



def signal(stage, s):
    sems, _, dmas = stage
    return sems[s if dmas else 0]


def done(stage, i, s, back=0):
    sems, slots, dmas = stage
    if dmas:
        return sems[(s - back) % slots], (i + ((s - back) // slots + 1)) * (16 * dmas)
    return sems[0], i * slots + (s - back + 1)


def total(stage, rounds):
    sems, slots, dmas = stage
    return [(sem, rounds * (16 * dmas if dmas else slots)) for sem in sems]


def pipelined(e, rounds, slots, stages, cut=0):
    most = max(lag for _, lag in stages)

    def step(i, s, which=lambda lag: True):
        for stage, lag in stages:
            if which(lag):
                stage(i + (s - lag) // slots, (s - lag) % slots)

    def loop(first, last):
        if first < last:
            with e.Fori(first, last) as i:
                for s in range(slots):
                    step(i, s)

    start = 1 - (-most // slots)
    assert start < rounds
    for i in range(start):
        for s in range(slots):
            step(i, s, lambda lag: i * slots + s >= lag)
    if cut >= start:
        loop(start, cut)
        start = cut - (-most // slots)
        for i in range(cut, start):
            for s in range(slots):
                step(i, s)
    loop(start, rounds)
    for s in range(most):
        step(rounds, s, lambda lag: lag > s)


def build(nc, N, x, src, dst, dst_next, ew, rbfT, attr3T, attr64T, w0T, b0, w1T, w1, a1, encW, bias1,
          wfc, wfcT, ah, ae, weT, bias2, wf1, bf1, wf2, bf2, wu1, bu1, wu2, bu2, gamma, beta, out):
    C = x.shape[1]
    NP = P * C
    VC = N - (P - 1) * C
    assert C % 8 == 0 and VC % 8 == 0 and 0 < VC < C

    alone = (nc.sync.engine, nc.gpsimd.engine, nc.scalar.engine)
    used = {}

    def fresh(name):
        used[name] = used.get(name, 0) + 1
        return f"{name}_{used[name]}"

    def semaphore(name):
        return nc.alloc_semaphore(fresh(name))

    def stage_of(name, slots, dmas=0):
        return [semaphore(f"{name}{s}") for s in range(slots if dmas else 1)], slots, dmas

    def sbuf(name, shape, dt):
        return nc.sbuf_tensor(fresh(name), shape, dt)

    def psum(name, shape, dt):
        return nc.psum_tensor(fresh(name), shape, dt)

    marks = nc.alloc_semaphore("marks")

    def hold(e, sem, value):
        if isinstance(value, int) and value <= 0:
            return
        e.wait_ge(sem, value)
        if e.engine in alone:
            e.sem_inc(marks, 1)

    def dram(name, rows, width):
        return nc.dram_tensor(name, (rows, width), F32).ap()

    def nodes(t):
        return t[0:NP, :].rearrange("(p c) d -> p c d", p=P)

    Y, S = dram("Y", NP, D), dram("S", NP, SW)
    X1, X2, X3 = dram("X1", NP, D), dram("X2", NP, D), dram("X3", NP, D)
    T1, T2, ET = dram("T1", NP, TW), dram("T2", NP, SW), dram("ET", NP, H)
    A = [dram("A0", NP + P, D), dram("A1", NP + P, D)]
    HT = nc.dram_tensor("HT", (P, K, C * P), F32).ap()

    with ExitStack() as keep:
        def sb(name, shape, dt=F32):
            return keep.enter_context(sbuf(name, shape, dt))

        src_i, dst_i, scat_i = sb("src_i", [P, C], I32), sb("dst_i", [P, C], I32), sb("scat_i", [P, C], I32)
        src_f, same, pen, w_sb = sb("src_f", [P, C]), sb("same", [P, C]), sb("pen", [P, C]), sb("w_sb", [P, C])
        dinv, ca, cb, srcmt = sb("dinv", [P, C]), sb("ca", [P, C]), sb("cb", [P, C]), sb("srcmt", [P, C])
        first_i = sb("first_i", [P, 1], I32)
        trash = sb("trash", [P, 1])
        ident, before, earlier, chain, chainT, penT = [sb(n, [P, P]) for n in ("ident", "before", "earlier", "chain", "chainT", "penT")]
        epsc = sb("epsc", [P, 1])
        w0s, wf2s, wu1s, wu2s = [sb(n, [P, K, D]) for n in ("w0s", "wf2s", "wu1s", "wu2s")]
        w1s, w2s = sb("w1s", [P, K, DW]), sb("w2s", [P, K, DW])
        encs, wf1s, fes = sb("encs", [4, D]), sb("wf1s", [wf1.shape[0], D]), sb("fes", [attr64T.shape[0], H])
        b0s, b1s, b2s, bf2s = [sb(n, [P, D]) for n in ("b0s", "b1s", "b2s", "bf2s")]
        bf1s, bu1s, bu2s, gms, bts = [sb(n, [P, K]) for n in ("bf1s", "bu1s", "bu2s", "gms", "bts")]
        zero = sb("zero", [P, SW])
        stats = sb("stats", [P, K, C // 2, 6])

        def setup():
            with ExitStack() as ctx:
                def tmp(name, shape, dt=F32):
                    return ctx.enter_context(sbuf(name, shape, dt))

                def sem(name):
                    return semaphore(name)

                dst_f, next_i, islast, notl = tmp("dst_f", [P, C]), tmp("next_i", [P, C], I32), tmp("islast", [P, C]), tmp("notl", [P, C])
                any_last, firstf, lastf = tmp("any_last", [P, 1]), tmp("firstf", [P, 1]), tmp("lastf", [P, 1])
                cols, rows0 = tmp("cols", [P, C]), tmp("rows0", [P, P])
                pcol, w1n, a1s, wfT, ahs, aes, weTs = (tmp("pcol", [P, 1]), tmp("w1n", [P, K, D]), tmp("a1s", [P, K, 2 * H]),
                                                  tmp("wfT", [P, K, D]), tmp("ahs", [P, K, 2 * H]), tmp("aes", [P, K, H]),
                                                  tmp("weTs", [P, K, attr64T.shape[0]]))
                part_i, part, col, over = tmp("part_i", [P, C], I32), tmp("part", [P, C]), tmp("col", [P, C]), tmp("over", [P, C])
                hot, hotc = tmp("hot", [P, 4, P]), tmp("hotc", [P, 4, C])
                psT = ctx.enter_context(psum("psT", [P, P], F32))
                psDeg = ctx.enter_context(psum("psDeg", [P, 512], F32))
                psF = ctx.enter_context(psum("psF", [P, K, 16], F32))
                psG = ctx.enter_context(psum("psG", [P, K, 16], F32))
                psE = ctx.enter_context(psum("psE", [P, 16], F32))
                loaded, zeroed, iotas, prep, tr, folds, onehot, summed, filled, rooted = [sem(n) for n in (
                    "loaded", "zeroed", "iotas", "prep", "tr", "folds", "onehot", "summed", "filled", "rooted")]
                loads = [(src_i[:], src), (dst_i[:], dst), (next_i[:], dst_next), (w_sb[:], ew),
                         (encs[:], encW), (wf1s[:], wf1)]
                loads += [(t[:, :, :], w.rearrange("(k p) d -> p k d", p=P)) for t, w in (
                    (w0s, w0T), (w1s[:, :, 0:D], w1T), (w2s[:, :, 0:D], wfc), (wf2s, wf2), (wu1s, wu1), (wu2s, wu2), (w1n, w1), (a1s, a1),
                    (wfT, wfcT), (ahs, ah), (aes, ae), (weTs, weT))]
                loads += [(t[:], b.to_broadcast([P, D])) for t, b in ((b0s, b0), (b1s, bias1), (b2s, bias2), (bf2s, bf2))]
                loads += [(t[:], b) for t, b in ((bf1s, bf1), (bu1s, bu1), (bu2s, bu2), (gms, gamma), (bts, beta))]
                NL = 16 * len(loads)
                fills = [(t[NP:NP + P, :], zero[:, 0:D]) for t in A]
                for c0 in range(0, C, 56):
                    n = min(56, C - c0)
                    fills.append((nodes(S)[:, c0:c0 + n, :], zero[:].rearrange("p (c d) -> p c d", c=1).to_broadcast([P, n, SW])))

                with nc.Block() as block:
                    @block.sync
                    def _(e):
                        for to, frm in loads:
                            e.dma_start(to, frm).then_inc(loaded, 16)
                        e.wait_ge(zeroed, 1)
                        for to, frm in fills:
                            e.dma_start(to, frm).then_inc(filled, 16)

                    @block.gpsimd
                    def _(e):
                        e.memset(zero[:], 0.0).then_inc(zeroed, 1)
                        e.memset(ident[:], 0.0).then_inc(iotas, 1)
                        e.memset(before[:], 1.0).then_inc(iotas, 1)
                        e.memset(epsc[:], EPS).then_inc(iotas, 1)
                        e.iota(cols[:], pattern=[[1, C]], base=0, channel_multiplier=0, allow_small_or_imprecise_dtypes=True).then_inc(iotas, 1)
                        e.iota(rows0[:], pattern=[[1, P]], base=0, channel_multiplier=0, allow_small_or_imprecise_dtypes=True).then_inc(iotas, 1)
                        e.iota(pcol[:], pattern=[[0, 1]], base=0, channel_multiplier=1, allow_small_or_imprecise_dtypes=True).then_inc(iotas, 1)
                        e.iota(trash[:], pattern=[[0, 1]], base=NP, channel_multiplier=1, allow_small_or_imprecise_dtypes=True).then_inc(iotas, 1)
                        e.memset(earlier[:], 1.0).then_inc(iotas, 1)
                        e.wait_ge(iotas, 8)
                        e.affine_select(out=ident[:], in_=ident[:], compare_op=ALU.not_equal, fill=1.0, base=0,
                                        pattern=[[-1, P]], channel_multiplier=1).then_inc(iotas, 1)
                        e.affine_select(out=before[:], in_=before[:], compare_op=ALU.is_gt, fill=0.0, base=0,
                                        pattern=[[1, P]], channel_multiplier=-1).then_inc(iotas, 1)
                        e.affine_select(out=earlier[:], in_=earlier[:], compare_op=ALU.is_gt, fill=0.0, base=0,
                                        pattern=[[-1, P]], channel_multiplier=1).then_inc(iotas, 1)

                    @block.vector
                    def _(e):
                        n = [0]

                        def link(ins):
                            n[0] += 1
                            ins.then_inc(prep, 1)
                            e.wait_ge(prep, n[0])

                        e.wait_ge(loaded, NL)
                        e.wait_ge(iotas, 11)
                        link(e.tensor_copy(src_f[:], src_i[:]))
                        link(e.tensor_copy(dst_f[:], dst_i[:]))
                        link(e.tensor_copy(notl[:], next_i[:]))
                        link(e.memset(same[:, 0:1], 0.0))
                        link(e.tensor_tensor(same[:, 1:C], dst_f[:, 1:C], dst_f[:, 0:C - 1], ALU.is_equal))
                        link(e.tensor_tensor(islast[:], dst_f[:], notl[:], ALU.is_lt))
                        link(e.tensor_scalar(pen[:], same[:], -1.0, -NONE, ALU.add, ALU.mult))
                        link(e.tensor_scalar(notl[:], dst_f[:], -OUT, None, ALU.add))
                        link(e.tensor_tensor(notl[:], notl[:], islast[:], ALU.mult))
                        link(e.tensor_scalar(scat_i[:], notl[:], OUT, None, ALU.add))
                        link(e.tensor_reduce(any_last[:], islast[:], AX, ALU.max))
                        link(e.tensor_copy(firstf[:], dst_f[:, 0:1]))
                        link(e.tensor_copy(lastf[:], dst_f[:, C - 1:C]))
                        link(e.tensor_scalar(pcol[:], firstf[:], -OUT, any_last[:], ALU.add, ALU.mult))
                        link(e.tensor_scalar(first_i[:], pcol[:], OUT, None, ALU.add))
                        link(e.tensor_scalar(srcmt[:], src_f[:], trash[:], None, ALU.subtract))
                        e.wait_ge(tr, 1)
                        link(e.tensor_scalar(chain[:], psT[:], lastf[:], None, ALU.is_equal))
                        link(e.tensor_tensor(chain[:], chain[:], before[:], ALU.mult))
                        e.wait_ge(tr, 2)
                        link(e.tensor_copy(chainT[:], psT[:]))
                        link(e.tensor_scalar(penT[:], chainT[:], -1.0, -NONE, ALU.add, ALU.mult))
                        e.wait_ge(folds, 1)
                        link(e.tensor_copy(w1s[:, :, D:DW], psF[:]))
                        link(e.tensor_copy(w2s[:, :, D:DW], psG[:]))
                        link(e.tensor_copy(fes[:], psE[0:fes.shape[0], 0:H]))
                        link(e.tensor_scalar(part_i[:], dst_f[:], 1.0 / C, None, ALU.mult))
                        link(e.tensor_copy(part[:], part_i[:]))
                        link(e.scalar_tensor_tensor(col[:], part[:], -float(C), dst_f[:], ALU.mult, ALU.add))
                        link(e.tensor_scalar(over[:], col[:], 0.0, None, ALU.is_lt))
                        link(e.tensor_tensor(part[:], part[:], over[:], ALU.subtract))
                        link(e.scalar_tensor_tensor(col[:], over[:], float(C), col[:], ALU.mult, ALU.add))
                        link(e.tensor_scalar(over[:], col[:], float(C), None, ALU.is_ge))
                        link(e.tensor_tensor(part[:], part[:], over[:], ALU.add))
                        link(e.scalar_tensor_tensor(col[:], over[:], -float(C), col[:], ALU.mult, ALU.add))

                    @block.tensor
                    def _(e):
                        e.wait_ge(prep, 13)
                        e.wait_ge(iotas, 11)
                        e.transpose(psT[:], firstf[:].to_broadcast([P, P]), ident[:]).then_inc(tr, 1)
                        e.wait_ge(prep, 18)
                        e.transpose(psT[:], chain[:], ident[:]).then_inc(tr, 1)
                        for m in range(K):
                            for k in range(K):
                                e.matmul(psF[:, m, :], w1n[:, k, m * P:(m + 1) * P], a1s[:, k, :], start=k == 0, stop=k == K - 1)
                            for k in range(K):
                                e.matmul(psG[:, m, :], wfT[:, k, m * P:(m + 1) * P], ahs[:, k, :], start=k == 0, stop=k == K - 1)
                        for k in range(K):
                            mm = e.matmul(psE[0:weTs.shape[2], 0:H], weTs[:, k, :], aes[:, k, :], start=k == 0, stop=k == K - 1)
                        mm.then_inc(folds, 1)

                with nc.Block() as block:
                    NS = 4
                    R = C // NS
                    hots, taken = stage_of("hots", NS), stage_of("taken", NS)

                    @block.sync
                    def _(e):
                        e.wait_ge(filled, 16 * len(fills))

                    @block.vector
                    def _(e):
                        def one_hot(i, s):
                            c = bass.ds(i * NS + s, 1)
                            hold(e, *done(taken, i, s, NS))
                            e.tensor_scalar(hot[:, s, :], rows0[:], part[:, c], w_sb[:, c], ALU.is_equal, ALU.mult)
                            e.tensor_scalar(hotc[:, s, :], cols[:], col[:, c], None, ALU.is_equal).then_inc(signal(hots, s), 1)

                        pipelined(e, R, NS, [(one_hot, 0)])

                    @block.tensor
                    def _(e):
                        def both(i, first, last):
                            for s in range(NS):
                                hold(e, *done(hots, i, s))
                                e.matmul(psDeg[:, 0:C], hot[:, s, :], hotc[:, s, :], start=first and s == 0, stop=last and s == NS - 1)\
                                    .then_inc(signal(taken, s), 1)

                        both(0, True, False)
                        with e.Fori(1, R - 1) as i:
                            both(i, False, False)
                        both(R - 1, False, True)

                with nc.Block() as block:
                    deg, ok, dsq = tmp("deg", [P, C]), tmp("ok", [P, C]), tmp("dsq", [P, C])
                    clamped, sq = sem("clamped"), sem("sq")

                    @block.vector
                    def _(e):
                        n = [0]

                        def link(ins):
                            n[0] += 1
                            ins.then_inc(clamped, 1)
                            e.wait_ge(clamped, n[0])

                        link(e.tensor_scalar(deg[:], psDeg[:, 0:C], 1.0, None, ALU.add))
                        link(e.tensor_scalar(ok[:], deg[:], 0.0, None, ALU.is_gt))
                        link(e.tensor_scalar(deg[:], deg[:], 1e-12, None, ALU.max))
                        e.wait_ge(sq, 1)
                        link(e.reciprocal(dsq[:], dsq[:]))
                        link(e.tensor_tensor(dinv[:], dsq[:], ok[:], ALU.mult))
                        link(e.scalar_tensor_tensor(ca[:], dinv[:], 0.5, dinv[:], ALU.mult, ALU.mult))
                        link(e.scalar_tensor_tensor(cb[:], ca[:], 0.5, dinv[:], ALU.add, ALU.mult))

                    @block.scalar
                    def _(e):
                        e.wait_ge(clamped, 3)
                        e.activation(dsq[:], deg[:], ACT.Sqrt).then_inc(sq, 1)

        def hop_table(first):
            with ExitStack() as ctx:
                G, NS = 2, 7
                R = C // (G * NS)
                tiles = lambda n, w: [ctx.enter_context(sbuf(f"{n}{s}", [P, G, w], F32)) for s in range(NS)]
                xt, st = tiles("xt", D), tiles("st", SW)
                loaded = stage_of("loaded", NS, 1 if first else 2)
                stored = stage_of("stored", NS, 1)
                scaled, ready = stage_of("scaled", NS), stage_of("ready", NS)
                
                with nc.Block() as block:
                    @block.sync
                    def _(e):

                        def load(i, s):
                            c = bass.ds(i * (G * NS) + s * G, G)
                            hold(e, *done(stored, i, s, NS))
                            e.dma_start(xt[s][:], x[:, c, :]).then_inc(signal(loaded, s), 16)
                            if not first:
                                e.dma_start(st[s][:], nodes(S)[:, c, :]).then_inc(signal(loaded, s), 16)

                        def store(i, s):
                            hold(e, *done(ready, i, s))
                            e.dma_start(nodes(Y)[:, bass.ds(i * (G * NS) + s * G, G), :], xt[s][:]).then_inc(signal(stored, s), 16)

                        pipelined(e, R, NS, [(load, 0), (store, 3)])
                        for sem, value in total(stored, R):
                            e.wait_ge(sem, value)

                    @block.scalar
                    def _(e):
                        def scale(i, s):
                            hold(e, *done(loaded, i, s))
                            for k in range(G):
                                c = bass.ds(i * (G * NS) + (s * G + k), 1)
                                if first and k % 2 == 0:
                                    ins = e.activation(xt[s][:, k, :], xt[s][:, k, :], ACT.Copy, scale=dinv[:, c])
                                elif not first:
                                    ins = e.activation(st[s][:, k, 0:D], st[s][:, k, 0:D], ACT.Copy, scale=ca[:, c])
                            ins.then_inc(signal(scaled, s), 1)

                        pipelined(e, R, NS, [(scale, 0)])

                    @block.vector
                    def _(e):
                        def add(i, s):
                            hold(e, *done(loaded, i, s))
                            hold(e, *done(scaled, i, s))
                            for k in range(G):
                                c = bass.ds(i * (G * NS) + (s * G + k), 1)
                                if first and k % 2 == 1:
                                    ins = e.tensor_scalar(xt[s][:, k, :], xt[s][:, k, :], dinv[:, c], None, ALU.mult)
                                elif not first:
                                    ins = e.scalar_tensor_tensor(xt[s][:, k, :], xt[s][:, k, :], cb[:, c], st[s][:, k, 0:D], ALU.mult, ALU.add)
                            ins.then_inc(signal(ready, s), 1)

                        pipelined(e, R, NS, [(add, 0)])

        def hop_edges(cleared_table):
            with ExitStack() as ctx:
                G, NS, LAG = 2, 4, 3
                R = C // (G * NS)
                tiles = lambda n, w, dt=F32: [ctx.enter_context(sbuf(f"{n}{s}", [P, G, w], dt)) for s in range(NS)]
                rows, sums = tiles("rows", D), tiles("sums", SW)
                gi, si = tiles("gi", 1, I32), tiles("si", 1, I32)
                placed = stage_of("placed", NS, 1)
                indexed, gathered, scattered = (stage_of("indexed", NS, 1), stage_of("gathered", NS, G),
                                                stage_of("scattered", NS, G))
                weighted, summed = stage_of("weighted", NS), stage_of("summed", NS)
                steps = semaphore("steps")
                started, filled = semaphore("started"), semaphore("filled")
                with nc.Block() as block:
                    @block.sync
                    def _(e):

                        def stage(i, s):
                            c = bass.ds(i * (G * NS) + s * G, G)
                            hold(e, *done(gathered, i, s, NS))
                            e.dma_start(gi[s][:, :, 0], src_i[:, c]).then_inc(signal(indexed, s), 16)
                            e.dma_start(nodes(cleared_table)[:, c, :], zero[:, 0:D].rearrange("p (g d) -> p g d", g=1).to_broadcast([P, G, D]))\
                                .then_inc(filled, 16)

                        def stage_scatter(i, s):
                            c = bass.ds(i * (G * NS) + s * G, G)
                            hold(e, *done(scattered, i, s, NS))
                            e.dma_start(si[s][:, :, 0], scat_i[:, c]).then_inc(signal(placed, s), 16)

                        pipelined(e, R, NS, [(stage, 0), (stage_scatter, 2)])
                        e.wait_ge(filled, 16 * R * NS)

                    @block.gpsimd
                    def _(e):
                        def gather(i, s):
                            hold(e, *done(indexed, i, s))
                            hold(e, *done(summed, i, s, NS))
                            for k in range(G):
                                e.indirect_dma_start(rows[s][:, k, :], None, Y, bass.IndirectOffsetOnAxis(ap=gi[s][:, k, :], axis=0))\
                                    .then_inc(signal(gathered, s), 16)

                        def scatter(i, s):
                            hold(e, *done(summed, i, s))
                            hold(e, *done(placed, i, s))
                            for k in range(G):
                                e.indirect_dma_start(S, bass.IndirectOffsetOnAxis(ap=si[s][:, k, :], axis=0), sums[s][:, k, :], None,
                                                     bounds_check=NP - 1, oob_is_err=False).then_inc(signal(scattered, s), 16)

                        pipelined(e, R, NS, [(gather, 0), (scatter, LAG)])
                        for sem, value in total(scattered, R):
                            e.wait_ge(sem, value)

                    @block.scalar
                    def _(e):
                        def weigh(i, s):
                            hold(e, *done(gathered, i, s))
                            for k in range(G):
                                ins = e.activation(rows[s][:, k, :], rows[s][:, k, :], ACT.Copy, scale=w_sb[:, bass.ds(i * (G * NS) + (s * G + k), 1)])
                            ins.then_inc(signal(weighted, s), 1)

                        pipelined(e, R, NS, [(weigh, 0)])

                    @block.vector
                    def _(e):
                        for s in range(NS):
                            ins = e.memset(sums[s][:], 0.0)
                        ins.then_inc(started, 1)
                        e.wait_ge(started, 1)

                        def add(i, s):
                            hold(e, *done(weighted, i, s))
                            hold(e, *done(scattered, i, s, NS))
                            for k in range(G):
                                last = sums[s][:, k - 1, 0:D] if k else sums[(s - 1) % NS][:, G - 1, 0:D]
                                ins = e.scalar_tensor_tensor(sums[s][:, k, 0:D], last, same[:, bass.ds(i * (G * NS) + (s * G + k), 1)],
                                                             rows[s][:, k, :], ALU.mult, ALU.add)
                                if k < G - 1:
                                    ins.then_inc(steps, 1)
                                    e.wait_ge(steps, i * NS * (G - 1) + (s * (G - 1) + k + 1))
                            ins.then_inc(signal(summed, s), 1)
                            hold(e, *done(summed, i, s))

                        pipelined(e, R, NS, [(add, 0)])
                with nc.Block() as block:
                    own, ps = ctx.enter_context(sbuf("own", [P, SW], F32)), ctx.enter_context(psum("psC", [P, D], F32))
                    fetched, cleared, carried, fixed, put = [semaphore(n) for n in (
                        "fetched", "cleared", "carried", "fixed", "put")]

                    @block.vector
                    def _(e):
                        e.memset(own[:], 0.0).then_inc(cleared, 1)
                        e.wait_ge(carried, 1)
                        e.wait_ge(fetched, 16)
                        e.tensor_tensor(own[:, 0:D], own[:, 0:D], ps[:], ALU.add).then_inc(fixed, 1)

                    @block.tensor
                    def _(e):
                        e.matmul(ps[:], chain[:], sums[NS - 1][:, G - 1, 0:D], start=True, stop=True).then_inc(carried, 1)

                    @block.gpsimd
                    def _(e):
                        at = bass.IndirectOffsetOnAxis(ap=first_i[:], axis=0)
                        e.wait_ge(cleared, 1)
                        e.indirect_dma_start(own[:], None, S, at, bounds_check=NP - 1, oob_is_err=False).then_inc(fetched, 16)
                        e.wait_ge(fixed, 1)
                        e.indirect_dma_start(S, at, own[:], None, bounds_check=NP - 1, oob_is_err=False).then_inc(put, 16)
                        e.wait_ge(put, 16)

        def norm_of(ctx, NS, G, z, y):
            t = lambda n, w: [ctx.enter_context(sbuf(f"{n}{s}", [P, G, w], F32)) for s in range(NS)]
            row_stats, mean_var, sd, rsd, shift = t("row_stats", 6), t("mean_var", 2), t("sd", 1), t("rsd", 1), t("shift", 1)
            measured, rooted, inverted, folded, recip = (
                stage_of(n, NS) for n in ("measured", "rooted", "inverted", "folded", "recip"))

            def ln_measure(e, i, s):
                for k in range(G):
                    ins = e.bn_stats(row_stats[s][:, k, :], z[s][:, k, :])
                ins.then_inc(signal(folded, s), 1)
                hold(e, *done(folded, i, s))
                e.sem_inc(marks, 1)
                for k in range(G):
                    ins = e.bn_aggr(mean_var[s][:, k, :], row_stats[s][:, k, :])
                ins.then_inc(signal(measured, s), 1)

            def ln_root(e, i, s):
                hold(e, *done(measured, i, s))
                e.activation(sd[s][:, :, 0], mean_var[s][:, :, 1], ACT.Sqrt, bias=epsc[:]).then_inc(signal(rooted, s), 1)

            def ln_invert(e, i, s):
                hold(e, *done(rooted, i, s))
                e.reciprocal(rsd[s][:, :, 0], sd[s][:, :, 0]).then_inc(signal(recip, s), 1)
                hold(e, *done(recip, i, s))
                e.scalar_tensor_tensor(shift[s][:, :, 0], mean_var[s][:, :, 0], -1.0, rsd[s][:, :, 0], ALU.mult, ALU.mult)\
                    .then_inc(signal(inverted, s), 1)

            def ln_apply(e, i, s, finished):
                hold(e, *done(inverted, i, s))
                for k in range(G):
                    ins = e.activation(y[s][:, k, :], z[s][:, k, :], ACT.Identity, bias=shift[s][:, k, :], scale=rsd[s][:, k, :])
                ins.then_inc(signal(finished, s), 1)

            return ln_measure, ln_root, ln_invert, ln_apply

        def layer_nodes(layer):
            xin = x if layer == 0 else nodes((X1, X2)[layer - 1])
            xout = nodes((X1, X2, X3)[layer])
            table = layer < 2
            with ExitStack() as ctx:
                G, NS = 2, 4
                R = C // (G * NS)
                tiles = lambda n, w: [ctx.enter_context(sbuf(f"{n}{s}", [P, G, w], F32)) for s in range(NS)]
                xt, st, xb, z, xo = tiles("xt", D), tiles("st", SW), tiles("xb", D), tiles("z", D), tiles("xo", D)
                yt, rT = (tiles("yt", D), tiles("rT", D)) if layer == 0 else (None, None)
                den = tiles("den", H) if layer else None
                xT, tt = (tiles("xT", D), tiles("tt", TW)) if table else (None, None)
                bank = lambda n, w: ctx.enter_context(psum(n, [P, w], F32))
                psR = [bank(f"psR{j}", G * D) for j in range(2)] if layer == 0 else None
                psZ = [bank(f"psZ{j}", G * D) for j in range(2)] if layer == 0 else None
                psX = [bank(f"psX{j}", G * D) for j in range(2)] if table else None
                psV = [bank(f"psV{j}", 512) for j in range(2)] if table else None
                weights = (w1s, w2s, None)[layer]
                NL = 3 if layer == 0 else 2
                names = "biased mixed rectified turned copied product summed normed turnedx copiedx tabled evened".split()
                st_ = {n: stage_of(n, NS) for n in names}
                loaded, stored = stage_of("loaded", NS, NL), stage_of("stored", NS, 1)
                stored_t = stage_of("stored_t", NS, 1 + layer % 2)
                steps, ones = semaphore("steps"), semaphore("ones")
                TURN, PRODUCT, ADD = 1, 2, 3 if layer == 0 else 1
                APPLY = ADD + 1
                TURNX, TABLE = APPLY + 1, APPLY + 2
                ln_measure, ln_root, ln_invert, ln_apply = norm_of(ctx, NS, G, z, xo)
                with nc.Block() as block:
                    @block.sync
                    def _(e):

                        def load(i, s):
                            c = bass.ds(i * (G * NS) + s * G, G)
                            hold(e, *done(st_["mixed"], i, s, NS))
                            hold(e, *done(st_["biased"], i, s, NS))
                            e.dma_start(xt[s][:], xin[:, c, :]).then_inc(signal(loaded, s), 16)
                            e.dma_start(st[s][:], nodes(S)[:, c, :]).then_inc(signal(loaded, s), 16)
                            if layer == 0:
                                hold(e, *done(st_["turned"], i, s, NS))
                                e.dma_start(yt[s][:], nodes(Y)[:, c, :]).then_inc(signal(loaded, s), 16)

                        def store(i, s):
                            c = bass.ds(i * (G * NS) + s * G, G)
                            hold(e, *done(st_["normed"], i, s))
                            e.dma_start(xout[:, c, :], xo[s][:]).then_inc(signal(stored, s), 16)

                        def store_table(i, s):
                            c = bass.ds(i * (G * NS) + s * G, G)
                            hold(e, *done(st_["evened"], i, s))
                            if layer == 0:
                                e.dma_start(nodes(T1)[:, c, :], tt[s][:]).then_inc(signal(stored_t, s), 16)
                            else:
                                e.dma_start(nodes(T2)[:, c, :], tt[s][:, :, 0:SW]).then_inc(signal(stored_t, s), 16)
                                e.dma_start(nodes(ET)[:, c, :], tt[s][:, :, SW:TW]).then_inc(signal(stored_t, s), 16)

                        pipelined(e, R, NS, [(load, 0), (store, APPLY + 2)] + ([(store_table, TABLE + 2)] if table else []))
                        for sem, value in total(stored, R) + (total(stored_t, R) if table else []):
                            e.wait_ge(sem, value)

                    @block.gpsimd
                    def _(e):
                        bias = (b0s, b1s, b2s)[layer]

                        def add_bias(i, s):
                            hold(e, *done(loaded, i, s))
                            hold(e, *done(st_["summed"], i, s, NS))
                            e.tensor_tensor(xb[s][:], xt[s][:], bias[:].rearrange("p (g d) -> p g d", g=1).to_broadcast([P, G, D]), ALU.add)\
                                .then_inc(signal(st_["biased"], s), 1)

                        pipelined(e, R, NS, [(add_bias, 0)])

                    @block.vector
                    def _(e):
                        if table:
                            for s in range(NS):
                                ins = e.memset(tt[s][:, :, 0:VW].rearrange("p g (h w) -> p g h w", h=H)[:, :, :, HD:HW], 1.0)
                            ins.then_inc(ones, 1)

                        def mix(i, s):
                            hold(e, *done(loaded, i, s))
                            if layer == 0:
                                e.tensor_tensor(yt[s][:], yt[s][:], st[s][:, :, 0:D], ALU.add).then_inc(steps, 1)
                                e.wait_ge(steps, i * NS + (s + 1))
                                for k in range(G):
                                    ins = e.scalar_tensor_tensor(yt[s][:, k, :], yt[s][:, k, :], dinv[:, bass.ds(i * (G * NS) + (s * G + k), 1)],
                                                                 xt[s][:, k, :], ALU.mult, ALU.add)
                                ins.then_inc(signal(st_["mixed"], s), 1)
                                return
                            v = st[s][:, :, 0:VW].rearrange("p g (h w) -> p g h w", h=H)
                            e.tensor_scalar(den[s][:], v[:, :, :, HD], 1e-10, None, ALU.max).then_inc(steps, 1)
                            e.wait_ge(steps, i * (2 * NS) + (2 * s + 1))
                            e.reciprocal(den[s][:], den[s][:]).then_inc(steps, 1)
                            e.wait_ge(steps, i * (2 * NS) + (2 * s + 2))
                            hold(e, *done(st_["normed"], i, s, NS))
                            e.tensor_tensor(z[s][:].rearrange("p g (h d) -> p g h d", h=H), v[:, :, :, 0:HD],
                                            den[s][:].rearrange("p g (h w) -> p g h w", w=1).to_broadcast([P, G, H, HD]), ALU.mult)\
                                .then_inc(signal(st_["mixed"], s), 1)

                        def add(i, s):
                            if layer == 0:
                                hold(e, *done(st_["normed"], i, s, NS))
                                hold(e, *done(st_["product"], i, s))
                                more = psZ[s % 2][:].rearrange("p (g d) -> p g d", g=G)
                            else:
                                hold(e, *done(st_["mixed"], i, s))
                                more = z[s][:]
                            hold(e, *done(st_["biased"], i, s))
                            e.tensor_tensor(z[s][:], more, xb[s][:], ALU.add).then_inc(signal(st_["summed"], s), 1)
                            hold(e, *done(st_["summed"], i, s))
                            ln_measure(e, i, s)

                        stages = [(mix, 0), (add, ADD), (lambda i, s: ln_invert(e, i, s), APPLY)]

                        pipelined(e, R, NS, stages)

                    @block.scalar
                    def _(e):
                        def rectify(i, s):
                            hold(e, *done(st_["mixed"], i, s))
                            e.activation(yt[s][:], yt[s][:], ACT.Relu, scale=0.5).then_inc(signal(st_["rectified"], s), 1)

                        def copy_turned(i, s):
                            hold(e, *done(st_["turned"], i, s))
                            hold(e, *done(st_["product"], i, s, NS))
                            e.copy(rT[s][:].rearrange("p g d -> p (g d)"), psR[s % 2][:]).then_inc(signal(st_["copied"], s), 1)

                        def copy_turned_x(i, s):
                            hold(e, *done(st_["turnedx"], i, s))
                            hold(e, *done(st_["tabled"], i, s, NS))
                            e.copy(xT[s][:].rearrange("p g d -> p (g d)"), psX[s % 2][:]).then_inc(signal(st_["copiedx"], s), 1)

                        def tabled_rows(i, s):
                            hold(e, *done(st_["tabled"], i, s))
                            hold(e, *done(stored_t, i, s, NS))
                            for k in range(G):
                                e.copy(tt[s][:, k, 0:VW].rearrange("p (h w) -> p h w", h=H)[:, :, 0:HD],
                                       psV[k][:, 0:D].rearrange("p (h d) -> p h d", h=H))
                                ins = e.copy(tt[s][:, k, VW:TW], psV[k][:, D:DW])
                            ins.then_inc(signal(st_["evened"], s), 1)

                        def apply(i, s):
                            hold(e, *done(stored, i, s, NS))
                            if table:
                                hold(e, *done(st_["turnedx"], i, s, NS))
                            ln_apply(e, i, s, st_["normed"])

                        stages = [(rectify, 0), (copy_turned, TURN)] if layer == 0 else []
                        stages += [(lambda i, s: ln_root(e, i, s), ADD), (apply, APPLY)]
                        if table:
                            stages += [(copy_turned_x, TURNX), (tabled_rows, TABLE)]
                            e.wait_ge(ones, 1)
                        pipelined(e, R, NS, stages)

                    @block.tensor
                    def _(e):
                        def turn(i, s, a, ps, finished):
                            for k in range(G):
                                for m in range(K):
                                    mm = e.transpose(ps[:, (k * K + m) * P:(k * K + m + 1) * P], a[:, k, m * P:(m + 1) * P], ident[:])
                            mm.then_inc(signal(finished, s), 1)

                        def turn_r(i, s):
                            hold(e, *done(st_["rectified"], i, s))
                            hold(e, *done(st_["copied"], i, s, 2))
                            turn(i, s, yt[s], psR[s % 2], st_["turned"])

                        def product(i, s):
                            hold(e, *done(st_["copied"], i, s))
                            hold(e, *done(st_["summed"], i, s, 2))
                            for k in range(G):
                                for m in range(K):
                                    mm = e.matmul(psZ[s % 2][:, k * D:(k + 1) * D], rT[s][:, k, m * P:(m + 1) * P], w0s[:, m, :],
                                                  start=m == 0, stop=m == K - 1)
                            mm.then_inc(signal(st_["product"], s), 1)

                        def turn_x(i, s):
                            hold(e, *done(st_["normed"], i, s))
                            hold(e, *done(st_["copiedx"], i, s, 2))
                            turn(i, s, xo[s], psX[s % 2], st_["turnedx"])

                        def tabulate(i, s):
                            hold(e, *done(st_["copiedx"], i, s))
                            hold(e, *done(st_["evened"], i, s, 1))
                            for k in range(G):
                                for m in range(K):
                                    mm = e.matmul(psV[k][:, 0:DW], xT[s][:, k, m * P:(m + 1) * P], weights[:, m, :],
                                                  start=m == 0, stop=m == K - 1)
                            mm.then_inc(signal(st_["tabled"], s), 1)

                        stages = [(turn_r, TURN), (product, PRODUCT)] if layer == 0 else []
                        if table:
                            stages += [(turn_x, TURNX), (tabulate, TABLE)]
                        if stages:
                            pipelined(e, R, NS, stages)

        def attention_edges(layer):
            with ExitStack() as ctx:
                G, NS, LAG = 2, 4, 3
                R = C // (G * NS)
                tiles = lambda n, w, dt=F32, p=P: [ctx.enter_context(sbuf(f"{n}{s}", [p, G, w], dt)) for s in range(NS)]
                table, dtable = (T1, T1) if layer == 1 else (T2, ET)
                W, WD = table.shape[1], dtable.shape[1]
                rows, rowsd, sums = tiles("rows", W), tiles("rowsd", WD), tiles("sums", SW)
                gi, gd, si = tiles("gi", 1, I32), tiles("gd", 1, I32), tiles("si", 1, I32)
                KA = 4 if layer == 1 else attr64T.shape[0]
                attr = tiles("attr", P, F32, KA)
                enc = tiles("enc", D) if layer == 1 else None
                lg, dot, mp, diff, ex = tiles("lg", H), tiles("dot", H), tiles("mp", H), tiles("diff", 2 * H), tiles("ex", 2 * H)
                EW = D if layer == 1 else H
                psE = [ctx.enter_context(psum(f"psE{j}", [P, 512], F32)) for j in range(2)]
                placed = stage_of("placed", NS, 1)
                indexed, gathered, scattered, attred = (stage_of("indexed", NS, 2), stage_of("gathered", NS, 2 * G),
                                                        stage_of("scattered", NS, G), stage_of("attred", NS, 1))
                encoded, rectified, scored, exped, summed = (stage_of(n, NS) for n in ("encoded", "rectified", "scored", "exped", "summed"))
                steps, bsteps, started = [semaphore(n) for n in ("steps", "bsteps", "started")]
                heads = lambda a: a.rearrange("p (h w) -> p h w", h=H)
                with nc.Block() as block:
                    @block.sync
                    def _(e):
                        e.wait_ge(started, 1)
                        edge_attr = attr3T if layer == 1 else attr64T

                        def stage(i, s):
                            c = bass.ds(i * (G * NS) + s * G, G)
                            hold(e, *done(encoded, i, s, NS))
                            e.dma_start(attr[s][0:edge_attr.shape[0]], edge_attr[:, c, :]).then_inc(signal(attred, s), 16)
                            hold(e, *done(gathered, i, s, NS))
                            e.dma_start(gi[s][:, :, 0], src_i[:, c]).then_inc(signal(indexed, s), 16)
                            e.dma_start(gd[s][:, :, 0], dst_i[:, c]).then_inc(signal(indexed, s), 16)

                        def stage_scatter(i, s):
                            c = bass.ds(i * (G * NS) + s * G, G)
                            hold(e, *done(scattered, i, s, NS))
                            e.dma_start(si[s][:, :, 0], scat_i[:, c]).then_inc(signal(placed, s), 16)

                        pipelined(e, R, NS, [(stage, 0), (stage_scatter, 2)])

                    @block.gpsimd
                    def _(e):
                        def gather(i, s):
                            hold(e, *done(indexed, i, s))
                            hold(e, *done(summed, i, s, NS))
                            for k in range(G):
                                e.indirect_dma_start(rowsd[s][:, k, :], None, dtable, bass.IndirectOffsetOnAxis(ap=gd[s][:, k, :], axis=0))\
                                    .then_inc(signal(gathered, s), 16)
                                e.indirect_dma_start(rows[s][:, k, :], None, table, bass.IndirectOffsetOnAxis(ap=gi[s][:, k, :], axis=0))\
                                    .then_inc(signal(gathered, s), 16)

                        def scatter(i, s):
                            hold(e, *done(summed, i, s))
                            hold(e, *done(placed, i, s))
                            for k in range(G):
                                e.indirect_dma_start(S, bass.IndirectOffsetOnAxis(ap=si[s][:, k, :], axis=0), sums[s][:, k, :], None,
                                                     bounds_check=NP - 1, oob_is_err=False).then_inc(signal(scattered, s), 16)

                        pipelined(e, R, NS, [(gather, 0), (scatter, LAG)])
                        for sem, value in total(scattered, R):
                            e.wait_ge(sem, value)

                    @block.tensor
                    def _(e):
                        weights = encs if layer == 1 else fes

                        def encode(i, s):
                            hold(e, *done(attred, i, s))
                            if layer == 1:
                                hold(e, *done(rectified, i, s, 2))
                            else:
                                hold(e, *done(scored, i, s, 2))
                            for k in range(G):
                                mm = e.matmul(psE[s % 2][:, k * EW:(k + 1) * EW], attr[s][:, k, :], weights[:], start=True, stop=True)
                            mm.then_inc(signal(encoded, s), 1)

                        pipelined(e, R, NS, [(encode, 0)])

                    @block.scalar
                    def _(e):
                        def rectify(i, s):
                            hold(e, *done(encoded, i, s))
                            hold(e, *done(scored, i, s, NS))
                            e.activation(enc[s][:].rearrange("p g d -> p (g d)"), psE[s % 2][:], ACT.Relu).then_inc(signal(rectified, s), 1)

                        def exponentials(i, s):
                            hold(e, *done(scored, i, s))
                            hold(e, *done(summed, i, s, NS))
                            e.activation(ex[s][:], diff[s][:], ACT.Exp).then_inc(signal(exped, s), 1)

                        pipelined(e, R, NS, ([(rectify, 0)] if layer == 1 else []) + [(exponentials, 0)])

                    @block.vector
                    def _(e):
                        for s in range(NS):
                            ins = e.memset(sums[s][:], 0.0)
                            if layer == 1:
                                ins = e.memset(attr[s][:], 1.0)
                        ins.then_inc(started, 1)
                        e.wait_ge(started, 1)
                        SC = 8 if layer == 1 else 6

                        def score(i, s):
                            n = [0]

                            def link(ins):
                                n[0] += 1
                                ins.then_inc(steps, 1)
                                e.wait_ge(steps, i * (NS * SC) + (s * SC + n[0]))

                            hold(e, *done(gathered, i, s))
                            hold(e, *done(scattered, i, s, NS))
                            hold(e, *done(summed, i, s, NS))
                            hold(e, *done(exped, i, s, NS))
                            if layer == 1:
                                hd = rowsd[s][:, :, 0:VW].rearrange("p g (h w) -> p g h w", h=H)[:, :, :, 0:HD]
                                e4 = enc[s][:].rearrange("p g (h d) -> p g h d", h=H)
                                hold(e, *done(rectified, i, s))
                                link(e.tensor_tensor(e4, e4, hd, ALU.mult))
                                link(e.tensor_reduce(dot[s][:], e4, AX, ALU.add))
                                link(e.tensor_tensor(dot[s][:], dot[s][:], rows[s][:, :, VW:SW], ALU.add))
                                link(e.tensor_tensor(dot[s][:], dot[s][:], rowsd[s][:, :, SW:TW], ALU.add))
                            else:
                                hold(e, *done(encoded, i, s))
                                link(e.tensor_tensor(dot[s][:], rows[s][:, :, VW:SW], rowsd[s][:], ALU.add))
                                link(e.tensor_tensor(dot[s][:], dot[s][:], psE[s % 2][:, 0:G * H].rearrange("p (g h) -> p g h", g=G), ALU.add))
                            link(e.scalar_tensor_tensor(lg[s][:], dot[s][:], 0.2, dot[s][:], ALU.mult, ALU.max))
                            for k in range(G):
                                pc = pen[:, bass.ds(i * (G * NS) + (s * G + k), 1)]
                                last = sums[s][:, k - 1, VW:SW] if k else sums[(s - 1) % NS][:, G - 1, VW:SW]
                                e.tensor_scalar(mp[s][:, k, :], last, pc, None, ALU.add)
                                link(e.scalar_tensor_tensor(sums[s][:, k, VW:SW], last, pc, lg[s][:, k, :], ALU.add, ALU.max))
                            link(e.tensor_tensor(diff[s][:, :, 0:H], mp[s][:], sums[s][:, :, VW:SW], ALU.subtract))
                            e.tensor_tensor(diff[s][:, :, H:2 * H], lg[s][:], sums[s][:, :, VW:SW], ALU.subtract).then_inc(signal(scored, s), 1)
                            assert n[0] == SC

                        def add(i, s):
                            hold(e, *done(exped, i, s))
                            wide = lambda a: a.rearrange("p g (h w) -> p g h w", w=1).to_broadcast([P, G, H, HW])
                            v = rows[s][:, :, 0:VW].rearrange("p g (h w) -> p g h w", h=H)
                            e.tensor_tensor(v, v, wide(ex[s][:, :, H:2 * H]), ALU.mult)
                            B = 2 * G - 1
                            n = 0
                            for k in range(G):
                                last = sums[s][:, k - 1, 0:VW] if k else sums[(s - 1) % NS][:, G - 1, 0:VW]
                                r = ex[s][:, k, 0:H].rearrange("p (h w) -> p h w", w=1).to_broadcast([P, H, HW])
                                n += 1
                                e.tensor_tensor(heads(sums[s][:, k, 0:VW]), heads(last), r, ALU.mult).then_inc(bsteps, 1)
                                e.wait_ge(bsteps, i * (NS * B) + (s * B + n))
                                ins = e.tensor_tensor(sums[s][:, k, 0:VW], sums[s][:, k, 0:VW], rows[s][:, k, 0:VW], ALU.add)
                                if k < G - 1:
                                    n += 1
                                    ins.then_inc(bsteps, 1)
                                    e.wait_ge(bsteps, i * (NS * B) + (s * B + n))
                            ins.then_inc(signal(summed, s), 1)
                            hold(e, *done(summed, i, s))

                        pipelined(e, R, NS, [(score, 0), (add, 1)])
                with nc.Block() as block:
                    end = sums[NS - 1][:, G - 1, :]
                    t = lambda n, sh: ctx.enter_context(sbuf(n, sh, F32))
                    own, mall, eT, mc, mn, r, dm = (t("own", [P, SW]), t("mall", [P, H, P]), t("eT", [P, H, P]), t("mc", [P, H]),
                                                    t("mn", [P, H]), t("r", [P, H]), t("dm", [P, H]))
                    psM = ctx.enter_context(psum("psM", [P, H, P], F32))
                    psC = ctx.enter_context(psum("psC", [P, 512], F32))
                    fetched, cleared, turned, fx, exd, put = [semaphore(n) for n in (
                        "fetched", "cleared", "fturned", "fx", "exd", "put")]

                    @block.gpsimd
                    def _(e):
                        at = bass.IndirectOffsetOnAxis(ap=first_i[:], axis=0)
                        e.wait_ge(cleared, 1)
                        e.indirect_dma_start(own[:], None, S, at, bounds_check=NP - 1, oob_is_err=False).then_inc(fetched, 16)
                        e.wait_ge(fx, 9)
                        e.indirect_dma_start(S, at, own[:], None, bounds_check=NP - 1, oob_is_err=False).then_inc(put, 16)
                        e.wait_ge(put, 16)

                    @block.tensor
                    def _(e):
                        for h in range(H):
                            mm = e.transpose(psM[:, h, :], end[:, VW + h:VW + h + 1].to_broadcast([P, P]), ident[:])
                        mm.then_inc(turned, 1)
                        e.wait_ge(exd, 1)
                        for h in range(H):
                            mm = e.transpose(psM[:, h, :], mall[:, h, :], ident[:])
                        mm.then_inc(turned, 1)
                        e.wait_ge(fx, 6)
                        for h in range(H):
                            mm = e.matmul(psC[:, h * HW:(h + 1) * HW], eT[:, h, :], end[:, h * HW:(h + 1) * HW], start=True, stop=True)
                        mm.then_inc(turned, 1)

                    @block.scalar
                    def _(e):
                        e.wait_ge(fx, 5)
                        e.activation(mall[:], mall[:], ACT.Exp).then_inc(exd, 1)
                        e.activation(r[:], dm[:], ACT.Exp).then_inc(exd, 1)

                    @block.vector
                    def _(e):
                        n = [0]

                        def link(ins):
                            n[0] += 1
                            ins.then_inc(fx, 1)
                            e.wait_ge(fx, n[0])

                        e.memset(own[:], 0.0).then_inc(cleared, 1)
                        e.wait_ge(turned, 1)
                        link(e.tensor_tensor(mall[:], psM[:], penT[:].rearrange("p (h q) -> p h q", h=1).to_broadcast([P, H, P]), ALU.add))
                        link(e.tensor_reduce(mc[:], mall[:], AX, ALU.max))
                        e.wait_ge(fetched, 16)
                        link(e.tensor_tensor(mn[:], mc[:], own[:, VW:SW], ALU.max))
                        link(e.tensor_tensor(dm[:], own[:, VW:SW], mn[:], ALU.subtract))
                        link(e.tensor_tensor(mall[:], mall[:], mn[:].rearrange("p (h q) -> p h q", q=1).to_broadcast([P, H, P]), ALU.subtract))
                        e.wait_ge(turned, 2)
                        link(e.tensor_copy(eT[:], psM[:]))
                        e.wait_ge(exd, 2)
                        link(e.tensor_tensor(heads(own[:, 0:VW]), heads(own[:, 0:VW]), r[:].rearrange("p (h w) -> p h w", w=1).to_broadcast([P, H, HW]), ALU.mult))
                        e.wait_ge(turned, 3)
                        link(e.tensor_tensor(own[:, 0:VW], own[:, 0:VW], psC[:, 0:VW], ALU.add))
                        link(e.tensor_copy(own[:, VW:SW], mn[:]))

        def filter_edges():
            with ExitStack() as ctx:
                G, NS, LAG = 2, 4, 3
                R = C // (G * NS)
                tiles = lambda n, w, dt=F32, p=P: [ctx.enter_context(sbuf(f"{n}{s}", [p, G, w], dt)) for s in range(NS)]
                NG = rbfT.shape[0]
                rbf = tiles("rbf", P, F32, NG)
                rows, comb, eq, low = tiles("rows", D), tiles("comb", D), tiles("eq", P), tiles("low", P)
                hid = [ctx.enter_context(sbuf(f"hid{s}", [P, K, G * P], F32)) for s in range(NS)]
                fl = tiles("fl", D)
                sc, cnt, gi, ai = tiles("sc", 1), tiles("cnt", 1), tiles("gi", 1, I32), tiles("ai", 1, I32)
                bank = lambda n: ctx.enter_context(psum(n, [P, 512], F32))
                psH, psI, psF, psM = [[bank(f"{n}{j}") for j in range(2)] for n in ("psH", "psI", "psF", "psM")]
                indexed, gathered, added, attred = (stage_of("indexed", NS, 1), stage_of("gathered", NS, G),
                                                    stage_of("added", NS, G), stage_of("attred", NS, 1))
                stages = [stage_of(n, NS) for n in (
                    "columned", "hidden", "sourced", "active", "filtered", "compared", "message", "joined", "copied")]
                columned, hidden, sourced, active, filtered, compared, message, joined, copied = stages
                steps, msteps = [semaphore(n) for n in ("steps", "msteps")]
                with nc.Block() as block:
                    @block.sync
                    def _(e):

                        def stage(i, s):
                            c = bass.ds(i * (G * NS) + s * G, G)
                            hold(e, *done(hidden, i, s, NS))
                            e.dma_start(rbf[s][:], rbfT[:, c, :]).then_inc(signal(attred, s), 16)
                            hold(e, *done(gathered, i, s, NS))
                            e.dma_start(gi[s][:, :, 0], dst_i[:, c]).then_inc(signal(indexed, s), 16)

                        pipelined(e, R, NS, [(stage, 0)])

                    @block.gpsimd
                    def _(e):
                        def gather(i, s):
                            hold(e, *done(indexed, i, s))
                            hold(e, *done(message, i, s, NS))
                            for k in range(G):
                                e.indirect_dma_start(rows[s][:, k, :], None, X3, bass.IndirectOffsetOnAxis(ap=gi[s][:, k, :], axis=0))\
                                    .then_inc(signal(gathered, s), 16)

                        def add(i, s):
                            hold(e, *done(copied, i, s))
                            hold(e, *done(added, i, s, 1))
                            for k in range(G):
                                e.indirect_dma_start(A[k], bass.IndirectOffsetOnAxis(ap=ai[s][:, k, :], axis=0), comb[s][:, k, :], None,
                                                     compute_op=ALU.add).then_inc(signal(added, s), 16)

                        pipelined(e, R, NS, [(gather, 0), (add, LAG)])
                        for sem, value in total(added, R):
                            e.wait_ge(sem, value)

                    @block.tensor
                    def _(e):
                        def hide(i, s):
                            hold(e, *done(attred, i, s))
                            hold(e, *done(active, i, s, 2))
                            for m in range(K):
                                mm = e.matmul(psH[s % 2][:, m * G * P:(m + 1) * G * P], wf1s[:, m * P:(m + 1) * P],
                                              rbf[s][:].rearrange("p g q -> p (g q)"), start=True, stop=True)
                            mm.then_inc(signal(hidden, s), 1)
                            hold(e, *done(compared, i, s, 2))
                            hold(e, *done(columned, i, s))
                            for k in range(G):
                                mm = e.transpose(psI[s % 2][:, k * P:(k + 1) * P], sc[s][:, k, :].to_broadcast([P, P]), ident[:])
                            mm.then_inc(signal(sourced, s), 1)

                        def filt(i, s):
                            hold(e, *done(active, i, s))
                            hold(e, *done(message, i, s, 2))
                            for k in range(G):
                                for m in range(K):
                                    mm = e.matmul(psF[s % 2][:, k * D:(k + 1) * D], hid[s][:, m, k * P:(k + 1) * P], wf2s[:, m, :],
                                                  start=m == 0, stop=m == K - 1)
                            mm.then_inc(signal(filtered, s), 1)

                        def join(i, s):
                            hold(e, *done(message, i, s))
                            hold(e, *done(compared, i, s))
                            hold(e, *done(copied, i, s, 2))
                            for k in range(G):
                                mm = e.matmul(psM[s % 2][:, k * D:(k + 1) * D], eq[s][:, k, :], fl[s][:, k, :], start=True, stop=True)
                            mm.then_inc(signal(joined, s), 1)

                        pipelined(e, R, NS, [(hide, 0), (filt, 1), (join, 2)])

                    @block.scalar
                    def _(e):
                        def column(i, s):
                            hold(e, *done(sourced, i, s, NS))
                            e.copy(sc[s][:, :, 0], src_f[:, bass.ds(i * (G * NS) + s * G, G)]).then_inc(signal(columned, s), 1)

                        def activate(i, s):
                            hold(e, *done(hidden, i, s))
                            hold(e, *done(message, i, s, NS))
                            for m in range(K):
                                ins = e.activation(hid[s][:, m, :], psH[s % 2][:, m * G * P:(m + 1) * G * P], ACT.Silu, bias=bf1s[:, m:m + 1])
                            ins.then_inc(signal(active, s), 1)

                        def copy(i, s):
                            hold(e, *done(joined, i, s))
                            hold(e, *done(added, i, s, NS))
                            e.copy(comb[s][:].rearrange("p g d -> p (g d)"), psM[s % 2][:]).then_inc(signal(copied, s), 1)

                        pipelined(e, R, NS, [(column, 0), (activate, 0), (copy, 2)])

                    @block.vector
                    def _(e):
                        def compare(i, s):
                            hold(e, *done(sourced, i, s))
                            hold(e, *done(joined, i, s, NS))
                            hold(e, *done(added, i, s, NS))
                            for k in range(G):
                                c = bass.ds(i * (G * NS) + (s * G + k), 1)
                                turned_k = psI[s % 2][:, k * P:(k + 1) * P]
                                e.tensor_scalar(eq[s][:, k, :], turned_k, src_f[:, c], None, ALU.is_equal)
                                e.scalar_tensor_tensor(low[s][:, k, :], turned_k, src_f[:, c], earlier[:], ALU.is_equal, ALU.mult,
                                                       accum_out=cnt[s][:, k, :]).then_inc(steps, 1)
                            base = G + 2
                            e.wait_ge(steps, i * (NS * base) + (s * base + G))
                            e.tensor_scalar(cnt[s][:], cnt[s][:], 0.0, None, ALU.is_equal).then_inc(steps, 1)
                            e.wait_ge(steps, i * (NS * base) + (s * base + G + 1))
                            c = bass.ds(i * (G * NS) + s * G, G)
                            e.tensor_tensor(cnt[s][:, :, 0], cnt[s][:, :, 0], srcmt[:, c], ALU.mult).then_inc(steps, 1)
                            e.wait_ge(steps, i * (NS * base) + (s * base + G + 2))
                            e.tensor_scalar(ai[s][:], cnt[s][:], trash[:], None, ALU.add).then_inc(signal(compared, s), 1)

                        def multiply(i, s):
                            hold(e, *done(filtered, i, s))
                            hold(e, *done(joined, i, s, NS))
                            hold(e, *done(gathered, i, s))
                            e.tensor_tensor(fl[s][:], psF[s % 2][:].rearrange("p (g d) -> p g d", g=G),
                                            bf2s[:].rearrange("p (g d) -> p g d", g=1).to_broadcast([P, G, D]), ALU.add).then_inc(msteps, 1)
                            e.wait_ge(msteps, i * NS + (s + 1))
                            e.tensor_tensor(fl[s][:], fl[s][:], rows[s][:], ALU.mult).then_inc(signal(message, s), 1)

                        pipelined(e, R, NS, [(compare, 0), (multiply, 1)])

        def update_nodes():
            with ExitStack() as ctx:
                G, NS = 2, 4
                R = C // (G * NS)
                t = lambda n: [ctx.enter_context(sbuf(f"{n}{s}", [P, K, G * P], F32)) for s in range(NS)]
                agg, more = [[ctx.enter_context(sbuf(f"{n}{s}", [P, G, D], F32)) for s in range(NS)] for n in ("agg", "more")]
                aT, hid, ht = t("aT"), t("hid"), t("ht")
                psA, psH, psO = [[ctx.enter_context(psum(f"{n}{j}", [P, K, G * P], F32)) for j in range(2)] for n in ("psA", "psH", "psO")]
                loaded, stored = stage_of("loaded", NS, 2), stage_of("stored", NS, 1)
                stages = [stage_of(n, NS) for n in ("summed", "turned", "copied", "hidden", "active", "updated", "biased", "measured")]
                summed, turned, copied, hidden, active, updated, biased, measured = stages
                with nc.Block() as block:
                    @block.sync
                    def _(e):

                        def load(i, s):
                            c = bass.ds(i * (G * NS) + s * G, G)
                            hold(e, *done(turned, i, s, NS))
                            e.dma_start(agg[s][:], nodes(A[0])[:, c, :]).then_inc(signal(loaded, s), 16)
                            e.dma_start(more[s][:], nodes(A[1])[:, c, :]).then_inc(signal(loaded, s), 16)

                        def store(i, s):
                            hold(e, *done(biased, i, s))
                            e.dma_start(HT[:, :, bass.ds(i * (G * NS * P) + s * (G * P), G * P)], ht[s][:]).then_inc(signal(stored, s), 16)

                        pipelined(e, R, NS, [(load, 0), (store, 4)])
                        for sem, value in total(stored, R):
                            e.wait_ge(sem, value)

                    @block.tensor
                    def _(e):
                        def turn(i, s):
                            hold(e, *done(summed, i, s))
                            hold(e, *done(copied, i, s, 2))
                            for m in range(K):
                                for k in range(G):
                                    mm = e.transpose(psA[s % 2][:, m, k * P:(k + 1) * P], agg[s][:, k, m * P:(m + 1) * P], ident[:])
                            mm.then_inc(signal(turned, s), 1)

                        def product(a, w, ps, finished, s):
                            for n in range(K):
                                for m in range(K):
                                    mm = e.matmul(ps[:, n, :], w[:, m, n * P:(n + 1) * P], a[s][:, m, :], start=m == 0, stop=m == K - 1)
                            mm.then_inc(signal(finished, s), 1)

                        def hide(i, s):
                            hold(e, *done(copied, i, s))
                            hold(e, *done(active, i, s, 2))
                            product(aT, wu1s, psH[s % 2], hidden, s)

                        def update(i, s):
                            hold(e, *done(active, i, s))
                            hold(e, *done(biased, i, s, 2))
                            product(hid, wu2s, psO[s % 2], updated, s)

                        pipelined(e, R, NS, [(turn, 0), (hide, 1), (update, 2)])

                    @block.scalar
                    def _(e):
                        def activate(i, s):
                            hold(e, *done(hidden, i, s))
                            hold(e, *done(updated, i, s, NS))
                            for m in range(K):
                                ins = e.activation(hid[s][:, m, :], psH[s % 2][:, m, :], ACT.Silu, bias=bu1s[:, m:m + 1])
                            ins.then_inc(signal(active, s), 1)

                        def bias(i, s):
                            hold(e, *done(updated, i, s))
                            hold(e, *done(stored, i, s, NS))
                            hold(e, *done(measured, i, s, NS))
                            for m in range(K):
                                ins = e.activation(ht[s][:, m, :], psO[s % 2][:, m, :], ACT.Identity, bias=bu2s[:, m:m + 1])
                            ins.then_inc(signal(biased, s), 1)

                        pipelined(e, R, NS, [(activate, 1), (bias, 2)])

                    @block.vector
                    def _(e):
                        def add(i, s):
                            hold(e, *done(loaded, i, s))
                            e.tensor_tensor(agg[s][:], agg[s][:], more[s][:], ALU.add).then_inc(signal(summed, s), 1)

                        def copy(i, s):
                            hold(e, *done(turned, i, s))
                            hold(e, *done(hidden, i, s, NS))
                            e.tensor_copy(aT[s][:], psA[s % 2][:]).then_inc(signal(copied, s), 1)

                        full = VC // (G * NS)
                        there = [P]

                        def measure(i, s):
                            if isinstance(i, int):
                                there[0] = P if i < full else P - 1
                            hold(e, *done(biased, i, s))
                            for m in range(K):
                                h4 = ht[s][:, m, :].rearrange("p (g q) -> p g q", g=G)[:, :, 0:there[0]]
                                ins = e.bn_stats(stats[:, m, bass.ds(i * NS + s, 1), :].rearrange("p a b -> p (a b)"), h4)
                            ins.then_inc(signal(measured, s), 1)

                        pipelined(e, R, NS, [(add, 0), (copy, 0), (measure, 3)], cut=full)

        def finish_nodes():
            with ExitStack() as ctx:
                G, NS = 2, 4
                R = C // (G * NS)
                mv, sd, scale, shift = [ctx.enter_context(sbuf(n, [P, K, w], F32)) for n, w in (("bmv", 2), ("bsd", 1), ("scale", 1), ("shift", 1))]
                ht = [ctx.enter_context(sbuf(f"ht{s}", [P, K, G * P], F32)) for s in range(NS)]
                xt, z, xo = [[ctx.enter_context(sbuf(f"{n}{s}", [P, G, D], F32)) for s in range(NS)] for n in ("xt", "z", "xo")]
                ps = [ctx.enter_context(psum(f"psN{j}", [P, G, D], F32)) for j in range(NS)]
                loaded, stored = stage_of("loaded", NS, 2), stage_of("stored", NS, 1)
                stages = [stage_of(n, NS) for n in ("normed", "turned", "summed", "finished")]
                normed, turned, summed, finished = stages
                ln_measure, ln_root, ln_invert, ln_apply = norm_of(ctx, NS, G, z, xo)
                agged, rooted, scaled = [semaphore(n) for n in ("agged", "brooted", "scaled")]
                with nc.Block() as block:
                    @block.sync
                    def _(e):

                        def load(i, s):
                            hold(e, *done(turned, i, s, NS))
                            e.dma_start(ht[s][:], HT[:, :, bass.ds(i * (G * NS * P) + s * (G * P), G * P)]).then_inc(signal(loaded, s), 16)
                            hold(e, *done(summed, i, s, NS))
                            e.dma_start(xt[s][:], nodes(X3)[:, bass.ds(i * (G * NS) + s * G, G), :]).then_inc(signal(loaded, s), 16)

                        def store(i, s):
                            hold(e, *done(finished, i, s))
                            e.dma_start(out[:, bass.ds(i * (G * NS) + s * G, G), :], xo[s][:]).then_inc(signal(stored, s), 16)

                        pipelined(e, R, NS, [(load, 0), (store, 5)])
                        for sem, value in total(stored, R):
                            e.wait_ge(sem, value)

                    @block.tensor
                    def _(e):
                        def turn(i, s):
                            hold(e, *done(normed, i, s))
                            hold(e, *done(summed, i, s, NS))
                            for k in range(G):
                                for m in range(K):
                                    mm = e.transpose(ps[s][:, k, m * P:(m + 1) * P], ht[s][:, m, k * P:(k + 1) * P], ident[:])
                            mm.then_inc(signal(turned, s), 1)

                        pipelined(e, R, NS, [(turn, 1)])

                    @block.scalar
                    def _(e):
                        e.wait_ge(agged, 1)
                        e.activation(sd[:, :, 0], mv[:, :, 1], ACT.Sqrt, bias=epsc[:]).then_inc(rooted, 1)
                        e.wait_ge(scaled, 4)

                        def batch_norm(i, s):
                            hold(e, *done(loaded, i, s))
                            for m in range(K):
                                ins = e.activation(ht[s][:, m, :], ht[s][:, m, :], ACT.Identity, bias=shift[:, m, :], scale=scale[:, m, :])
                            ins.then_inc(signal(normed, s), 1)

                        def apply(i, s):
                            hold(e, *done(stored, i, s, NS))
                            ln_apply(e, i, s, finished)

                        pipelined(e, R, NS, [(batch_norm, 0), (lambda i, s: ln_root(e, i, s), 2), (apply, 3)])

                    @block.vector
                    def _(e):
                        for m in range(K):
                            ins = e.bn_aggr(mv[:, m, :], stats[:, m, :, :].rearrange("p a b -> p (a b)"))
                        ins.then_inc(agged, 1)
                        e.wait_ge(rooted, 1)
                        e.reciprocal(sd[:], sd[:]).then_inc(scaled, 1)
                        e.wait_ge(scaled, 1)
                        e.tensor_tensor(scale[:, :, 0], sd[:, :, 0], gms[:], ALU.mult).then_inc(scaled, 1)
                        e.wait_ge(scaled, 2)
                        e.tensor_tensor(shift[:, :, 0], scale[:, :, 0], mv[:, :, 0], ALU.mult).then_inc(scaled, 1)
                        e.wait_ge(scaled, 3)
                        e.tensor_tensor(shift[:, :, 0], bts[:], shift[:, :, 0], ALU.subtract).then_inc(scaled, 1)

                        def add(i, s):
                            hold(e, *done(turned, i, s))
                            hold(e, *done(finished, i, s, NS))
                            e.scalar_tensor_tensor(z[s][:], xt[s][:], 2.0, ps[s][:], ALU.mult, ALU.add).then_inc(signal(summed, s), 1)
                            hold(e, *done(summed, i, s))
                            ln_measure(e, i, s)

                        pipelined(e, R, NS, [(add, 2), (lambda i, s: ln_invert(e, i, s), 3)])

        for phase in (setup, lambda: hop_table(True), lambda: hop_edges(A[0]), lambda: hop_table(False), lambda: hop_edges(A[1]),
                      lambda: layer_nodes(0), lambda: attention_edges(1), lambda: layer_nodes(1),
                      lambda: attention_edges(2), lambda: layer_nodes(2), filter_edges, update_nodes, finish_nodes):
            with nc.cleanup_on_exit():
                phase()


def kernel(**inputs):
    import numpy as np
    import concourse.bacc as bacc
    from concourse.bass_utils import run_bass_kernel_spmd

    a = {k: np.asarray(v) for k, v in inputs.items()}
    N, E = a["x"].shape[0], a["src"].shape[0]
    C = -(-max(N, E) // (P * 8)) * 8
    NP = P * C

    def pad(v, fill=0):
        return np.concatenate([v, np.full((NP - v.shape[0], *v.shape[1:]), fill, v.dtype)])

    def by_column(v):
        return np.ascontiguousarray(pad(v).reshape(P, C, -1).transpose(2, 1, 0))

    def spread(v):
        m = np.zeros((D, H), v.dtype)
        for h in range(H):
            m[h * HD:(h + 1) * HD, h] = v[h]
        return m

    halves = lambda v: np.ascontiguousarray(v.reshape(K, P).T)
    row = lambda v: v.reshape(1, D)
    dst = np.concatenate([pad(a["dst"], N), np.full(1, N + 1, a["dst"].dtype)])
    T = lambda v: np.ascontiguousarray(v.T)
    arrays = dict(
        x=pad(a["x"]).reshape(P, C, D), src=pad(a["src"], N).reshape(P, C), dst=np.ascontiguousarray(dst[:NP].reshape(P, C)),
        dst_next=np.ascontiguousarray(dst[1:].reshape(P, C)), ew=pad(a["edge_weight"]).reshape(P, C),
        rbfT=by_column(a["edge_attr_20"]), attr3T=by_column(a["edge_attr_3"]), attr64T=by_column(a["edge_attr_64"]),
        w0T=T(a["L0_gnn_W"]), b0=row(a["L0_gnn_b"]),
        w1T=T(a["L1_gnn_W"]), w1=a["L1_gnn_W"],
        a1=np.concatenate([spread(a["L1_gnn_a_src"]), spread(a["L1_gnn_a_dst"])], axis=1),
        encW=np.concatenate([T(a["L1_gnn_edge_W"]), row(a["L1_gnn_edge_b"])]), bias1=row(a["L1_gnn_bias"]),
        wfc=a["L2_gnn_W_fc"], wfcT=T(a["L2_gnn_W_fc"]),
        ah=np.concatenate([spread(a["L2_gnn_attn_h"]), spread(a["L2_gnn_attn_t"])], axis=1),
        ae=spread(a["L2_gnn_attn_e"]), weT=T(a["L2_gnn_W_e"]), bias2=row(a["L2_gnn_bias"]),
        wf1=a["L3_gnn_Wf1"], bf1=halves(a["L3_gnn_bf1"]), wf2=a["L3_gnn_Wf2"], bf2=row(a["L3_gnn_bf2"]),
        wu1=a["L3_gnn_Wu1"], bu1=halves(a["L3_gnn_bu1"]), wu2=a["L3_gnn_Wu2"], bu2=halves(a["L3_gnn_bu2"]),
        gamma=halves(a["L3_gnn_gamma"]), beta=halves(a["L3_gnn_beta"]))
    nc = bacc.Bacc("TRN2", target_bir_lowering=False, num_devices=1)
    args = {n: nc.dram_tensor(f"in_{n}", v.shape, mybir.dt.from_np(v.dtype), kind="ExternalInput").ap() for n, v in arrays.items()}
    out = nc.dram_tensor("out", (P, C, D), F32, kind="ExternalOutput").ap()
    build(nc, N, out=out, **args)
    r = run_bass_kernel_spmd(nc, [{f"in_{n}": v for n, v in arrays.items()}], core_ids=[0])
    return r.results[0]["out"].reshape(NP, D)[:N]
```

```python
from contextlib import ExitStack

import concourse.bass as bass
from concourse import mybir

P = 128
D = 256
H = 8
HD = D // H
HW = HD + 1
VW = H * HW
SW = VW + H
TW = SW + H
DW = D + 2 * H
K = D // P
NONE = -1.0e30
OUT = 1.0e6
EPS = 1e-5

ALU = mybir.AluOpType
ACT = mybir.ActivationFunctionType
AX = mybir.AxisListType.X
F32 = mybir.dt.float32
I32 = mybir.dt.int32



def signal(stage, s):
    sems, _, dmas = stage
    return sems[s if dmas else 0]


def done(stage, i, s, back=0):
    sems, slots, dmas = stage
    if dmas:
        return sems[(s - back) % slots], (i + ((s - back) // slots + 1)) * (16 * dmas)
    return sems[0], i * slots + (s - back + 1)


def total(stage, rounds):
    sems, slots, dmas = stage
    return [(sem, rounds * (16 * dmas if dmas else slots)) for sem in sems]


def pipelined(e, rounds, slots, stages, cut=0):
    most = max(lag for _, lag in stages)

    def step(i, s, which=lambda lag: True):
        for stage, lag in stages:
            if which(lag):
                stage(i + (s - lag) // slots, (s - lag) % slots)

    def loop(first, last):
        if first < last:
            with e.Fori(first, last) as i:
                for s in range(slots):
                    step(i, s)

    start = 1 - (-most // slots)
    assert start < rounds
    for i in range(start):
        for s in range(slots):
            step(i, s, lambda lag: i * slots + s >= lag)
    if cut >= start:
        loop(start, cut)
        start = cut - (-most // slots)
        for i in range(cut, start):
            for s in range(slots):
                step(i, s)
    loop(start, rounds)
    for s in range(most):
        step(rounds, s, lambda lag: lag > s)


def build(nc, N, x, src, srcT, dst, dst_next, ew, rbfT, attr3T, attr64T, w0T, b0, w1T, w1, a1, encW, bias1,
          wfc, wfcT, ah, ae, weT, bias2, wf1, bf1, wf2, bf2, wu1, bu1, wu2, bu2, gamma, beta, out):
    C = x.shape[1]
    NP = P * C
    VC = N - (P - 1) * C
    assert C % 8 == 0 and VC % 8 == 0 and 0 < VC < C

    alone = (nc.sync.engine, nc.gpsimd.engine, nc.scalar.engine)
    used = {}

    def fresh(name):
        used[name] = used.get(name, 0) + 1
        return f"{name}_{used[name]}"

    def semaphore(name):
        return nc.alloc_semaphore(fresh(name))

    def stage_of(name, slots, dmas=0):
        return [semaphore(f"{name}{s}") for s in range(slots if dmas else 1)], slots, dmas

    def sbuf(name, shape, dt):
        return nc.sbuf_tensor(fresh(name), shape, dt)

    def psum(name, shape, dt):
        return nc.psum_tensor(fresh(name), shape, dt)

    marks = nc.alloc_semaphore("marks")

    def hold(e, sem, value):
        if isinstance(value, int) and value <= 0:
            return
        e.wait_ge(sem, value)
        if e.engine in alone:
            e.sem_inc(marks, 1)

    def dram(name, rows, width):
        return nc.dram_tensor(name, (rows, width), F32).ap()

    def nodes(t):
        return t[0:NP, :].rearrange("(p c) d -> p c d", p=P)

    SPARE = 8
    T, S = dram("T", NP + SPARE * P, D), dram("S", NP, SW)
    X1, X2, X3 = dram("X1", NP, D), dram("X2", NP, D), dram("X3", NP, D)
    T1, T2, ET = dram("T1", NP, TW), dram("T2", NP, SW), dram("ET", NP, H)
    A = [dram("A0", NP + P, D), dram("A1", NP + P, D)]
    HT = nc.dram_tensor("HT", (P, K, C * P), F32).ap()

    with ExitStack() as keep:
        def sb(name, shape, dt=F32):
            return keep.enter_context(sbuf(name, shape, dt))

        src_i, dst_i, scat_i = sb("src_i", [P, C], I32), sb("dst_i", [P, C], I32), sb("scat_i", [P, C], I32)
        src_f, src_col, same, pen, w_sb = sb("src_f", [P, C]), sb("src_col", [P, C]), sb("same", [P, C]), sb("pen", [P, C]), sb("w_sb", [P, C])
        dinv, ca, cb, srcmt = sb("dinv", [P, C]), sb("ca", [P, C]), sb("cb", [P, C]), sb("srcmt", [P, C])
        add_i, first_add_i, ca_first = sb("add_i", [P, C], I32), sb("first_add_i", [P, 1], I32), sb("ca_first", [P, 1])
        first_i, low, high, cols = sb("first_i", [P, 1], I32), sb("low", [P, 1]), sb("high", [P, 1]), sb("cols", [P, C])
        trash = sb("trash", [P, 1])
        ident, before, earlier, chain, chainT, penT = [sb(n, [P, P]) for n in ("ident", "before", "earlier", "chain", "chainT", "penT")]
        epsc = sb("epsc", [P, 1])
        w0s, wf2s, wu1s, wu2s = [sb(n, [P, K, D]) for n in ("w0s", "wf2s", "wu1s", "wu2s")]
        w1s, w2s = sb("w1s", [P, K, DW]), sb("w2s", [P, K, DW])
        encs, wf1s, fes = sb("encs", [4, D]), sb("wf1s", [wf1.shape[0], D]), sb("fes", [attr64T.shape[0], H])
        b0s, b1s, b2s, bf2s = [sb(n, [P, D]) for n in ("b0s", "b1s", "b2s", "bf2s")]
        bf1s, bu1s, bu2s, gms, bts = [sb(n, [P, K]) for n in ("bf1s", "bu1s", "bu2s", "gms", "bts")]
        zero = sb("zero", [P, SW])
        stats = sb("stats", [P, K, C // 2, 6])

        def setup():
            with ExitStack() as ctx:
                def tmp(name, shape, dt=F32):
                    return ctx.enter_context(sbuf(name, shape, dt))

                def sem(name):
                    return semaphore(name)

                dst_f, next_i, islast, notl = tmp("dst_f", [P, C]), tmp("next_i", [P, C], I32), tmp("islast", [P, C]), tmp("notl", [P, C])
                any_last, firstf, lastf = tmp("any_last", [P, 1]), tmp("firstf", [P, 1]), tmp("lastf", [P, 1])
                rows0 = tmp("rows0", [P, P])
                pcol, w1n, a1s, wfT, ahs, aes, weTs = (tmp("pcol", [P, 1]), tmp("w1n", [P, K, D]), tmp("a1s", [P, K, 2 * H]),
                                                  tmp("wfT", [P, K, D]), tmp("ahs", [P, K, 2 * H]), tmp("aes", [P, K, H]),
                                                  tmp("weTs", [P, K, attr64T.shape[0]]))
                part_i, part, col, over = tmp("part_i", [P, C], I32), tmp("part", [P, C]), tmp("col", [P, C]), tmp("over", [P, C])
                spare, at_first, run = tmp("spare", [P, C]), tmp("at_first", [P, C]), tmp("run", [P, C])
                hot, hotc = tmp("hot", [P, 4, P]), tmp("hotc", [P, 4, C])
                psT = ctx.enter_context(psum("psT", [P, P], F32))
                psDeg = ctx.enter_context(psum("psDeg", [P, 512], F32))
                psF = ctx.enter_context(psum("psF", [P, K, 16], F32))
                psG = ctx.enter_context(psum("psG", [P, K, 16], F32))
                psE = ctx.enter_context(psum("psE", [P, 16], F32))
                loaded, zeroed, iotas, prep, tr, folds, onehot, summed, filled, rooted = [sem(n) for n in (
                    "loaded", "zeroed", "iotas", "prep", "tr", "folds", "onehot", "summed", "filled", "rooted")]
                loads = [(src_i[:], src), (dst_i[:], dst), (next_i[:], dst_next), (w_sb[:], ew),
                         (encs[:], encW), (wf1s[:], wf1)]
                loads += [(t[:, :, :], w.rearrange("(k p) d -> p k d", p=P)) for t, w in (
                    (w0s, w0T), (w1s[:, :, 0:D], w1T), (w2s[:, :, 0:D], wfc), (wf2s, wf2), (wu1s, wu1), (wu2s, wu2), (w1n, w1), (a1s, a1),
                    (wfT, wfcT), (ahs, ah), (aes, ae), (weTs, weT))]
                loads += [(t[:], b.to_broadcast([P, D])) for t, b in ((b0s, b0), (b1s, bias1), (b2s, bias2), (bf2s, bf2))]
                loads += [(t[:], b) for t, b in ((bf1s, bf1), (bu1s, bu1), (bu2s, bu2), (gms, gamma), (bts, beta))]
                NL = 16 * len(loads)
                fills = [(t[NP:NP + P, :], zero[:, 0:D]) for t in A]
                fills += [(T[NP + j * P:NP + (j + 1) * P, :], zero[:, 0:D]) for j in range(SPARE)]
                fills += [(nodes(T)[:, c0:min(c0 + 56, C), :], x[:, c0:min(c0 + 56, C), :]) for c0 in range(0, C, 56)]

                with nc.Block() as block:
                    @block.sync
                    def _(e):
                        for to, frm in loads:
                            e.dma_start(to, frm).then_inc(loaded, 16)
                        e.wait_ge(zeroed, 1)
                        for to, frm in fills:
                            e.dma_start(to, frm).then_inc(filled, 16)

                    @block.gpsimd
                    def _(e):
                        e.memset(zero[:], 0.0).then_inc(zeroed, 1)
                        e.memset(ident[:], 0.0).then_inc(iotas, 1)
                        e.memset(before[:], 1.0).then_inc(iotas, 1)
                        e.memset(epsc[:], EPS).then_inc(iotas, 1)
                        e.iota(cols[:], pattern=[[1, C]], base=0, channel_multiplier=0, allow_small_or_imprecise_dtypes=True).then_inc(iotas, 1)
                        e.iota(rows0[:], pattern=[[1, P]], base=0, channel_multiplier=0, allow_small_or_imprecise_dtypes=True).then_inc(iotas, 1)
                        e.iota(pcol[:], pattern=[[0, 1]], base=0, channel_multiplier=1, allow_small_or_imprecise_dtypes=True).then_inc(iotas, 1)
                        e.iota(trash[:], pattern=[[0, 1]], base=NP, channel_multiplier=1, allow_small_or_imprecise_dtypes=True).then_inc(iotas, 1)
                        e.memset(earlier[:], 1.0).then_inc(iotas, 1)
                        e.iota(low[:], pattern=[[0, 1]], base=0, channel_multiplier=C, allow_small_or_imprecise_dtypes=True).then_inc(iotas, 1)
                        e.iota(high[:], pattern=[[0, 1]], base=C, channel_multiplier=C, allow_small_or_imprecise_dtypes=True).then_inc(iotas, 1)
                        e.iota(spare[:].rearrange("p (b j) -> p b j", j=SPARE), pattern=[[0, C // SPARE], [P, SPARE]], base=NP,
                               channel_multiplier=1, allow_small_or_imprecise_dtypes=True).then_inc(iotas, 1)
                        e.wait_ge(iotas, 11)
                        e.affine_select(out=ident[:], in_=ident[:], compare_op=ALU.not_equal, fill=1.0, base=0,
                                        pattern=[[-1, P]], channel_multiplier=1).then_inc(iotas, 1)
                        e.affine_select(out=before[:], in_=before[:], compare_op=ALU.is_gt, fill=0.0, base=0,
                                        pattern=[[1, P]], channel_multiplier=-1).then_inc(iotas, 1)
                        e.affine_select(out=earlier[:], in_=earlier[:], compare_op=ALU.is_gt, fill=0.0, base=0,
                                        pattern=[[-1, P]], channel_multiplier=1).then_inc(iotas, 1)

                    @block.vector
                    def _(e):
                        n = [0]

                        def link(ins):
                            n[0] += 1
                            ins.then_inc(prep, 1)
                            e.wait_ge(prep, n[0])

                        e.wait_ge(loaded, NL)
                        e.wait_ge(iotas, 14)
                        link(e.tensor_copy(src_f[:], src_i[:]))
                        link(e.tensor_copy(dst_f[:], dst_i[:]))
                        link(e.tensor_copy(notl[:], next_i[:]))
                        link(e.memset(same[:, 0:1], 0.0))
                        link(e.tensor_tensor(same[:, 1:C], dst_f[:, 1:C], dst_f[:, 0:C - 1], ALU.is_equal))
                        link(e.tensor_tensor(islast[:], dst_f[:], notl[:], ALU.is_lt))
                        link(e.tensor_scalar(pen[:], same[:], -1.0, -NONE, ALU.add, ALU.mult))
                        link(e.tensor_scalar(notl[:], dst_f[:], -OUT, None, ALU.add))
                        link(e.tensor_tensor(notl[:], notl[:], islast[:], ALU.mult))
                        link(e.tensor_scalar(scat_i[:], notl[:], OUT, None, ALU.add))
                        link(e.tensor_reduce(any_last[:], islast[:], AX, ALU.max))
                        link(e.tensor_copy(firstf[:], dst_f[:, 0:1]))
                        link(e.tensor_copy(lastf[:], dst_f[:, C - 1:C]))
                        link(e.tensor_scalar(pcol[:], firstf[:], -OUT, any_last[:], ALU.add, ALU.mult))
                        link(e.tensor_scalar(first_i[:], pcol[:], OUT, None, ALU.add))
                        link(e.tensor_scalar(srcmt[:], src_f[:], trash[:], None, ALU.subtract))
                        e.wait_ge(tr, 1)
                        link(e.tensor_scalar(chain[:], psT[:], lastf[:], None, ALU.is_equal))
                        link(e.tensor_tensor(chain[:], chain[:], before[:], ALU.mult))
                        e.wait_ge(tr, 2)
                        link(e.tensor_copy(chainT[:], psT[:]))
                        link(e.tensor_scalar(penT[:], chainT[:], -1.0, -NONE, ALU.add, ALU.mult))
                        e.wait_ge(folds, 1)
                        link(e.tensor_copy(w1s[:, :, D:DW], psF[:]))
                        link(e.tensor_copy(w2s[:, :, D:DW], psG[:]))
                        link(e.tensor_copy(fes[:], psE[0:fes.shape[0], 0:H]))
                        link(e.tensor_tensor(over[:], dst_f[:], spare[:], ALU.subtract))
                        link(e.tensor_tensor(over[:], over[:], islast[:], ALU.mult))
                        link(e.tensor_tensor(add_i[:], over[:], spare[:], ALU.add))
                        link(e.tensor_scalar(pcol[:], firstf[:], trash[:], any_last[:], ALU.subtract, ALU.mult))
                        link(e.tensor_scalar(first_add_i[:], pcol[:], trash[:], None, ALU.add))
                        link(e.tensor_scalar(at_first[:], dst_f[:], firstf[:], None, ALU.is_equal))
                        link(e.tensor_tensor(at_first[:], at_first[:], islast[:], ALU.mult))
                        link(e.tensor_tensor_scan(run[:], same[:], w_sb[:], 0.0, ALU.mult, ALU.add))
                        e.wait_ge(folds, 2)
                        link(e.tensor_copy(over[:], w_sb[:]))
                        link(e.tensor_tensor(over[:, 0:1], over[:, 0:1], psT[:, 0:1], ALU.add))
                        link(e.tensor_tensor_scan(run[:], same[:], over[:], 0.0, ALU.mult, ALU.add))
                        for node, at in ((src_f, src_col), (dst_f, col)):
                            link(e.tensor_scalar(part_i[:], node[:], 1.0 / C, None, ALU.mult))
                            link(e.tensor_copy(part[:], part_i[:]))
                            link(e.scalar_tensor_tensor(at[:], part[:], -float(C), node[:], ALU.mult, ALU.add))
                            link(e.tensor_scalar(over[:], at[:], 0.0, None, ALU.is_lt))
                            link(e.tensor_tensor(part[:], part[:], over[:], ALU.subtract))
                            link(e.scalar_tensor_tensor(at[:], over[:], float(C), at[:], ALU.mult, ALU.add))
                            link(e.tensor_scalar(over[:], at[:], float(C), None, ALU.is_ge))
                            link(e.tensor_tensor(part[:], part[:], over[:], ALU.add))
                            link(e.scalar_tensor_tensor(at[:], over[:], -float(C), at[:], ALU.mult, ALU.add))

                    @block.tensor
                    def _(e):
                        e.wait_ge(prep, 13)
                        e.wait_ge(iotas, 14)
                        e.transpose(psT[:], firstf[:].to_broadcast([P, P]), ident[:]).then_inc(tr, 1)
                        e.wait_ge(prep, 18)
                        e.transpose(psT[:], chain[:], ident[:]).then_inc(tr, 1)
                        for m in range(K):
                            for k in range(K):
                                e.matmul(psF[:, m, :], w1n[:, k, m * P:(m + 1) * P], a1s[:, k, :], start=k == 0, stop=k == K - 1)
                            for k in range(K):
                                e.matmul(psG[:, m, :], wfT[:, k, m * P:(m + 1) * P], ahs[:, k, :], start=k == 0, stop=k == K - 1)
                        for k in range(K):
                            mm = e.matmul(psE[0:weTs.shape[2], 0:H], weTs[:, k, :], aes[:, k, :], start=k == 0, stop=k == K - 1)
                        mm.then_inc(folds, 1)
                        e.wait_ge(prep, 31)
                        e.matmul(psT[:, 0:1], chain[:], run[:, C - 1:C], start=True, stop=True).then_inc(folds, 1)

                with nc.Block() as block:
                    NS = 4
                    R = C // NS
                    hots, taken = stage_of("hots", NS), stage_of("taken", NS)

                    @block.sync
                    def _(e):
                        e.wait_ge(filled, 16 * len(fills))

                    @block.vector
                    def _(e):
                        def one_hot(i, s):
                            c = bass.ds(i * NS + s, 1)
                            hold(e, *done(taken, i, s, NS))
                            e.tensor_scalar(hot[:, s, :], rows0[:], part[:, c], w_sb[:, c], ALU.is_equal, ALU.mult)
                            e.tensor_scalar(hotc[:, s, :], cols[:], col[:, c], None, ALU.is_equal).then_inc(signal(hots, s), 1)

                        pipelined(e, R, NS, [(one_hot, 0)])

                    @block.tensor
                    def _(e):
                        def both(i, first, last):
                            for s in range(NS):
                                hold(e, *done(hots, i, s))
                                e.matmul(psDeg[:, 0:C], hot[:, s, :], hotc[:, s, :], start=first and s == 0, stop=last and s == NS - 1)\
                                    .then_inc(signal(taken, s), 1)

                        both(0, True, False)
                        with e.Fori(1, R - 1) as i:
                            both(i, False, False)
                        both(R - 1, False, True)

                with nc.Block() as block:
                    deg, ok, dsq = tmp("deg", [P, 2, C]), tmp("ok", [P, 2, C]), tmp("dsq", [P, 2, C])
                    clamped, sq = sem("clamped"), sem("sq")

                    @block.vector
                    def _(e):
                        n = [0]

                        def link(ins):
                            n[0] += 1
                            ins.then_inc(clamped, 1)
                            e.wait_ge(clamped, n[0])

                        link(e.tensor_scalar(deg[:, 0, :], psDeg[:, 0:C], 1.0, None, ALU.add))
                        link(e.tensor_scalar(deg[:, 1, :], run[:], 1.0, None, ALU.add))
                        link(e.tensor_scalar(ok[:], deg[:], 0.0, None, ALU.is_gt))
                        link(e.tensor_scalar(deg[:], deg[:], 1e-12, None, ALU.max))
                        e.wait_ge(sq, 1)
                        link(e.reciprocal(dsq[:], dsq[:]))
                        link(e.tensor_tensor(dsq[:], dsq[:], ok[:], ALU.mult))
                        link(e.tensor_copy(dinv[:], dsq[:, 0, :]))
                        link(e.scalar_tensor_tensor(cb[:], dinv[:], 0.5, dinv[:], ALU.mult, ALU.mult))
                        link(e.scalar_tensor_tensor(cb[:], cb[:], 0.5, dinv[:], ALU.add, ALU.mult))
                        link(e.tensor_tensor(ca[:], dsq[:, 1, :], dsq[:, 1, :], ALU.mult))
                        link(e.tensor_scalar(ca[:], ca[:], 1.0, None, ALU.add))
                        link(e.reciprocal(ca[:], ca[:]))
                        link(e.tensor_tensor(ca[:], ca[:], dsq[:, 1, :], ALU.mult))
                        link(e.tensor_tensor(at_first[:], at_first[:], ca[:], ALU.mult))
                        link(e.tensor_reduce(ca_first[:], at_first[:], AX, ALU.add))

                    @block.scalar
                    def _(e):
                        e.wait_ge(clamped, 4)
                        e.activation(dsq[:], deg[:], ACT.Sqrt).then_inc(sq, 1)

        def hop_edges(hop, cleared_table):
            table, rows_i = ((x.rearrange("p c d -> (p c) d"), add_i), (T, scat_i))[hop]
            factors = (dinv, cb)[hop]
            cleared = ([S] if hop == 0 else []) + [cleared_table]
            with ExitStack() as ctx:
                G, NS, LAG = 2, 4, 3
                R = C // (G * NS)
                tiles = lambda n, w, dt=F32: [ctx.enter_context(sbuf(f"{n}{s}", [P, G, w], dt)) for s in range(NS)]
                rows, sums = tiles("rows", D), tiles("sums", SW)
                scaled_sums = tiles("scaled_sums", D) if hop == 0 else None
                gi, si = tiles("gi", 1, I32), tiles("si", 1, I32)
                placed = stage_of("placed", NS, 1)
                indexed, gathered, scattered = (stage_of("indexed", NS, 1), stage_of("gathered", NS, G),
                                                stage_of("scattered", NS, G))
                weighted, summed, scaled = stage_of("weighted", NS), stage_of("summed", NS), stage_of("scaled", NS)
                steps = semaphore("steps")
                started, filled = semaphore("started"), semaphore("filled")
                srow, above, hot = tiles("srow", P, I32), tiles("above", P), tiles("hot", P)
                picked, fsrc, factor = tiles("picked", C), tiles("fsrc", 1), tiles("factor", 1)
                psL = [ctx.enter_context(psum(f"psL{j}", [P, G, 512], F32)) for j in range(2)]
                spread = stage_of("spread", NS, 1)
                marked, hots, found, masked, looked, factored = (stage_of(n, NS) for n in (
                    "marked", "hots", "found", "masked", "looked", "factored"))
                with nc.Block() as block:
                    @block.sync
                    def _(e):

                        def stage(i, s):
                            c = bass.ds(i * (G * NS) + s * G, G)
                            hold(e, *done(hots, i, s, NS))
                            e.dma_start(srow[s][:], srcT[c, :].rearrange("(o g) p -> o g p", o=1).to_broadcast([P, G, P]))\
                                .then_inc(signal(spread, s), 16)
                            hold(e, *done(gathered, i, s, NS))
                            e.dma_start(gi[s][:, :, 0], src_i[:, c]).then_inc(signal(indexed, s), 16)
                            for t in cleared:
                                w = t.shape[1]
                                e.dma_start(nodes(t)[:, c, :], zero[:, 0:w].rearrange("p (g d) -> p g d", g=1).to_broadcast([P, G, w])).then_inc(filled, 16)

                        def stage_scatter(i, s):
                            c = bass.ds(i * (G * NS) + s * G, G)
                            hold(e, *done(scattered, i, s, NS))
                            e.dma_start(si[s][:, :, 0], rows_i[:, c]).then_inc(signal(placed, s), 16)

                        pipelined(e, R, NS, [(stage, 0), (stage_scatter, 2)])
                        e.wait_ge(filled, 16 * len(cleared) * R * NS)

                    @block.gpsimd
                    def _(e):
                        def gather(i, s):
                            hold(e, *done(indexed, i, s))
                            hold(e, *done(summed, i, s, NS))
                            for k in range(G):
                                e.indirect_dma_start(rows[s][:, k, :], None, table, bass.IndirectOffsetOnAxis(ap=gi[s][:, k, :], axis=0))\
                                    .then_inc(signal(gathered, s), 16)

                        def scatter(i, s):
                            hold(e, *done(placed, i, s))
                            hold(e, *done(summed if hop else scaled, i, s))
                            for k in range(G):
                                at = bass.IndirectOffsetOnAxis(ap=si[s][:, k, :], axis=0)
                                if hop == 0:
                                    e.indirect_dma_start(T, at, scaled_sums[s][:, k, :], None, compute_op=ALU.add)\
                                        .then_inc(signal(scattered, s), 16)
                                else:
                                    e.indirect_dma_start(S, at, sums[s][:, k, :], None, bounds_check=NP - 1, oob_is_err=False)\
                                        .then_inc(signal(scattered, s), 16)

                        pipelined(e, R, NS, [(gather, 0), (scatter, LAG)])
                        for sem, value in total(scattered, R):
                            e.wait_ge(sem, value)

                    @block.scalar
                    def _(e):
                        def weigh(i, s):
                            hold(e, *done(gathered, i, s))
                            hold(e, *done(factored, i, s))
                            for k in range(G):
                                ins = e.activation(rows[s][:, k, :], rows[s][:, k, :], ACT.Copy, scale=factor[s][:, k, :])
                            ins.then_inc(signal(weighted, s), 1)

                        def scale(i, s):
                            hold(e, *done(summed, i, s))
                            hold(e, *done(scattered, i, s, NS))
                            for k in range(G):
                                ins = e.activation(scaled_sums[s][:, k, :], sums[s][:, k, 0:D], ACT.Copy, scale=ca[:, bass.ds(i * (G * NS) + (s * G + k), 1)])
                            ins.then_inc(signal(scaled, s), 1)

                        pipelined(e, R, NS, [(weigh, 0)] + ([(scale, 1)] if hop == 0 else []))

                    @block.vector
                    def _(e):
                        for s in range(NS):
                            ins = e.memset(sums[s][:], 0.0)
                        ins.then_inc(started, 1)
                        e.wait_ge(started, 1)

                        def add(i, s):
                            hold(e, *done(weighted, i, s))
                            hold(e, *done(scattered if hop else scaled, i, s, NS))
                            for k in range(G):
                                last = sums[s][:, k - 1, 0:D] if k else sums[(s - 1) % NS][:, G - 1, 0:D]
                                ins = e.scalar_tensor_tensor(sums[s][:, k, 0:D], last, same[:, bass.ds(i * (G * NS) + (s * G + k), 1)],
                                                             rows[s][:, k, :], ALU.mult, ALU.add)
                                if k < G - 1:
                                    ins.then_inc(steps, 1)
                                    e.wait_ge(steps, i * NS * (G - 1) + (s * (G - 1) + k + 1))
                            ins.then_inc(signal(summed, s), 1)
                            hold(e, *done(summed, i, s))

                        def mark(i, s):
                            hold(e, *done(spread, i, s))
                            e.tensor_scalar(above[s][:], srow[s][:], low[:], None, ALU.is_ge).then_inc(signal(marked, s), 1)

                        def one_hot(i, s):
                            hold(e, *done(marked, i, s))
                            hold(e, *done(found, i, s, NS))
                            e.scalar_tensor_tensor(hot[s][:], srow[s][:], high[:], above[s][:], ALU.is_lt, ALU.mult).then_inc(signal(hots, s), 1)

                        def mask(i, s):
                            hold(e, *done(found, i, s))
                            for k in range(G):
                                ins = e.scalar_tensor_tensor(picked[s][:, k, :], cols[:], src_col[:, bass.ds(i * (G * NS) + (s * G + k), 1)],
                                                             psL[s % 2][:, k, 0:C], ALU.is_equal, ALU.mult)
                            ins.then_inc(signal(masked, s), 1)

                        def pick(i, s):
                            hold(e, *done(masked, i, s))
                            e.tensor_reduce(fsrc[s][:, :, 0], picked[s][:], AX, ALU.add).then_inc(signal(looked, s), 1)

                        def multiply(i, s):
                            hold(e, *done(looked, i, s))
                            hold(e, *done(weighted, i, s, NS))
                            e.tensor_tensor(factor[s][:, :, 0], fsrc[s][:, :, 0], w_sb[:, bass.ds(i * (G * NS) + s * G, G)], ALU.mult)\
                                .then_inc(signal(factored, s), 1)

                        pipelined(e, R, NS, [(mark, 0), (one_hot, 1), (mask, 2), (add, 3), (pick, 2), (multiply, 2)])

                    @block.tensor
                    def _(e):
                        def find(i, s):
                            hold(e, *done(hots, i, s))
                            hold(e, *done(masked, i, s, 2))
                            for k in range(G):
                                mm = e.matmul(psL[s % 2][:, k, 0:C], hot[s][:, k, :], factors[:], start=True, stop=True)
                            mm.then_inc(signal(found, s), 1)

                        pipelined(e, R, NS, [(find, 0)])

                with nc.Block() as block:
                    own, ps = ctx.enter_context(sbuf("own", [P, SW], F32)), ctx.enter_context(psum("psC", [P, D], F32))
                    fetched, cleared, carried, fixed, put = [semaphore(n) for n in (
                        "fetched", "cleared", "carried", "fixed", "put")]

                    @block.vector
                    def _(e):
                        if hop:
                            e.memset(own[:], 0.0).then_inc(cleared, 1)
                            e.wait_ge(fetched, 16)
                        e.wait_ge(carried, 1)
                        if hop == 0:
                            e.tensor_scalar(own[:, 0:D], ps[:], ca_first[:], None, ALU.mult).then_inc(fixed, 1)
                        else:
                            e.tensor_tensor(own[:, 0:D], own[:, 0:D], ps[:], ALU.add).then_inc(fixed, 1)

                    @block.tensor
                    def _(e):
                        e.matmul(ps[:], chain[:], sums[NS - 1][:, G - 1, 0:D], start=True, stop=True).then_inc(carried, 1)

                    @block.gpsimd
                    def _(e):
                        at = bass.IndirectOffsetOnAxis(ap=first_i[:], axis=0)
                        if hop:
                            e.wait_ge(cleared, 1)
                            e.indirect_dma_start(own[:], None, S, at, bounds_check=NP - 1, oob_is_err=False).then_inc(fetched, 16)
                        e.wait_ge(fixed, 1)
                        if hop:
                            e.indirect_dma_start(S, at, own[:], None, bounds_check=NP - 1, oob_is_err=False).then_inc(put, 16)
                        else:
                            e.indirect_dma_start(T, bass.IndirectOffsetOnAxis(ap=first_add_i[:], axis=0), own[:, 0:D], None,
                                                 compute_op=ALU.add).then_inc(put, 16)
                        e.wait_ge(put, 16)

        def norm_of(ctx, NS, G, z, y):
            t = lambda n, w: [ctx.enter_context(sbuf(f"{n}{s}", [P, G, w], F32)) for s in range(NS)]
            row_stats, mean_var, sd, rsd, shift = t("row_stats", 6), t("mean_var", 2), t("sd", 1), t("rsd", 1), t("shift", 1)
            measured, rooted, inverted, folded, recip = (
                stage_of(n, NS) for n in ("measured", "rooted", "inverted", "folded", "recip"))

            def ln_stats(e, i, s, complete):
                hold(e, *done(complete, i, s))
                for k in range(G):
                    ins = e.bn_stats(row_stats[s][:, k, :], z[s][:, k, :])
                ins.then_inc(signal(folded, s), 1)

            def ln_measure(e, i, s):
                hold(e, *done(folded, i, s))
                e.sem_inc(marks, 1)
                for k in range(G):
                    ins = e.bn_aggr(mean_var[s][:, k, :], row_stats[s][:, k, :])
                ins.then_inc(signal(measured, s), 1)

            def ln_root(e, i, s):
                hold(e, *done(measured, i, s))
                e.activation(sd[s][:, :, 0], mean_var[s][:, :, 1], ACT.Sqrt, bias=epsc[:]).then_inc(signal(rooted, s), 1)

            def ln_invert(e, i, s):
                hold(e, *done(rooted, i, s))
                e.reciprocal(rsd[s][:, :, 0], sd[s][:, :, 0]).then_inc(signal(recip, s), 1)

            def ln_shift(e, i, s):
                hold(e, *done(recip, i, s))
                e.scalar_tensor_tensor(shift[s][:, :, 0], mean_var[s][:, :, 0], -1.0, rsd[s][:, :, 0], ALU.mult, ALU.mult)\
                    .then_inc(signal(inverted, s), 1)

            def ln_apply(e, i, s, finished):
                hold(e, *done(inverted, i, s))
                for k in range(G):
                    ins = e.activation(y[s][:, k, :], z[s][:, k, :], ACT.Identity, bias=shift[s][:, k, :], scale=rsd[s][:, k, :])
                ins.then_inc(signal(finished, s), 1)

            return ln_stats, ln_measure, ln_root, ln_invert, ln_shift, ln_apply

        def layer_nodes(layer):
            xin = x if layer == 0 else nodes((X1, X2)[layer - 1])
            xout = nodes((X1, X2, X3)[layer])
            table = layer < 2
            with ExitStack() as ctx:
                G, NS = 2, 4
                R = C // (G * NS)
                tiles = lambda n, w: [ctx.enter_context(sbuf(f"{n}{s}", [P, G, w], F32)) for s in range(NS)]
                xt, st, xb, z, xo = tiles("xt", D), tiles("st", SW), tiles("xb", D), tiles("z", D), tiles("xo", D)
                yt, rT = (tiles("yt", D), tiles("rT", D)) if layer == 0 else (None, None)
                den = tiles("den", H) if layer else None
                xT, tt = (tiles("xT", D), tiles("tt", TW)) if table else (None, None)
                bank = lambda n, w: ctx.enter_context(psum(n, [P, w], F32))
                psR = [bank(f"psR{j}", G * D) for j in range(2)] if layer == 0 else None
                psZ = [bank(f"psZ{j}", G * D) for j in range(2)] if layer == 0 else None
                psX = [bank(f"psX{j}", G * D) for j in range(2)] if table else None
                psV = [bank(f"psV{j}", 512) for j in range(2)] if table else None
                weights = (w1s, w2s, None)[layer]
                NL = 3 if layer == 0 else 2
                names = "combined weighed biased mixed rectified turned copied product summed normed turnedx copiedx tabled evened".split()
                st_ = {n: stage_of(n, NS) for n in names}
                loaded, stored = stage_of("loaded", NS, NL), stage_of("stored", NS, 1)
                stored_t = stage_of("stored_t", NS, 1 + layer % 2)
                ones = semaphore("ones")
                TURN, PRODUCT, ADD = 1, 2, 3 if layer == 0 else 1
                APPLY = ADD + 1
                TURNX, TABLE = APPLY + 1, APPLY + 2
                ln_stats, ln_measure, ln_root, ln_invert, ln_shift, ln_apply = norm_of(ctx, NS, G, z, xo)
                with nc.Block() as block:
                    @block.sync
                    def _(e):

                        def load(i, s):
                            c = bass.ds(i * (G * NS) + s * G, G)
                            hold(e, *done(st_["mixed"], i, s, NS))
                            hold(e, *done(st_["biased"], i, s, NS))
                            e.dma_start(xt[s][:], xin[:, c, :]).then_inc(signal(loaded, s), 16)
                            e.dma_start(st[s][:], nodes(S)[:, c, :]).then_inc(signal(loaded, s), 16)
                            if layer == 0:
                                hold(e, *done(st_["turned"], i, s, NS))
                                e.dma_start(yt[s][:], nodes(T)[:, c, :]).then_inc(signal(loaded, s), 16)

                        def store(i, s):
                            c = bass.ds(i * (G * NS) + s * G, G)
                            hold(e, *done(st_["normed"], i, s))
                            e.dma_start(xout[:, c, :], xo[s][:]).then_inc(signal(stored, s), 16)

                        def store_table(i, s):
                            c = bass.ds(i * (G * NS) + s * G, G)
                            hold(e, *done(st_["evened"], i, s))
                            if layer == 0:
                                e.dma_start(nodes(T1)[:, c, :], tt[s][:]).then_inc(signal(stored_t, s), 16)
                            else:
                                e.dma_start(nodes(T2)[:, c, :], tt[s][:, :, 0:SW]).then_inc(signal(stored_t, s), 16)
                                e.dma_start(nodes(ET)[:, c, :], tt[s][:, :, SW:TW]).then_inc(signal(stored_t, s), 16)

                        pipelined(e, R, NS, [(load, 0), (store, APPLY + 2)] + ([(store_table, TABLE + 2)] if table else []))
                        for sem, value in total(stored, R) + (total(stored_t, R) if table else []):
                            e.wait_ge(sem, value)

                    @block.gpsimd
                    def _(e):
                        bias = (b0s, b1s, b2s)[layer]

                        def add_bias(i, s):
                            hold(e, *done(loaded, i, s))
                            hold(e, *done(st_["summed"], i, s, NS))
                            e.tensor_tensor(xb[s][:], xt[s][:], bias[:].rearrange("p (g d) -> p g d", g=1).to_broadcast([P, G, D]), ALU.add)\
                                .then_inc(signal(st_["biased"], s), 1)

                        pipelined(e, R, NS, [(add_bias, 0)])

                    @block.vector
                    def _(e):
                        if table:
                            for s in range(NS):
                                ins = e.memset(tt[s][:, :, 0:VW].rearrange("p g (h w) -> p g h w", h=H)[:, :, :, HD:HW], 1.0)
                            ins.then_inc(ones, 1)

                        def combine(i, s):
                            hold(e, *done(loaded, i, s))
                            if layer == 0:
                                for k in range(G):
                                    ins = e.scalar_tensor_tensor(yt[s][:, k, :], yt[s][:, k, :], cb[:, bass.ds(i * (G * NS) + (s * G + k), 1)],
                                                                 st[s][:, k, 0:D], ALU.mult, ALU.add)
                            else:
                                v = st[s][:, :, 0:VW].rearrange("p g (h w) -> p g h w", h=H)
                                ins = e.tensor_scalar(den[s][:], v[:, :, :, HD], 1e-10, None, ALU.max)
                            ins.then_inc(signal(st_["combined"], s), 1)

                        def invert_weights(i, s):
                            hold(e, *done(st_["combined"], i, s))
                            e.reciprocal(den[s][:], den[s][:]).then_inc(signal(st_["weighed"], s), 1)

                        def mix(i, s):
                            if layer == 0:
                                hold(e, *done(st_["combined"], i, s))
                                for k in range(G):
                                    ins = e.scalar_tensor_tensor(yt[s][:, k, :], yt[s][:, k, :], dinv[:, bass.ds(i * (G * NS) + (s * G + k), 1)],
                                                                 xt[s][:, k, :], ALU.mult, ALU.add)
                                ins.then_inc(signal(st_["mixed"], s), 1)
                                return
                            hold(e, *done(st_["weighed"], i, s))
                            hold(e, *done(st_["normed"], i, s, NS))
                            v = st[s][:, :, 0:VW].rearrange("p g (h w) -> p g h w", h=H)
                            e.tensor_tensor(z[s][:].rearrange("p g (h d) -> p g h d", h=H), v[:, :, :, 0:HD],
                                            den[s][:].rearrange("p g (h w) -> p g h w", w=1).to_broadcast([P, G, H, HD]), ALU.mult)\
                                .then_inc(signal(st_["mixed"], s), 1)

                        def add(i, s):
                            if layer == 0:
                                hold(e, *done(st_["normed"], i, s, NS))
                                hold(e, *done(st_["product"], i, s))
                                more = psZ[s % 2][:].rearrange("p (g d) -> p g d", g=G)
                            else:
                                hold(e, *done(st_["mixed"], i, s))
                                more = z[s][:]
                            hold(e, *done(st_["biased"], i, s))
                            e.tensor_tensor(z[s][:], more, xb[s][:], ALU.add).then_inc(signal(st_["summed"], s), 1)

                        pipelined(e, R, NS, [(combine, 0), (add, ADD), (lambda i, s: ln_invert(e, i, s), APPLY)]
                                  + ([(invert_weights, 0)] if layer else [])
                                  + [(lambda i, s: ln_stats(e, i, s, st_["summed"]), ADD), (lambda i, s: ln_shift(e, i, s), APPLY),
                                     (mix, 0), (lambda i, s: ln_measure(e, i, s), ADD)])

                    @block.scalar
                    def _(e):
                        def rectify(i, s):
                            hold(e, *done(st_["mixed"], i, s))
                            e.activation(yt[s][:], yt[s][:], ACT.Relu, scale=0.5).then_inc(signal(st_["rectified"], s), 1)

                        def copy_turned(i, s):
                            hold(e, *done(st_["turned"], i, s))
                            hold(e, *done(st_["product"], i, s, NS))
                            e.copy(rT[s][:].rearrange("p g d -> p (g d)"), psR[s % 2][:]).then_inc(signal(st_["copied"], s), 1)

                        def copy_turned_x(i, s):
                            hold(e, *done(st_["turnedx"], i, s))
                            hold(e, *done(st_["tabled"], i, s, NS))
                            e.copy(xT[s][:].rearrange("p g d -> p (g d)"), psX[s % 2][:]).then_inc(signal(st_["copiedx"], s), 1)

                        def tabled_rows(i, s):
                            hold(e, *done(st_["tabled"], i, s))
                            hold(e, *done(stored_t, i, s, NS))
                            for k in range(G):
                                e.copy(tt[s][:, k, 0:VW].rearrange("p (h w) -> p h w", h=H)[:, :, 0:HD],
                                       psV[k][:, 0:D].rearrange("p (h d) -> p h d", h=H))
                                ins = e.copy(tt[s][:, k, VW:TW], psV[k][:, D:DW])
                            ins.then_inc(signal(st_["evened"], s), 1)

                        def apply(i, s):
                            hold(e, *done(stored, i, s, NS))
                            if table:
                                hold(e, *done(st_["turnedx"], i, s, NS))
                            ln_apply(e, i, s, st_["normed"])

                        stages = [(rectify, 0), (copy_turned, TURN)] if layer == 0 else []
                        stages += [(lambda i, s: ln_root(e, i, s), ADD), (apply, APPLY)]
                        if table:
                            stages += [(copy_turned_x, TURNX), (tabled_rows, TABLE)]
                            e.wait_ge(ones, 1)
                        pipelined(e, R, NS, stages)

                    @block.tensor
                    def _(e):
                        def turn(i, s, a, ps, finished):
                            for k in range(G):
                                for m in range(K):
                                    mm = e.transpose(ps[:, (k * K + m) * P:(k * K + m + 1) * P], a[:, k, m * P:(m + 1) * P], ident[:])
                            mm.then_inc(signal(finished, s), 1)

                        def turn_r(i, s):
                            hold(e, *done(st_["rectified"], i, s))
                            hold(e, *done(st_["copied"], i, s, 2))
                            turn(i, s, yt[s], psR[s % 2], st_["turned"])

                        def product(i, s):
                            hold(e, *done(st_["copied"], i, s))
                            hold(e, *done(st_["summed"], i, s, 2))
                            for k in range(G):
                                for m in range(K):
                                    mm = e.matmul(psZ[s % 2][:, k * D:(k + 1) * D], rT[s][:, k, m * P:(m + 1) * P], w0s[:, m, :],
                                                  start=m == 0, stop=m == K - 1)
                            mm.then_inc(signal(st_["product"], s), 1)

                        def turn_x(i, s):
                            hold(e, *done(st_["normed"], i, s))
                            hold(e, *done(st_["copiedx"], i, s, 2))
                            turn(i, s, xo[s], psX[s % 2], st_["turnedx"])

                        def tabulate(i, s):
                            hold(e, *done(st_["copiedx"], i, s))
                            hold(e, *done(st_["evened"], i, s, 1))
                            for k in range(G):
                                for m in range(K):
                                    mm = e.matmul(psV[k][:, 0:DW], xT[s][:, k, m * P:(m + 1) * P], weights[:, m, :],
                                                  start=m == 0, stop=m == K - 1)
                            mm.then_inc(signal(st_["tabled"], s), 1)

                        stages = [(turn_r, TURN), (product, PRODUCT)] if layer == 0 else []
                        if table:
                            stages += [(turn_x, TURNX), (tabulate, TABLE)]
                        if stages:
                            pipelined(e, R, NS, stages)

        def attention_edges(layer):
            with ExitStack() as ctx:
                G, NS, LAG = 2, 4, 3
                R = C // (G * NS)
                tiles = lambda n, w, dt=F32, p=P: [ctx.enter_context(sbuf(f"{n}{s}", [p, G, w], dt)) for s in range(NS)]
                table, dtable = (T1, T1) if layer == 1 else (T2, ET)
                W, WD = table.shape[1], dtable.shape[1]
                rows, rowsd, sums = tiles("rows", W), tiles("rowsd", WD), tiles("sums", SW)
                gi, gd, si = tiles("gi", 1, I32), tiles("gd", 1, I32), tiles("si", 1, I32)
                KA = 4 if layer == 1 else attr64T.shape[0]
                attr = tiles("attr", P, F32, KA)
                enc = tiles("enc", D) if layer == 1 else None
                lg, dot, mp, diff, ex = tiles("lg", H), tiles("dot", H), tiles("mp", H), tiles("diff", 2 * H), tiles("ex", 2 * H)
                EW = D if layer == 1 else H
                psE = [ctx.enter_context(psum(f"psE{j}", [P, 512], F32)) for j in range(2)]
                placed = stage_of("placed", NS, 1)
                indexed, gathered, scattered, attred = (stage_of("indexed", NS, 2), stage_of("gathered", NS, 2 * G),
                                                        stage_of("scattered", NS, G), stage_of("attred", NS, 1))
                encoded, rectified, scored, exped, summed = (stage_of(n, NS) for n in ("encoded", "rectified", "scored", "exped", "summed"))
                steps, bsteps, started = [semaphore(n) for n in ("steps", "bsteps", "started")]
                heads = lambda a: a.rearrange("p (h w) -> p h w", h=H)
                with nc.Block() as block:
                    @block.sync
                    def _(e):
                        e.wait_ge(started, 1)
                        edge_attr = attr3T if layer == 1 else attr64T

                        def stage(i, s):
                            c = bass.ds(i * (G * NS) + s * G, G)
                            hold(e, *done(encoded, i, s, NS))
                            e.dma_start(attr[s][0:edge_attr.shape[0]], edge_attr[:, c, :]).then_inc(signal(attred, s), 16)
                            hold(e, *done(gathered, i, s, NS))
                            e.dma_start(gi[s][:, :, 0], src_i[:, c]).then_inc(signal(indexed, s), 16)
                            e.dma_start(gd[s][:, :, 0], dst_i[:, c]).then_inc(signal(indexed, s), 16)

                        def stage_scatter(i, s):
                            c = bass.ds(i * (G * NS) + s * G, G)
                            hold(e, *done(scattered, i, s, NS))
                            e.dma_start(si[s][:, :, 0], scat_i[:, c]).then_inc(signal(placed, s), 16)

                        pipelined(e, R, NS, [(stage, 0), (stage_scatter, 2)])

                    @block.gpsimd
                    def _(e):
                        def gather(i, s):
                            hold(e, *done(indexed, i, s))
                            hold(e, *done(summed, i, s, NS))
                            for k in range(G):
                                e.indirect_dma_start(rowsd[s][:, k, :], None, dtable, bass.IndirectOffsetOnAxis(ap=gd[s][:, k, :], axis=0))\
                                    .then_inc(signal(gathered, s), 16)
                                e.indirect_dma_start(rows[s][:, k, :], None, table, bass.IndirectOffsetOnAxis(ap=gi[s][:, k, :], axis=0))\
                                    .then_inc(signal(gathered, s), 16)

                        def scatter(i, s):
                            hold(e, *done(summed, i, s))
                            hold(e, *done(placed, i, s))
                            for k in range(G):
                                e.indirect_dma_start(S, bass.IndirectOffsetOnAxis(ap=si[s][:, k, :], axis=0), sums[s][:, k, :], None,
                                                     bounds_check=NP - 1, oob_is_err=False).then_inc(signal(scattered, s), 16)

                        pipelined(e, R, NS, [(gather, 0), (scatter, LAG)])
                        for sem, value in total(scattered, R):
                            e.wait_ge(sem, value)

                    @block.tensor
                    def _(e):
                        weights = encs if layer == 1 else fes

                        def encode(i, s):
                            hold(e, *done(attred, i, s))
                            if layer == 1:
                                hold(e, *done(rectified, i, s, 2))
                            else:
                                hold(e, *done(scored, i, s, 2))
                            for k in range(G):
                                mm = e.matmul(psE[s % 2][:, k * EW:(k + 1) * EW], attr[s][:, k, :], weights[:], start=True, stop=True)
                            mm.then_inc(signal(encoded, s), 1)

                        pipelined(e, R, NS, [(encode, 0)])

                    @block.scalar
                    def _(e):
                        def rectify(i, s):
                            hold(e, *done(encoded, i, s))
                            hold(e, *done(scored, i, s, NS))
                            e.activation(enc[s][:].rearrange("p g d -> p (g d)"), psE[s % 2][:], ACT.Relu).then_inc(signal(rectified, s), 1)

                        def exponentials(i, s):
                            hold(e, *done(scored, i, s))
                            hold(e, *done(summed, i, s, NS))
                            e.activation(ex[s][:], diff[s][:], ACT.Exp).then_inc(signal(exped, s), 1)

                        pipelined(e, R, NS, ([(rectify, 0)] if layer == 1 else []) + [(exponentials, 0)])

                    @block.vector
                    def _(e):
                        for s in range(NS):
                            ins = e.memset(sums[s][:], 0.0)
                            if layer == 1:
                                ins = e.memset(attr[s][:], 1.0)
                        ins.then_inc(started, 1)
                        e.wait_ge(started, 1)
                        SC = 8 if layer == 1 else 6

                        def score(i, s):
                            n = [0]

                            def link(ins):
                                n[0] += 1
                                ins.then_inc(steps, 1)
                                e.wait_ge(steps, i * (NS * SC) + (s * SC + n[0]))

                            hold(e, *done(gathered, i, s))
                            hold(e, *done(scattered, i, s, NS))
                            hold(e, *done(summed, i, s, NS))
                            hold(e, *done(exped, i, s, NS))
                            if layer == 1:
                                hd = rowsd[s][:, :, 0:VW].rearrange("p g (h w) -> p g h w", h=H)[:, :, :, 0:HD]
                                e4 = enc[s][:].rearrange("p g (h d) -> p g h d", h=H)
                                hold(e, *done(rectified, i, s))
                                link(e.tensor_tensor(e4, e4, hd, ALU.mult))
                                link(e.tensor_reduce(dot[s][:], e4, AX, ALU.add))
                                link(e.tensor_tensor(dot[s][:], dot[s][:], rows[s][:, :, VW:SW], ALU.add))
                                link(e.tensor_tensor(dot[s][:], dot[s][:], rowsd[s][:, :, SW:TW], ALU.add))
                            else:
                                hold(e, *done(encoded, i, s))
                                link(e.tensor_tensor(dot[s][:], rows[s][:, :, VW:SW], rowsd[s][:], ALU.add))
                                link(e.tensor_tensor(dot[s][:], dot[s][:], psE[s % 2][:, 0:G * H].rearrange("p (g h) -> p g h", g=G), ALU.add))
                            link(e.scalar_tensor_tensor(lg[s][:], dot[s][:], 0.2, dot[s][:], ALU.mult, ALU.max))
                            for k in range(G):
                                pc = pen[:, bass.ds(i * (G * NS) + (s * G + k), 1)]
                                last = sums[s][:, k - 1, VW:SW] if k else sums[(s - 1) % NS][:, G - 1, VW:SW]
                                e.tensor_scalar(mp[s][:, k, :], last, pc, None, ALU.add)
                                link(e.scalar_tensor_tensor(sums[s][:, k, VW:SW], last, pc, lg[s][:, k, :], ALU.add, ALU.max))
                            link(e.tensor_tensor(diff[s][:, :, 0:H], mp[s][:], sums[s][:, :, VW:SW], ALU.subtract))
                            e.tensor_tensor(diff[s][:, :, H:2 * H], lg[s][:], sums[s][:, :, VW:SW], ALU.subtract).then_inc(signal(scored, s), 1)
                            assert n[0] == SC

                        def add(i, s):
                            hold(e, *done(exped, i, s))
                            wide = lambda a: a.rearrange("p g (h w) -> p g h w", w=1).to_broadcast([P, G, H, HW])
                            v = rows[s][:, :, 0:VW].rearrange("p g (h w) -> p g h w", h=H)
                            e.tensor_tensor(v, v, wide(ex[s][:, :, H:2 * H]), ALU.mult)
                            B = 2 * G - 1
                            n = 0
                            for k in range(G):
                                last = sums[s][:, k - 1, 0:VW] if k else sums[(s - 1) % NS][:, G - 1, 0:VW]
                                r = ex[s][:, k, 0:H].rearrange("p (h w) -> p h w", w=1).to_broadcast([P, H, HW])
                                n += 1
                                e.tensor_tensor(heads(sums[s][:, k, 0:VW]), heads(last), r, ALU.mult).then_inc(bsteps, 1)
                                e.wait_ge(bsteps, i * (NS * B) + (s * B + n))
                                ins = e.tensor_tensor(sums[s][:, k, 0:VW], sums[s][:, k, 0:VW], rows[s][:, k, 0:VW], ALU.add)
                                if k < G - 1:
                                    n += 1
                                    ins.then_inc(bsteps, 1)
                                    e.wait_ge(bsteps, i * (NS * B) + (s * B + n))
                            ins.then_inc(signal(summed, s), 1)
                            hold(e, *done(summed, i, s))

                        pipelined(e, R, NS, [(score, 0), (add, 1)])
                with nc.Block() as block:
                    end = sums[NS - 1][:, G - 1, :]
                    t = lambda n, sh: ctx.enter_context(sbuf(n, sh, F32))
                    own, mall, eT, mc, mn, r, dm = (t("own", [P, SW]), t("mall", [P, H, P]), t("eT", [P, H, P]), t("mc", [P, H]),
                                                    t("mn", [P, H]), t("r", [P, H]), t("dm", [P, H]))
                    psM = ctx.enter_context(psum("psM", [P, H, P], F32))
                    psC = ctx.enter_context(psum("psC", [P, 512], F32))
                    fetched, cleared, turned, fx, exd, put = [semaphore(n) for n in (
                        "fetched", "cleared", "fturned", "fx", "exd", "put")]

                    @block.gpsimd
                    def _(e):
                        at = bass.IndirectOffsetOnAxis(ap=first_i[:], axis=0)
                        e.wait_ge(cleared, 1)
                        e.indirect_dma_start(own[:], None, S, at, bounds_check=NP - 1, oob_is_err=False).then_inc(fetched, 16)
                        e.wait_ge(fx, 9)
                        e.indirect_dma_start(S, at, own[:], None, bounds_check=NP - 1, oob_is_err=False).then_inc(put, 16)
                        e.wait_ge(put, 16)

                    @block.tensor
                    def _(e):
                        for h in range(H):
                            mm = e.transpose(psM[:, h, :], end[:, VW + h:VW + h + 1].to_broadcast([P, P]), ident[:])
                        mm.then_inc(turned, 1)
                        e.wait_ge(exd, 1)
                        for h in range(H):
                            mm = e.transpose(psM[:, h, :], mall[:, h, :], ident[:])
                        mm.then_inc(turned, 1)
                        e.wait_ge(fx, 6)
                        for h in range(H):
                            mm = e.matmul(psC[:, h * HW:(h + 1) * HW], eT[:, h, :], end[:, h * HW:(h + 1) * HW], start=True, stop=True)
                        mm.then_inc(turned, 1)

                    @block.scalar
                    def _(e):
                        e.wait_ge(fx, 5)
                        e.activation(mall[:], mall[:], ACT.Exp).then_inc(exd, 1)
                        e.activation(r[:], dm[:], ACT.Exp).then_inc(exd, 1)

                    @block.vector
                    def _(e):
                        n = [0]

                        def link(ins):
                            n[0] += 1
                            ins.then_inc(fx, 1)
                            e.wait_ge(fx, n[0])

                        e.memset(own[:], 0.0).then_inc(cleared, 1)
                        e.wait_ge(turned, 1)
                        link(e.tensor_tensor(mall[:], psM[:], penT[:].rearrange("p (h q) -> p h q", h=1).to_broadcast([P, H, P]), ALU.add))
                        link(e.tensor_reduce(mc[:], mall[:], AX, ALU.max))
                        e.wait_ge(fetched, 16)
                        link(e.tensor_tensor(mn[:], mc[:], own[:, VW:SW], ALU.max))
                        link(e.tensor_tensor(dm[:], own[:, VW:SW], mn[:], ALU.subtract))
                        link(e.tensor_tensor(mall[:], mall[:], mn[:].rearrange("p (h q) -> p h q", q=1).to_broadcast([P, H, P]), ALU.subtract))
                        e.wait_ge(turned, 2)
                        link(e.tensor_copy(eT[:], psM[:]))
                        e.wait_ge(exd, 2)
                        link(e.tensor_tensor(heads(own[:, 0:VW]), heads(own[:, 0:VW]), r[:].rearrange("p (h w) -> p h w", w=1).to_broadcast([P, H, HW]), ALU.mult))
                        e.wait_ge(turned, 3)
                        link(e.tensor_tensor(own[:, 0:VW], own[:, 0:VW], psC[:, 0:VW], ALU.add))
                        link(e.tensor_copy(own[:, VW:SW], mn[:]))

        def filter_edges():
            with ExitStack() as ctx:
                G, NS, LAG = 2, 4, 3
                R = C // (G * NS)
                tiles = lambda n, w, dt=F32, p=P: [ctx.enter_context(sbuf(f"{n}{s}", [p, G, w], dt)) for s in range(NS)]
                NG = rbfT.shape[0]
                rbf = tiles("rbf", P, F32, NG)
                rows, comb, eq, low = tiles("rows", D), tiles("comb", D), tiles("eq", P), tiles("low", P)
                hid = [ctx.enter_context(sbuf(f"hid{s}", [P, K, G * P], F32)) for s in range(NS)]
                fl = tiles("fl", D)
                sc, cnt, gi, ai = tiles("sc", 1), tiles("cnt", 1), tiles("gi", 1, I32), tiles("ai", 1, I32)
                bank = lambda n: ctx.enter_context(psum(n, [P, 512], F32))
                psH, psI, psF, psM = [[bank(f"{n}{j}") for j in range(2)] for n in ("psH", "psI", "psF", "psM")]
                indexed, gathered, added, attred = (stage_of("indexed", NS, 1), stage_of("gathered", NS, G),
                                                    stage_of("added", NS, G), stage_of("attred", NS, 1))
                stages = [stage_of(n, NS) for n in (
                    "columned", "hidden", "sourced", "active", "filtered", "compared", "message", "joined", "copied")]
                columned, hidden, sourced, active, filtered, compared, message, joined, copied = stages
                steps, msteps = [semaphore(n) for n in ("steps", "msteps")]
                with nc.Block() as block:
                    @block.sync
                    def _(e):

                        def stage(i, s):
                            c = bass.ds(i * (G * NS) + s * G, G)
                            hold(e, *done(hidden, i, s, NS))
                            e.dma_start(rbf[s][:], rbfT[:, c, :]).then_inc(signal(attred, s), 16)
                            hold(e, *done(gathered, i, s, NS))
                            e.dma_start(gi[s][:, :, 0], dst_i[:, c]).then_inc(signal(indexed, s), 16)

                        pipelined(e, R, NS, [(stage, 0)])

                    @block.gpsimd
                    def _(e):
                        def gather(i, s):
                            hold(e, *done(indexed, i, s))
                            hold(e, *done(message, i, s, NS))
                            for k in range(G):
                                e.indirect_dma_start(rows[s][:, k, :], None, X3, bass.IndirectOffsetOnAxis(ap=gi[s][:, k, :], axis=0))\
                                    .then_inc(signal(gathered, s), 16)

                        def add(i, s):
                            hold(e, *done(copied, i, s))
                            hold(e, *done(added, i, s, 1))
                            for k in range(G):
                                e.indirect_dma_start(A[k], bass.IndirectOffsetOnAxis(ap=ai[s][:, k, :], axis=0), comb[s][:, k, :], None,
                                                     compute_op=ALU.add).then_inc(signal(added, s), 16)

                        pipelined(e, R, NS, [(gather, 0), (add, LAG)])
                        for sem, value in total(added, R):
                            e.wait_ge(sem, value)

                    @block.tensor
                    def _(e):
                        def hide(i, s):
                            hold(e, *done(attred, i, s))
                            hold(e, *done(active, i, s, 2))
                            for m in range(K):
                                mm = e.matmul(psH[s % 2][:, m * G * P:(m + 1) * G * P], wf1s[:, m * P:(m + 1) * P],
                                              rbf[s][:].rearrange("p g q -> p (g q)"), start=True, stop=True)
                            mm.then_inc(signal(hidden, s), 1)
                            hold(e, *done(compared, i, s, 2))
                            hold(e, *done(columned, i, s))
                            for k in range(G):
                                mm = e.transpose(psI[s % 2][:, k * P:(k + 1) * P], sc[s][:, k, :].to_broadcast([P, P]), ident[:])
                            mm.then_inc(signal(sourced, s), 1)

                        def filt(i, s):
                            hold(e, *done(active, i, s))
                            hold(e, *done(message, i, s, 2))
                            for k in range(G):
                                for m in range(K):
                                    mm = e.matmul(psF[s % 2][:, k * D:(k + 1) * D], hid[s][:, m, k * P:(k + 1) * P], wf2s[:, m, :],
                                                  start=m == 0, stop=m == K - 1)
                            mm.then_inc(signal(filtered, s), 1)

                        def join(i, s):
                            hold(e, *done(message, i, s))
                            hold(e, *done(compared, i, s))
                            hold(e, *done(copied, i, s, 2))
                            for k in range(G):
                                mm = e.matmul(psM[s % 2][:, k * D:(k + 1) * D], eq[s][:, k, :], fl[s][:, k, :], start=True, stop=True)
                            mm.then_inc(signal(joined, s), 1)

                        pipelined(e, R, NS, [(hide, 0), (filt, 1), (join, 2)])

                    @block.scalar
                    def _(e):
                        def column(i, s):
                            hold(e, *done(sourced, i, s, NS))
                            e.copy(sc[s][:, :, 0], src_f[:, bass.ds(i * (G * NS) + s * G, G)]).then_inc(signal(columned, s), 1)

                        def activate(i, s):
                            hold(e, *done(hidden, i, s))
                            hold(e, *done(message, i, s, NS))
                            for m in range(K):
                                ins = e.activation(hid[s][:, m, :], psH[s % 2][:, m * G * P:(m + 1) * G * P], ACT.Silu, bias=bf1s[:, m:m + 1])
                            ins.then_inc(signal(active, s), 1)

                        def copy(i, s):
                            hold(e, *done(joined, i, s))
                            hold(e, *done(added, i, s, NS))
                            e.copy(comb[s][:].rearrange("p g d -> p (g d)"), psM[s % 2][:]).then_inc(signal(copied, s), 1)

                        pipelined(e, R, NS, [(column, 0), (activate, 0), (copy, 2)])

                    @block.vector
                    def _(e):
                        def compare(i, s):
                            hold(e, *done(sourced, i, s))
                            hold(e, *done(joined, i, s, NS))
                            hold(e, *done(added, i, s, NS))
                            for k in range(G):
                                c = bass.ds(i * (G * NS) + (s * G + k), 1)
                                turned_k = psI[s % 2][:, k * P:(k + 1) * P]
                                e.tensor_scalar(eq[s][:, k, :], turned_k, src_f[:, c], None, ALU.is_equal)
                                e.scalar_tensor_tensor(low[s][:, k, :], turned_k, src_f[:, c], earlier[:], ALU.is_equal, ALU.mult,
                                                       accum_out=cnt[s][:, k, :]).then_inc(steps, 1)
                            base = G + 2
                            e.wait_ge(steps, i * (NS * base) + (s * base + G))
                            e.tensor_scalar(cnt[s][:], cnt[s][:], 0.0, None, ALU.is_equal).then_inc(steps, 1)
                            e.wait_ge(steps, i * (NS * base) + (s * base + G + 1))
                            c = bass.ds(i * (G * NS) + s * G, G)
                            e.tensor_tensor(cnt[s][:, :, 0], cnt[s][:, :, 0], srcmt[:, c], ALU.mult).then_inc(steps, 1)
                            e.wait_ge(steps, i * (NS * base) + (s * base + G + 2))
                            e.tensor_scalar(ai[s][:], cnt[s][:], trash[:], None, ALU.add).then_inc(signal(compared, s), 1)

                        def multiply(i, s):
                            hold(e, *done(filtered, i, s))
                            hold(e, *done(joined, i, s, NS))
                            hold(e, *done(gathered, i, s))
                            e.tensor_tensor(fl[s][:], psF[s % 2][:].rearrange("p (g d) -> p g d", g=G),
                                            bf2s[:].rearrange("p (g d) -> p g d", g=1).to_broadcast([P, G, D]), ALU.add).then_inc(msteps, 1)
                            e.wait_ge(msteps, i * NS + (s + 1))
                            e.tensor_tensor(fl[s][:], fl[s][:], rows[s][:], ALU.mult).then_inc(signal(message, s), 1)

                        pipelined(e, R, NS, [(compare, 0), (multiply, 1)])

        def update_nodes():
            with ExitStack() as ctx:
                G, NS = 2, 4
                R = C // (G * NS)
                t = lambda n: [ctx.enter_context(sbuf(f"{n}{s}", [P, K, G * P], F32)) for s in range(NS)]
                agg, more = [[ctx.enter_context(sbuf(f"{n}{s}", [P, G, D], F32)) for s in range(NS)] for n in ("agg", "more")]
                aT, hid, ht = t("aT"), t("hid"), t("ht")
                psA, psH, psO = [[ctx.enter_context(psum(f"{n}{j}", [P, K, G * P], F32)) for j in range(2)] for n in ("psA", "psH", "psO")]
                loaded, stored = stage_of("loaded", NS, 2), stage_of("stored", NS, 1)
                stages = [stage_of(n, NS) for n in ("summed", "turned", "copied", "hidden", "active", "updated", "biased", "measured")]
                summed, turned, copied, hidden, active, updated, biased, measured = stages
                with nc.Block() as block:
                    @block.sync
                    def _(e):

                        def load(i, s):
                            c = bass.ds(i * (G * NS) + s * G, G)
                            hold(e, *done(turned, i, s, NS))
                            e.dma_start(agg[s][:], nodes(A[0])[:, c, :]).then_inc(signal(loaded, s), 16)
                            e.dma_start(more[s][:], nodes(A[1])[:, c, :]).then_inc(signal(loaded, s), 16)

                        def store(i, s):
                            hold(e, *done(biased, i, s))
                            e.dma_start(HT[:, :, bass.ds(i * (G * NS * P) + s * (G * P), G * P)], ht[s][:]).then_inc(signal(stored, s), 16)

                        pipelined(e, R, NS, [(load, 0), (store, 4)])
                        for sem, value in total(stored, R):
                            e.wait_ge(sem, value)

                    @block.tensor
                    def _(e):
                        def turn(i, s):
                            hold(e, *done(summed, i, s))
                            hold(e, *done(copied, i, s, 2))
                            for m in range(K):
                                for k in range(G):
                                    mm = e.transpose(psA[s % 2][:, m, k * P:(k + 1) * P], agg[s][:, k, m * P:(m + 1) * P], ident[:])
                            mm.then_inc(signal(turned, s), 1)

                        def product(a, w, ps, finished, s):
                            for n in range(K):
                                for m in range(K):
                                    mm = e.matmul(ps[:, n, :], w[:, m, n * P:(n + 1) * P], a[s][:, m, :], start=m == 0, stop=m == K - 1)
                            mm.then_inc(signal(finished, s), 1)

                        def hide(i, s):
                            hold(e, *done(copied, i, s))
                            hold(e, *done(active, i, s, 2))
                            product(aT, wu1s, psH[s % 2], hidden, s)

                        def update(i, s):
                            hold(e, *done(active, i, s))
                            hold(e, *done(biased, i, s, 2))
                            product(hid, wu2s, psO[s % 2], updated, s)

                        pipelined(e, R, NS, [(turn, 0), (hide, 1), (update, 2)])

                    @block.scalar
                    def _(e):
                        def activate(i, s):
                            hold(e, *done(hidden, i, s))
                            hold(e, *done(updated, i, s, NS))
                            for m in range(K):
                                ins = e.activation(hid[s][:, m, :], psH[s % 2][:, m, :], ACT.Silu, bias=bu1s[:, m:m + 1])
                            ins.then_inc(signal(active, s), 1)

                        def bias(i, s):
                            hold(e, *done(updated, i, s))
                            hold(e, *done(stored, i, s, NS))
                            hold(e, *done(measured, i, s, NS))
                            for m in range(K):
                                ins = e.activation(ht[s][:, m, :], psO[s % 2][:, m, :], ACT.Identity, bias=bu2s[:, m:m + 1])
                            ins.then_inc(signal(biased, s), 1)

                        pipelined(e, R, NS, [(activate, 1), (bias, 2)])

                    @block.vector
                    def _(e):
                        def add(i, s):
                            hold(e, *done(loaded, i, s))
                            e.tensor_tensor(agg[s][:], agg[s][:], more[s][:], ALU.add).then_inc(signal(summed, s), 1)

                        def copy(i, s):
                            hold(e, *done(turned, i, s))
                            hold(e, *done(hidden, i, s, NS))
                            e.tensor_copy(aT[s][:], psA[s % 2][:]).then_inc(signal(copied, s), 1)

                        full = VC // (G * NS)
                        there = [P]

                        def measure(i, s):
                            if isinstance(i, int):
                                there[0] = P if i < full else P - 1
                            hold(e, *done(biased, i, s))
                            for m in range(K):
                                h4 = ht[s][:, m, :].rearrange("p (g q) -> p g q", g=G)[:, :, 0:there[0]]
                                ins = e.bn_stats(stats[:, m, bass.ds(i * NS + s, 1), :].rearrange("p a b -> p (a b)"), h4)
                            ins.then_inc(signal(measured, s), 1)

                        pipelined(e, R, NS, [(add, 0), (copy, 0), (measure, 3)], cut=full)

        def finish_nodes():
            with ExitStack() as ctx:
                G, NS = 2, 4
                R = C // (G * NS)
                mv, sd, scale, shift = [ctx.enter_context(sbuf(n, [P, K, w], F32)) for n, w in (("bmv", 2), ("bsd", 1), ("scale", 1), ("shift", 1))]
                ht = [ctx.enter_context(sbuf(f"ht{s}", [P, K, G * P], F32)) for s in range(NS)]
                xt, z, xo = [[ctx.enter_context(sbuf(f"{n}{s}", [P, G, D], F32)) for s in range(NS)] for n in ("xt", "z", "xo")]
                ps = [ctx.enter_context(psum(f"psN{j}", [P, G, D], F32)) for j in range(NS)]
                loaded, stored = stage_of("loaded", NS, 2), stage_of("stored", NS, 1)
                stages = [stage_of(n, NS) for n in ("normed", "turned", "summed", "finished")]
                normed, turned, summed, finished = stages
                ln_stats, ln_measure, ln_root, ln_invert, ln_shift, ln_apply = norm_of(ctx, NS, G, z, xo)
                agged, rooted, scaled = [semaphore(n) for n in ("agged", "brooted", "scaled")]
                with nc.Block() as block:
                    @block.sync
                    def _(e):

                        def load(i, s):
                            hold(e, *done(turned, i, s, NS))
                            e.dma_start(ht[s][:], HT[:, :, bass.ds(i * (G * NS * P) + s * (G * P), G * P)]).then_inc(signal(loaded, s), 16)
                            hold(e, *done(summed, i, s, NS))
                            e.dma_start(xt[s][:], nodes(X3)[:, bass.ds(i * (G * NS) + s * G, G), :]).then_inc(signal(loaded, s), 16)

                        def store(i, s):
                            hold(e, *done(finished, i, s))
                            e.dma_start(out[:, bass.ds(i * (G * NS) + s * G, G), :], xo[s][:]).then_inc(signal(stored, s), 16)

                        pipelined(e, R, NS, [(load, 0), (store, 5)])
                        for sem, value in total(stored, R):
                            e.wait_ge(sem, value)

                    @block.tensor
                    def _(e):
                        def turn(i, s):
                            hold(e, *done(normed, i, s))
                            hold(e, *done(summed, i, s, NS))
                            for k in range(G):
                                for m in range(K):
                                    mm = e.transpose(ps[s][:, k, m * P:(m + 1) * P], ht[s][:, m, k * P:(k + 1) * P], ident[:])
                            mm.then_inc(signal(turned, s), 1)

                        pipelined(e, R, NS, [(turn, 1)])

                    @block.scalar
                    def _(e):
                        e.wait_ge(agged, 1)
                        e.activation(sd[:, :, 0], mv[:, :, 1], ACT.Sqrt, bias=epsc[:]).then_inc(rooted, 1)
                        e.wait_ge(scaled, 4)

                        def batch_norm(i, s):
                            hold(e, *done(loaded, i, s))
                            for m in range(K):
                                ins = e.activation(ht[s][:, m, :], ht[s][:, m, :], ACT.Identity, bias=shift[:, m, :], scale=scale[:, m, :])
                            ins.then_inc(signal(normed, s), 1)

                        def apply(i, s):
                            hold(e, *done(stored, i, s, NS))
                            ln_apply(e, i, s, finished)

                        pipelined(e, R, NS, [(batch_norm, 0), (lambda i, s: ln_root(e, i, s), 2), (apply, 3)])

                    @block.vector
                    def _(e):
                        for m in range(K):
                            ins = e.bn_aggr(mv[:, m, :], stats[:, m, :, :].rearrange("p a b -> p (a b)"))
                        ins.then_inc(agged, 1)
                        e.wait_ge(rooted, 1)
                        e.reciprocal(sd[:], sd[:]).then_inc(scaled, 1)
                        e.wait_ge(scaled, 1)
                        e.tensor_tensor(scale[:, :, 0], sd[:, :, 0], gms[:], ALU.mult).then_inc(scaled, 1)
                        e.wait_ge(scaled, 2)
                        e.tensor_tensor(shift[:, :, 0], scale[:, :, 0], mv[:, :, 0], ALU.mult).then_inc(scaled, 1)
                        e.wait_ge(scaled, 3)
                        e.tensor_tensor(shift[:, :, 0], bts[:], shift[:, :, 0], ALU.subtract).then_inc(scaled, 1)

                        def add(i, s):
                            hold(e, *done(turned, i, s))
                            hold(e, *done(finished, i, s, NS))
                            e.scalar_tensor_tensor(z[s][:], xt[s][:], 2.0, ps[s][:], ALU.mult, ALU.add).then_inc(signal(summed, s), 1)

                        pipelined(e, R, NS, [(add, 2), (lambda i, s: ln_invert(e, i, s), 3), (lambda i, s: ln_stats(e, i, s, summed), 2),
                                             (lambda i, s: ln_shift(e, i, s), 3), (lambda i, s: ln_measure(e, i, s), 2)])

        for phase in (setup, lambda: hop_edges(0, A[0]), lambda: hop_edges(1, A[1]),
                      lambda: layer_nodes(0), lambda: attention_edges(1), lambda: layer_nodes(1),
                      lambda: attention_edges(2), lambda: layer_nodes(2), filter_edges, update_nodes, finish_nodes):
            with nc.cleanup_on_exit():
                phase()


def kernel(**inputs):
    import numpy as np
    import concourse.bacc as bacc
    from concourse.bass_utils import run_bass_kernel_spmd

    a = {k: np.asarray(v) for k, v in inputs.items()}
    N, E = a["x"].shape[0], a["src"].shape[0]
    C = -(-max(N, E) // (P * 8)) * 8
    NP = P * C

    def pad(v, fill=0):
        return np.concatenate([v, np.full((NP - v.shape[0], *v.shape[1:]), fill, v.dtype)])

    def by_column(v):
        return np.ascontiguousarray(pad(v).reshape(P, C, -1).transpose(2, 1, 0))

    def spread(v):
        m = np.zeros((D, H), v.dtype)
        for h in range(H):
            m[h * HD:(h + 1) * HD, h] = v[h]
        return m

    halves = lambda v: np.ascontiguousarray(v.reshape(K, P).T)
    row = lambda v: v.reshape(1, D)
    dst = np.concatenate([pad(a["dst"], N), np.full(1, N + 1, a["dst"].dtype)])
    T = lambda v: np.ascontiguousarray(v.T)
    arrays = dict(
        x=pad(a["x"]).reshape(P, C, D), src=pad(a["src"], N).reshape(P, C), srcT=T(pad(a["src"], N).reshape(P, C)),
        dst=np.ascontiguousarray(dst[:NP].reshape(P, C)),
        dst_next=np.ascontiguousarray(dst[1:].reshape(P, C)), ew=pad(a["edge_weight"]).reshape(P, C),
        rbfT=by_column(a["edge_attr_20"]), attr3T=by_column(a["edge_attr_3"]), attr64T=by_column(a["edge_attr_64"]),
        w0T=T(a["L0_gnn_W"]), b0=row(a["L0_gnn_b"]),
        w1T=T(a["L1_gnn_W"]), w1=a["L1_gnn_W"],
        a1=np.concatenate([spread(a["L1_gnn_a_src"]), spread(a["L1_gnn_a_dst"])], axis=1),
        encW=np.concatenate([T(a["L1_gnn_edge_W"]), row(a["L1_gnn_edge_b"])]), bias1=row(a["L1_gnn_bias"]),
        wfc=a["L2_gnn_W_fc"], wfcT=T(a["L2_gnn_W_fc"]),
        ah=np.concatenate([spread(a["L2_gnn_attn_h"]), spread(a["L2_gnn_attn_t"])], axis=1),
        ae=spread(a["L2_gnn_attn_e"]), weT=T(a["L2_gnn_W_e"]), bias2=row(a["L2_gnn_bias"]),
        wf1=a["L3_gnn_Wf1"], bf1=halves(a["L3_gnn_bf1"]), wf2=a["L3_gnn_Wf2"], bf2=row(a["L3_gnn_bf2"]),
        wu1=a["L3_gnn_Wu1"], bu1=halves(a["L3_gnn_bu1"]), wu2=a["L3_gnn_Wu2"], bu2=halves(a["L3_gnn_bu2"]),
        gamma=halves(a["L3_gnn_gamma"]), beta=halves(a["L3_gnn_beta"]))
    nc = bacc.Bacc("TRN2", target_bir_lowering=False, num_devices=1)
    args = {n: nc.dram_tensor(f"in_{n}", v.shape, mybir.dt.from_np(v.dtype), kind="ExternalInput").ap() for n, v in arrays.items()}
    out = nc.dram_tensor("out", (P, C, D), F32, kind="ExternalOutput").ap()
    build(nc, N, out=out, **args)
    r = run_bass_kernel_spmd(nc, [{f"in_{n}": v for n, v in arrays.items()}], core_ids=[0])
    return r.results[0]["out"].reshape(NP, D)[:N]
```
